# Optimizing a Trainium2 kernel written in Bass

```python
import numpy as np
import jax
import jax.numpy as jnp

def _softmax(x, axis=-1):
    return jax.nn.softmax(x, axis=axis)

def _gelu(x):
    return jax.nn.gelu(x, approximate=True)

def _silu(x):
    return jax.nn.silu(x)

def _sigmoid(x):
    return jax.nn.sigmoid(x)

def _layernorm(x, axis=-1, eps=1e-05):
    m = jnp.mean(x, axis=axis, keepdims=True)
    v = jnp.var(x, axis=axis, keepdims=True)
    return (x - m) / jnp.sqrt(v + eps)

def _scatter_add(tgt, idx, src, axis=0):
    return tgt.at[idx].add(src)

def _segment_sum(src, seg, n):
    return jax.ops.segment_sum(src, seg, n)
kernel_name = 'mk_seq_postln_d1_jaxref_r8_a7e5bb'

def setup_inputs(seed: int=0):
    np.random.seed(seed)
    _w = jnp.asarray

    def _L0_attn_setup():
        import jax, jax.numpy as jnp
        import numpy as np
        B, S, D = (4, 512, 128)
        CHUNK = 64
        MAX_LR = 0.2
        MIN_DECAY = 0.5
        MAX_NORM = 30.0
        NORM_EPS = 1e-05

        def _forward(x, M_init, eta_w, eta_b, alpha_w, alpha_b, gate_w, gate_b, vg_w1, vg_w2):
            b, s, d = x.shape
            n_ch = s // CHUNK

            def value_gen(y):
                h = jax.nn.silu(y @ vg_w1.T) @ vg_w2.T
                return h + y
            x_chunks = x.reshape(b, n_ch, CHUNK, d).transpose(1, 0, 2, 3)
            M0 = jnp.broadcast_to(M_init, (b, d, d))

            def step(M, chunk):
                eta_tok = jax.nn.sigmoid(chunk @ eta_w + eta_b[0]) * MAX_LR
                alpha_tok = MIN_DECAY + jax.nn.sigmoid(chunk @ alpha_w + alpha_b[0]) * (1.0 - MIN_DECAY)
                eta = eta_tok.mean(axis=1)[:, None, None]
                alpha = alpha_tok.mean(axis=1)[:, None, None]
                outputs = jnp.einsum('bci,boi->bco', chunk, M)
                nrm = jnp.sqrt(jnp.sum(chunk * chunk, axis=-1, keepdims=True))
                keys = chunk / jnp.maximum(nrm, NORM_EPS)
                k_mean = keys.mean(axis=1)
                v_target = value_gen(outputs).mean(axis=1)
                Mk = jnp.einsum('boi,bi->bo', M, k_mean)
                err = v_target - Mk
                update = err[:, :, None] * k_mean[:, None, :]
                M_new = alpha * M + eta * update
                gate = jax.nn.sigmoid(k_mean @ gate_w + gate_b[0])[:, None, None]
                M_new = gate * M_new + (1.0 - gate) * M
                M_norm = jnp.sqrt(jnp.sum(M_new * M_new, axis=(-2, -1), keepdims=True))
                scale = jnp.minimum(MAX_NORM / (M_norm + 1e-06), 1.0)
                return (M_new * scale, outputs)
            M_final, outs = jax.lax.scan(step, M0, x_chunks)
            outs = outs.transpose(1, 0, 2, 3).reshape(b, s, d)
            final_out = value_gen(outs)
            return (final_out, M_final)

        def _reference_tuple_inner(x, M_init, eta_w, eta_b, alpha_w, alpha_b, gate_w, gate_b, vg_w1, vg_w2):
            return _forward(x, M_init, eta_w, eta_b, alpha_w, alpha_b, gate_w, gate_b, vg_w1, vg_w2)
        key = jax.random.key(seed)
        ks = jax.random.split(key, 10)
        return {'x': jax.random.normal(ks[0], (B, S, D), jnp.float32), 'M_init': jax.random.normal(ks[1], (D, D), jnp.float32) * 0.02, 'eta_w': jax.random.normal(ks[2], (D,), jnp.float32) * 0.02, 'eta_b': jax.random.normal(ks[3], (1,), jnp.float32), 'alpha_w': jax.random.normal(ks[4], (D,), jnp.float32) * 0.02, 'alpha_b': jax.random.normal(ks[5], (1,), jnp.float32), 'gate_w': jax.random.normal(ks[6], (D,), jnp.float32) * 0.02, 'gate_b': jax.random.normal(ks[7], (1,), jnp.float32), 'vg_w1': jax.random.normal(ks[8], (D, D), jnp.float32) * 0.02, 'vg_w2': jax.random.normal(ks[9], (D, D), jnp.float32) * 0.02}
    _L0_attn_in = _L0_attn_setup()

    def _L0_ffn_setup():
        import jax, jax.numpy as jnp
        import numpy as np
        E = 8
        K = 2
        C = 128
        F = 256
        EPS = 1e-05
        key = jax.random.key(seed)
        ks = jax.random.split(key, 6)
        x = jax.random.normal(ks[0], (2, 128, C), dtype=jnp.float32)
        ln_gamma = 1.0 + 0.02 * jax.random.normal(ks[1], (C,), dtype=jnp.float32)
        ln_beta = 0.02 * jax.random.normal(ks[2], (C,), dtype=jnp.float32)
        gate_w = jax.random.normal(ks[3], (E, C), dtype=jnp.float32) / np.sqrt(C)
        w1 = jax.random.normal(ks[4], (E, F, C), dtype=jnp.float32) / np.sqrt(C)
        w2 = jax.random.normal(ks[5], (E, C, F), dtype=jnp.float32) / np.sqrt(F)
        return {'x': x, 'ln_gamma': ln_gamma, 'ln_beta': ln_beta, 'gate_w': gate_w, 'w1': w1, 'w2': w2}
    _L0_ffn_in = _L0_ffn_setup()
    _d = {'L0_attn_x': _L0_attn_in['x'], 'L0_attn_M_init': _L0_attn_in['M_init'], 'L0_attn_eta_w': _L0_attn_in['eta_w'], 'L0_attn_eta_b': _L0_attn_in['eta_b'], 'L0_attn_alpha_w': _L0_attn_in['alpha_w'], 'L0_attn_alpha_b': _L0_attn_in['alpha_b'], 'L0_attn_gate_w': _L0_attn_in['gate_w'], 'L0_attn_gate_b': _L0_attn_in['gate_b'], 'L0_attn_vg_w1': _L0_attn_in['vg_w1'], 'L0_attn_vg_w2': _L0_attn_in['vg_w2'], 'L0_ffn_ln_gamma': _L0_ffn_in['ln_gamma'], 'L0_ffn_ln_beta': _L0_ffn_in['ln_beta'], 'L0_ffn_gate_w': _L0_ffn_in['gate_w'], 'L0_ffn_w1': _L0_ffn_in['w1'], 'L0_ffn_w2': _L0_ffn_in['w2']}
    _x0 = _d['L0_attn_x']
    _d['L0_attn_x'] = jax.random.normal(jax.random.fold_in(jax.random.key(seed), 1), (8, 512, 128), dtype=_x0.dtype)
    del _x0
    return _d

def reference(L0_attn_x, L0_attn_M_init, L0_attn_eta_w, L0_attn_eta_b, L0_attn_alpha_w, L0_attn_alpha_b, L0_attn_gate_w, L0_attn_gate_b, L0_attn_vg_w1, L0_attn_vg_w2, L0_ffn_ln_gamma, L0_ffn_ln_beta, L0_ffn_gate_w, L0_ffn_w1, L0_ffn_w2):

    def _L0_attn_ref(x, M_init, eta_w, eta_b, alpha_w, alpha_b, gate_w, gate_b, vg_w1, vg_w2):
        import jax, jax.numpy as jnp
        import numpy as np
        B, S, D = (4, 512, 128)
        CHUNK = 64
        MAX_LR = 0.2
        MIN_DECAY = 0.5
        MAX_NORM = 30.0
        NORM_EPS = 1e-05

        def _forward(x, M_init, eta_w, eta_b, alpha_w, alpha_b, gate_w, gate_b, vg_w1, vg_w2):
            b, s, d = x.shape
            n_ch = s // CHUNK

            def value_gen(y):
                h = jax.nn.silu(y @ vg_w1.T) @ vg_w2.T
                return h + y
            x_chunks = x.reshape(b, n_ch, CHUNK, d).transpose(1, 0, 2, 3)
            M0 = jnp.broadcast_to(M_init, (b, d, d))

            def step(M, chunk):
                eta_tok = jax.nn.sigmoid(chunk @ eta_w + eta_b[0]) * MAX_LR
                alpha_tok = MIN_DECAY + jax.nn.sigmoid(chunk @ alpha_w + alpha_b[0]) * (1.0 - MIN_DECAY)
                eta = eta_tok.mean(axis=1)[:, None, None]
                alpha = alpha_tok.mean(axis=1)[:, None, None]
                outputs = jnp.einsum('bci,boi->bco', chunk, M)
                nrm = jnp.sqrt(jnp.sum(chunk * chunk, axis=-1, keepdims=True))
                keys = chunk / jnp.maximum(nrm, NORM_EPS)
                k_mean = keys.mean(axis=1)
                v_target = value_gen(outputs).mean(axis=1)
                Mk = jnp.einsum('boi,bi->bo', M, k_mean)
                err = v_target - Mk
                update = err[:, :, None] * k_mean[:, None, :]
                M_new = alpha * M + eta * update
                gate = jax.nn.sigmoid(k_mean @ gate_w + gate_b[0])[:, None, None]
                M_new = gate * M_new + (1.0 - gate) * M
                M_norm = jnp.sqrt(jnp.sum(M_new * M_new, axis=(-2, -1), keepdims=True))
                scale = jnp.minimum(MAX_NORM / (M_norm + 1e-06), 1.0)
                return (M_new * scale, outputs)
            M_final, outs = jax.lax.scan(step, M0, x_chunks)
            outs = outs.transpose(1, 0, 2, 3).reshape(b, s, d)
            final_out = value_gen(outs)
            return (final_out, M_final)

        def _reference_tuple_inner(x, M_init, eta_w, eta_b, alpha_w, alpha_b, gate_w, gate_b, vg_w1, vg_w2):
            return _forward(x, M_init, eta_w, eta_b, alpha_w, alpha_b, gate_w, gate_b, vg_w1, vg_w2)
        return _reference_tuple_inner(x, M_init, eta_w, eta_b, alpha_w, alpha_b, gate_w, gate_b, vg_w1, vg_w2)[0]

    def _L0_ffn_ref(x, ln_gamma, ln_beta, gate_w, w1, w2):
        import jax, jax.numpy as jnp
        import numpy as np
        E = 8
        K = 2
        C = 128
        F = 256
        EPS = 1e-05
        B, T, Cc = x.shape
        xf = x.reshape(-1, Cc)
        mu = jnp.mean(xf, axis=-1, keepdims=True)
        var = jnp.var(xf, axis=-1, keepdims=True)
        rn = (xf - mu) * jax.lax.rsqrt(var + EPS) * ln_gamma + ln_beta
        logits = rn @ gate_w.T
        probs = jax.nn.softmax(logits, axis=-1)
        rw, sel = jax.lax.top_k(probs, K)
        comb = jnp.sum(jax.nn.one_hot(sel, E, dtype=xf.dtype) * rw[..., None], axis=1)
        h = jax.nn.gelu(jnp.einsum('nc,efc->enf', xf, w1), approximate=False)
        y = jnp.einsum('enf,ecf->enc', h, w2)
        out = jnp.einsum('enc,ne->nc', y, comb)
        return out.reshape(B, T, Cc)
    x = L0_attn_x
    x = _layernorm(x + _L0_attn_ref(x, L0_attn_M_init, L0_attn_eta_w, L0_attn_eta_b, L0_attn_alpha_w, L0_attn_alpha_b, L0_attn_gate_w, L0_attn_gate_b, L0_attn_vg_w1, L0_attn_vg_w2), axis=-1)
    x = _layernorm(x + _L0_ffn_ref(x, L0_ffn_ln_gamma, L0_ffn_ln_beta, L0_ffn_gate_w, L0_ffn_w1, L0_ffn_w2), axis=-1)
    return x

_drawn_inputs = setup_inputs


def setup_inputs(seed=0):
    import zlib

    import numpy as np

    out = dict(_drawn_inputs(seed))
    spreads = {}
    factors = {'L0_attn_eta_w': 64.0,
     'L0_attn_alpha_w': 64.0,
     'L0_attn_gate_w': 64.0,
     'L0_attn_vg_w1': 5.566,
     'L0_attn_vg_w2': 5.891,
     'L0_ffn_ln_gamma': 2.78,
     'L0_ffn_ln_beta': 4.348}
    for name, (base, spread) in spreads.items():
        noise = np.random.default_rng([zlib.crc32(name.encode()), seed]).standard_normal(out[name].shape)
        drawn = base * np.exp(spread * noise) if base else spread * noise
        out[name] = jnp.asarray(drawn.astype(out[name].dtype))
    for name, factor in factors.items():
        out[name] = (out[name] * factor).astype(out[name].dtype)
    return out
```

```python
from contextlib import ExitStack

import numpy as np

import concourse.bass as bass
from concourse import mybir

F32 = mybir.dt.float32
F32R = mybir.dt.float32r
ALU = mybir.AluOpType
ACT = mybir.ActivationFunctionType
AX_X = mybir.AxisListType.X

P = 128
B, S, D = 8, 512, 128
CHUNK = 64
G = S // CHUNK
TOK = B * CHUNK
TILES = TOK // P
ALL_TILES = G * TILES
AUG = CHUNK + 1
HALF = B // 2
E = 8
F = 256
FB = F // P
BLOCKS = E * FB
H_BANKS = 3
H_RING = 6
FULL_RING = 4
Y_BANKS = 2
YM_RING = 3
COMB_PARTS = 2
COMB_E = E // COMB_PARTS
STAT_TILES = 8
STAT_STEPS = ALL_TILES // STAT_TILES
MAX_LR, MIN_DECAY, MAX_NORM, NORM_EPS, LN_EPS = 0.2, 0.5, 30.0, 1e-5, 1e-5

C_GAMMA, C_BETA, C_ETA_W, C_ALPHA_W, C_GATE_W, C_ETA_B, C_ALPHA_B, C_GATE_B, C_ROUTE = range(9)
C_PARAMS = C_ROUTE + E
K_IDENT, K_ONES, K_HALVES, K_LOWER = 0, P, 2 * P, 2 * P + 2
K_CONSTS = K_LOWER + E * E


def build(nc, x_tok, x_chan, m_init_t, vg_w1t, vg_w2t, w1t, w2t, params, consts, out):
    with ExitStack() as ctx:
        def sb(name, shape, dt=F32):
            return ctx.enter_context(nc.sbuf_tensor(name, shape, dt))

        def sem(name):
            return ctx.enter_context(nc.semaphore(name))

        def sems(name, n):
            return [sem(f"{name}{i}") for i in range(n)]

        hp = [ctx.enter_context(nc.psum_tensor(f"hp{i}", [P, TOK], F32)) for i in range(H_BANKS)]
        yp = [ctx.enter_context(nc.psum_tensor(f"yp{i}", [P, TOK], F32)) for i in range(Y_BANKS)]
        ca = ctx.enter_context(nc.psum_tensor("ca", [P, TOK], F32))
        cb = ctx.enter_context(nc.psum_tensor("cb", [P, TOK], F32))
        small = ctx.enter_context(nc.psum_tensor("small", [P, TOK], F32))
        err_ps = small[:, 0:B]
        errt_ps = small[0:B, 8:8 + P]
        ss_ps = small[:, 136:136 + B]
        logit_ps = small[:, 144:144 + TILES * 2 * E].rearrange("p (q e) -> p q e", q=TILES)
        combt_ps = small[0:E * TILES, 208:208 + P]
        kd_ps = [yp[i][:, 0:STAT_TILES * 4].rearrange("p (t w) -> p t w", w=4) for i in range(2)]
        route_ps = cb[:, 0:2 * E]
        lr_ps = small[0:CHUNK, 384:384 + 2 * G * B].rearrange("p (c w) -> p c w", w=2)
        mean_ps = hp[0][:, 0:2 * G * B].rearrange("p (w c) -> p w c", w=2)
        gate_ps = hp[1][:, 0:G * B]
        halves = [ca, cb]

        xtok = sb("xtok", [P, ALL_TILES, D])
        xt = sb("xt", [P, G, B, AUG])
        prm = sb("prm", [P, C_PARAMS])
        cst = sb("cst", [P, K_CONSTS])
        vw1 = sb("vw1", [P, D])
        vw2 = sb("vw2", [P, D])
        vw2h = sb("vw2h", [P, D])
        combb = [sb(f"combb{i}", [P, E, TOK]) for i in range(2)]
        raw = combb[1][:].rearrange("p e t -> p (e t)")
        w1 = raw[:, 0:E * F].rearrange("p (e f) -> p e f", e=E)
        w2 = raw[:, E * F:2 * E * F].rearrange("p (e k c) -> p e k c", e=E, k=FB)
        w1_hi, w1_lo = sb("w1_hi", [P, E, F], F32R), sb("w1_lo", [P, E, F], F32R)
        w2_hi, w2_lo = sb("w2_hi", [P, E, FB, D], F32R), sb("w2_lo", [P, E, FB, D], F32R)
        ident = cst[:, K_IDENT:K_IDENT + P]
        ones = cst[:, K_ONES:K_ONES + P]
        half64 = cst[:, K_HALVES:K_HALVES + 2]
        lower = cst[:, K_LOWER:K_LOWER + E * E].rearrange("p (e f) -> p e f", e=E)

        sq = sb("sq", [P, STAT_TILES, D])
        ssq = sb("ssq", [P, ALL_TILES])
        inv = sb("inv", [P, ALL_TILES])
        kdw = sb("kdw", [P, ALL_TILES, 4])
        km = sb("km", [P, G * B])
        kb = sb("kb", [P, G * B])
        kbrow = sb("kbrow", [B, G, P])
        lr_th = sb("lr_th", [CHUNK, 2, G * B])
        lr_bias = sb("lr_bias", [P, 3])
        eta = sb("eta", [P, G * B])
        alpha = sb("alpha", [P, G * B])
        gate = sb("gate", [P, G * B])
        gate_rep = sb("gate_rep", [P, P])
        decay = sb("decay", [P, G * B])
        lrate = sb("lrate", [P, G * B])
        c_half = sb("c_half", [P, ALL_TILES])
        c_root = sb("c_root", [P, B])
        c_e = sb("c_e", [P, TILES, E])

        mt = sb("mt", [P, B, D])
        am = sb("am", [P, B, D])
        msq = sb("msq", [P, B, D])
        scale = sb("scale", [P, B])
        ascale = sb("ascale", [P, B])
        nrm = [sb(f"nrm{i}", [P, B]) for i in range(4)]
        mss = sb("mss", [P, B])
        ot = sb("ot", [P, B, AUG])
        ox = sb("ox", [P, B, CHUNK])
        th = sb("th", [P, TOK])
        hid = sb("hid", [P, TOK])
        hsum = sb("hsum", [P, B])
        err = sb("err", [P, B])
        errrow = sb("errrow", [B, P])
        kmask = sb("kmask", [B, B, P])
        rt = sb("rt", [P, TOK])

        st = [sb(f"st{i}", [P, TILES, 6]) for i in range(3)]
        ln = [[sb(f"ln{i}_{j}", [P, TILES]) for j in range(9)] for i in range(3)]
        x1 = [sb(f"x1_{i}", [P, TILES, D]) for i in range(2)]
        x1t_hi = [sb(f"x1t_hi{i}", [P, TOK], F32R) for i in range(2)]
        x1t_lo = [sb(f"x1t_lo{i}", [P, TOK], F32R) for i in range(2)]
        route_w = sb("route_w", [P, 2 * E])
        route_r = sb("route_r", [P, 2 * E], F32R)
        route_s = sb("route_s", [P, 2 * E])
        lg = [sb(f"lg{i}", [P, TILES, E]) for i in range(12)]
        lmax = sb("lmax", [P, TILES])
        esum = sb("esum", [P, TILES])
        einv = sb("einv", [P, TILES])
        beats = sb("beats", [P, TILES, E, E])
        ties = sb("ties", [P, TILES, E, E])
        rank = sb("rank", [P, TILES, E])
        comb = sb("comb", [P, E, TILES])
        combt = sb("combt", [E * TILES, P])
        comb_dram = nc.dram_tensor("comb_dram", [2, E * TILES, P], F32).ap()

        h_full = sb("h_full", [P, FULL_RING, TOK])
        h_hi = sb("h_hi", [P, H_RING, TOK], F32R)
        h_lo = sb("h_lo", [P, H_RING, TOK], F32R)
        ym = sb("ym", [P, YM_RING, TOK])
        acc = [sb(f"acc{i}", [P, TOK]) for i in range(2)]
        r2 = sb("r2", [P, TILES, D])

        def result(g):
            return xtok[:, g * TILES:(g + 1) * TILES, :] if isinstance(g, int) else xtok[:, bass.ds(g * TILES, TILES), :]

        x_in = sems("x_in", STAT_STEPS)
        xt_in, m_in, par_in, vg_in, w1_in, w2_in = (sem(n) for n in ("xt_in", "m_in", "par_in", "vg_in", "w1_in", "w2_in"))
        const_set, par_set = sem("const_set"), sem("par_set")
        sq_set, ssq_set, inv_set, kdw_set, kd_mm, km_set = (sem(n) for n in ("sq_set", "ssq_set", "inv_set", "kdw_set", "kd_mm", "km_set"))
        lr_mm, lr_tanh, lr_mean, gate_mm, coef_step, coef_set, kb_mm, kb_set = (sem(n) for n in (
            "lr_mm", "lr_tanh", "lr_mean", "gate_mm", "coef_step", "coef_set", "kb_mm", "kb_set"))
        w1_hi_set, w1_lo_set, w2_hi_set, w2_lo_set = (sem(n) for n in ("w1_hi_set", "w1_lo_set", "w2_hi_set", "w2_lo_set"))
        route_mm = sem("route_mm")
        out_mm, ot_set, ox_set, hid_mm, th_set, hid_set, hsum_set, val_mm, rt_set, r_mm = (sem(n) for n in (
            "out_mm", "ot_set", "ox_set", "hid_mm", "th_set", "hid_set", "hsum_set", "val_mm", "rt_set", "r_mm"))
        err_mm, err_set, errt_mm, errrow_set, kmask_set, am_set, upd_mm, mt_set, msq_set, mss_set, ss_mm = (sem(n) for n in (
            "err_mm", "err_set", "errt_mm", "errrow_set", "kmask_set", "am_set", "upd_mm", "mt_set", "msq_set", "mss_set", "ss_mm"))
        nrm_in, nrm_root, nrm_add, nrm_inv, scale_set, ascale_set = (sem(n) for n in (
            "nrm_in", "nrm_root", "nrm_add", "nrm_inv", "scale_set", "ascale_set"))
        ln_stats, ln_sums, ln_sq, ln_var, ln_rstd, ln_bias = (sems(n, 3) for n in (
            "ln_stats", "ln_sums", "ln_sq", "ln_var", "ln_rstd", "ln_bias"))
        x1_set, x1t_mm, x1t_hi_set, x1t_lo_set, logit_mm = (sem(n) for n in ("x1_set", "x1t_mm", "x1t_hi_set", "x1t_lo_set", "logit_mm"))
        lg_step = sems("lg_step", 9)
        exp_set, rank_step, comb_set, combt_mm, combt_set, comb_out = sem("exp_set"), sems("rank_step", 4), sem("comb_set"), sem("combt_mm"), sem("combt_set"), sem("comb_out")
        comb_in = sems("comb_in", COMB_PARTS)
        w1_mm = sems("w1_mm", E)
        h_full_set = sems("h_full_set", E)
        h_lo_set = sems("h_lo_set", E)
        w2_mm = sems("w2_mm", E)
        y_weighted = sems("y_weighted", E)
        y_added = [None] + sems("y_added", E - 1)
        fin_mm, r2_set, osb_set = sem("fin_mm"), sem("r2_set"), sem("osb_set")
        stored = sem("stored")

        def earlier(n, ring, count):
            if n >= ring:
                return n - ring, True
            return max(m for m in range(count) if m % ring == n % ring), False

        def of_block(n, p):
            return p * FB + (n % FB + 1)

        def wait_earlier_block(eng, sem_list, n, ring, p):
            m, same = earlier(n, ring, BLOCKS)
            if same:
                eng.wait_ge(sem_list[m // FB], of_block(m, p))
            elif not (isinstance(p, int) and p == 0):
                eng.wait_ge(sem_list[m // FB], of_block(m, p - 1))

        def groups_before_loop_and_after(eng, body):
            body(-1, 1)
            body(0, 0)
            with eng.Fori(0, 2) as pair:
                for j in range(2):
                    body(pair * 2 + (1 + j), 1 - j)
            for p in range(5, G):
                body(p, p % 2)

        def chained(p):
            return not isinstance(p, int) or p + 1 < G

        def updated(p):
            return not isinstance(p, int) or p + 2 < G

        def ffn(p):
            return not isinstance(p, int) or p >= 0

        def finished(p):
            return not isinstance(p, int) or p >= 1

        def group(t, g):
            return t[:, bass.ds(g * B, B)] if not isinstance(g, int) else t[:, g * B:(g + 1) * B]

        def xgroup(g):
            return xt[:, g] if isinstance(g, int) else xt[:, bass.ds(g, 1)].rearrange("p o b c -> p (o b) c")

        def rows(g):
            return kbrow[:, g, :] if isinstance(g, int) else kbrow[:, bass.ds(g, 1), :].rearrange("p o c -> p (o c)")

        block = ctx.enter_context(nc.Block())

        @block.sync
        def _(sp):
            sp.dma_start(prm[:], params).then_inc(par_in, 16)
            sp.dma_start(cst[:], consts).then_inc(par_in, 16)
            for i in range(STAT_STEPS):
                part = slice(i * STAT_TILES, (i + 1) * STAT_TILES)
                sp.dma_start(xtok[:, part, :], x_tok[:, part, :]).then_inc(x_in[i], 16)
                if i == 0:
                    sp.dma_start(xt[:], x_chan).then_inc(xt_in, 16)
            sp.dma_start(w1, w1t).then_inc(w1_in, 16)
            sp.dma_start(w2, w2t).then_inc(w2_in, 16)

            def body(p, parity):
                g = p + 1
                if finished(p):
                    sp.wait_ge(osb_set, p)
                    row = out[p - 1] if isinstance(p, int) else out[bass.ds(p - 1, 1)].rearrange("o p c -> (o p) c")
                    sp.dma_start(row, result(p - 1).rearrange("p q c -> p (q c)")).then_inc(stored, 16)
                if chained(p):
                    sp.wait_ge(combt_set, g + 1)
                    sp.dma_start(comb_dram[1 - parity], combt[:]).then_inc(comb_out, 16)
                    sp.wait_ge(comb_out, g * 16 + 16)
                    for c in range(COMB_PARTS):
                        part = slice(c * COMB_E, (c + 1) * COMB_E)
                        if finished(p):
                            sp.wait_ge(y_weighted[(c + 1) * COMB_E - 1], p)
                        src = comb_dram[1 - parity, c * COMB_E * TILES:(c + 1) * COMB_E * TILES, :].rearrange("(o q) t -> o (q t)", o=1)
                        sp.dma_start(combb[1 - parity][:, part, :].rearrange("p e t -> p (e t)"),
                                     src.to_broadcast([P, COMB_E * TOK])).then_inc(comb_in[c], 16)

            groups_before_loop_and_after(sp, body)
            sp.wait_ge(osb_set, G)
            sp.dma_start(out[G - 1], result(G - 1).rearrange("p q c -> p (q c)")).then_inc(stored, 16)
            sp.wait_ge(stored, 16 * G)

        @block.gpsimd
        def _(pool):
            pool.memset(c_half[:], -0.5).then_inc(const_set, 1)
            pool.memset(c_root[:], 0.5).then_inc(const_set, 1)
            pool.memset(c_e[:], float(np.e)).then_inc(const_set, 1)
            pool.memset(scale[:], 1.0).then_inc(const_set, 1)
            pool.wait_ge(const_set, 4)
            for i in range(STAT_STEPS):
                part = slice(i * STAT_TILES, (i + 1) * STAT_TILES)
                pool.wait_ge(ssq_set, i + 1)
                pool.tensor_tensor(inv[:, part], ssq[:, part], c_half[:, part], ALU.pow).then_inc(inv_set, 1)
            for e in range(E):
                pool.wait_ge(w1_hi_set, e + 1)
                pool.tensor_tensor(w1_lo[:, e, :], w1[:, e, :], w1_hi[:, e, :].bitcast(F32), ALU.subtract).then_inc(w1_lo_set, 1)

            def power(i, g):
                pool.wait_ge(ln_var[i], g + 1)
                pool.tensor_tensor(ln[i][6][:], ln[i][5][:], c_half[:, 0:TILES], ALU.pow).then_inc(ln_rstd[i], 1)

            def y_add(e, p, parity):
                pool.wait_ge(y_weighted[e], p + 1)
                if e > 1:
                    pool.wait_ge(y_added[e - 1], p + 1)
                pool.tensor_tensor(acc[parity][:], acc[parity][:], ym[:, (e - 1) % YM_RING, :], ALU.add).then_inc(y_added[e], 1)

            def body(p, parity):
                g = p + 1
                if chained(p):
                    pool.wait_ge(ot_set, g + 1)
                    pool.tensor_tensor(ox[:], ot[:, :, 0:CHUNK], xgroup(g)[:, :, 0:CHUNK], ALU.add).then_inc(ox_set, 1)
                if chained(p):
                    if updated(p):
                        pool.wait_ge(ascale_set, g + 1)
                        pool.tensor_tensor(am[:], mt[:], ascale[:].unsqueeze(2).to_broadcast([P, B, D]), ALU.mult).then_inc(am_set, 1)
                        pool.wait_ge(kb_set, 1)
                        pool.tensor_tensor(kmask[:], rows(g).unsqueeze(1).to_broadcast([B, B, P]),
                                           ident[0:B, 0:B].unsqueeze(2).to_broadcast([B, B, P]), ALU.mult).then_inc(kmask_set, 1)
                    power(0, g)
                if ffn(p):
                    y_add(1, p, parity)
                if finished(p):
                    power(2, p - 1)
                if ffn(p):
                    y_add(2, p, parity)
                    y_add(3, p, parity)
                if chained(p):
                    power(1, g)
                    pool.wait_ge(lg_step[6], g + 1)
                    pool.tensor_tensor(lg[7][:], c_e[:], lg[6][:], ALU.pow).then_inc(exp_set, 1)
                if ffn(p):
                    y_add(4, p, parity)
                if chained(p) and updated(p):
                    pool.wait_ge(nrm_in, g + 1)
                    pool.tensor_tensor(nrm[1][:], nrm[0][:], c_root[:], ALU.pow).then_inc(nrm_root, 1)
                if ffn(p):
                    for e in range(5, E):
                        y_add(e, p, parity)

            groups_before_loop_and_after(pool, body)
            power(2, G - 1)

        @block.scalar
        def _(act):
            act.dma_start(mt[:], m_init_t.unsqueeze(1).to_broadcast([P, B, D])).then_inc(m_in, 16)
            act.dma_start(vw1[:], vg_w1t).then_inc(vg_in, 16)
            act.dma_start(vw2[:], vg_w2t).then_inc(vg_in, 16)
            for i in range(STAT_STEPS):
                act.wait_ge(x_in[i], 16)
                if i:
                    act.wait_ge(ssq_set, i)
                act.activation(sq[:], xtok[:, i * STAT_TILES:(i + 1) * STAT_TILES, :], ACT.Square).then_inc(sq_set, 1)
            act.wait_ge(lr_mm, 1)
            act.wait_ge(par_set, 1)
            for w in range(2):
                act.activation(lr_th[:, w, :], lr_ps[:, :, w], ACT.Tanh, scale=0.5, bias=lr_bias[0:CHUNK, w:w + 1]).then_inc(lr_tanh, 1)
            act.wait_ge(gate_mm, 1)
            act.activation(gate[:], gate_ps, ACT.Tanh, scale=0.5, bias=lr_bias[:, 2:3]).then_inc(lr_tanh, 1)
            act.wait_ge(w1_in, 16)
            for e in range(E):
                act.activation(w1_hi[:, e, :], w1[:, e, :], ACT.Copy).then_inc(w1_hi_set, 1)
            act.wait_ge(w2_in, 16)
            for e in range(E):
                act.activation(w2_hi[:, e], w2[:, e], ACT.Copy).then_inc(w2_hi_set, 1)

            def gelus(n, p):
                act.wait_ge(w1_mm[n // FB], of_block(n, p))
                m, same = earlier(n, H_RING, BLOCKS)
                if same:
                    act.wait_ge(w2_mm[m // FB], p + 1)
                elif not (isinstance(p, int) and p == 0):
                    act.wait_ge(w2_mm[m // FB], p)
                act.activation(h_hi[:, n % H_RING, :], hp[n % H_BANKS][:], ACT.Gelu)
                wait_earlier_block(act, h_lo_set, n, FULL_RING, p)
                act.activation(h_full[:, n % FULL_RING, :], hp[n % H_BANKS][:], ACT.Gelu).then_inc(h_full_set[n // FB], 1)

            def normalise(i, src, dst, done, g):
                act.wait_ge(ln_bias[i], g + 1)
                for q in range(TILES):
                    last = act.activation(dst[:, q, :], src[:, q, :], ACT.Identity,
                                          scale=ln[i][6][:, q:q + 1], bias=ln[i][7][:, q:q + 1])
                last.then_inc(done, 1)

            def body(p, parity):
                g = p + 1
                if ffn(p):
                    gelus(0, p)
                    gelus(1, p)
                if chained(p):
                    act.wait_ge(hid_mm, g + 1)
                    act.activation(th[:], ca[:], ACT.Tanh, scale=0.5).then_inc(th_set, 1)
                if ffn(p):
                    for n in range(2, 8):
                        gelus(n, p)
                if chained(p):
                    if finished(p):
                        act.wait_ge(r2_set, p)
                    normalise(0, ca[:].rearrange("p (q c) -> p q c", q=TILES), x1[1 - parity], x1_set, g)
                if ffn(p):
                    gelus(8, p)
                    gelus(9, p)
                if finished(p):
                    normalise(2, r2, result(p - 1), osb_set, p - 1)
                if chained(p):
                    act.wait_ge(x1t_mm, g + 1)
                    act.activation(x1t_hi[1 - parity][:], cb[:], ACT.Copy).then_inc(x1t_hi_set, 1)
                if ffn(p):
                    for n in range(10, 14):
                        gelus(n, p)
                if chained(p) and updated(p):
                    act.wait_ge(mt_set, g + 1)
                    act.activation(msq[:], mt[:], ACT.Square).then_inc(msq_set, 1)
                if ffn(p):
                    gelus(14, p)
                    gelus(15, p)

            groups_before_loop_and_after(act, body)
            normalise(2, r2, result(G - 1), osb_set, G - 1)

        @block.vector
        def _(dve):
            dve.wait_ge(par_in, 32)
            dve.tensor_scalar(lr_bias[:], prm[:, C_ETA_B:C_ETA_B + 3], 0.5, None, ALU.mult).then_inc(par_set, 1)
            dve.tensor_scalar(route_w[:, 0:E], prm[:, C_ROUTE:C_PARAMS], prm[:, C_GAMMA:C_GAMMA + 1], None, ALU.mult).then_inc(par_set, 1)
            dve.tensor_scalar(route_w[:, E:2 * E], prm[:, C_ROUTE:C_PARAMS], prm[:, C_BETA:C_BETA + 1], None, ALU.mult).then_inc(par_set, 1)
            dve.tensor_scalar(gate_rep[:], ones, prm[:, C_GATE_W:C_GATE_W + 1], None, ALU.mult).then_inc(par_set, 1)
            dve.wait_ge(par_set, 4)
            dve.tensor_copy(route_r[:, 0:E], route_w[:, 0:E]).then_inc(par_set, 1)
            dve.wait_ge(par_set, 5)
            dve.tensor_tensor(route_r[:, E:2 * E], route_w[:, 0:E], route_r[:, 0:E].bitcast(F32), ALU.subtract).then_inc(par_set, 1)
            dve.wait_ge(vg_in, 32)
            dve.tensor_scalar(vw2h[:], vw2[:], 0.5, None, ALU.mult).then_inc(par_set, 1)

            half_b = half64.unsqueeze(1).to_broadcast([P, STAT_TILES, 2])
            for i in range(STAT_STEPS):
                part = slice(i * STAT_TILES, (i + 1) * STAT_TILES)
                dve.wait_ge(sq_set, i + 1)
                dve.tensor_reduce(ssq[:, part], sq[:], AX_X, ALU.add).then_inc(coef_step, 1)
                dve.wait_ge(coef_step, 3 * i + 1)
                dve.tensor_scalar(ssq[:, part], ssq[:, part], NORM_EPS ** 2, None, ALU.max).then_inc(ssq_set, 1)
                dve.wait_ge(inv_set, i + 1)
                dve.tensor_tensor(kdw[:, part, 0:2], inv[:, part].unsqueeze(2).to_broadcast([P, STAT_TILES, 2]), half_b,
                                  ALU.mult).then_inc(coef_step, 1)
                dve.wait_ge(coef_step, 3 * i + 2)
                dve.tensor_tensor(kdw[:, part, 2:4], half_b, kdw[:, part, 0:2], ALU.subtract).then_inc(kdw_set, 1)
                dve.wait_ge(kd_mm, i + 1)
                dve.tensor_copy(km[:, i * 2 * STAT_TILES:(i + 1) * 2 * STAT_TILES].rearrange("p (t h) -> p t h", h=2),
                                kd_ps[i % 2][:, :, 0:2]).then_inc(coef_step, 1)
                dve.wait_ge(xt_in, 16)
                dve.tensor_copy(xt[:, 2 * i:2 * i + 2, :, CHUNK].rearrange("p t (q h) -> p (t q) h", h=2),
                                kd_ps[i % 2][:, :, 2:4]).then_inc(km_set, 1)

            dve.wait_ge(route_mm, 1)
            dve.tensor_copy(route_s[:], route_ps)
            step = 3 * STAT_STEPS
            dve.wait_ge(lr_mean, 1)
            dve.tensor_scalar(eta[:], mean_ps[:, 0, :], MAX_LR / 2 / CHUNK, MAX_LR / 2, ALU.mult, ALU.add).then_inc(coef_step, 1)
            dve.tensor_scalar(alpha[:], mean_ps[:, 1, :], (1 - MIN_DECAY) / 2 / CHUNK, (MIN_DECAY - 1) / 2, ALU.mult, ALU.add).then_inc(coef_step, 1)
            dve.wait_ge(lr_tanh, 3)
            dve.tensor_scalar(gate[:], gate[:], 0.5, 0.5, ALU.mult, ALU.add).then_inc(coef_step, 1)
            dve.wait_ge(coef_step, step + 3)
            dve.tensor_tensor(decay[:], gate[:], alpha[:], ALU.mult).then_inc(coef_step, 1)
            dve.tensor_tensor(lrate[:], gate[:], eta[:], ALU.mult).then_inc(coef_step, 1)
            dve.wait_ge(coef_step, step + 5)
            dve.tensor_scalar(decay[:], decay[:], 1.0, None, ALU.add).then_inc(coef_step, 1)
            dve.tensor_tensor(kb[:], km[:], lrate[:], ALU.mult).then_inc(coef_set, 1)
            dve.wait_ge(coef_step, step + 6)
            dve.wait_ge(kb_mm, 1)
            for i, bank in enumerate(halves):
                last = dve.tensor_copy(kbrow[:, i * G // 2:(i + 1) * G // 2, :], bank[0:B, :].rearrange("p (t c) -> p t c", c=P))
            last.then_inc(kb_set, 1)
            for e in range(E):
                dve.wait_ge(w2_hi_set, e + 1)
                dve.tensor_tensor(w2_lo[:, e], w2[:, e], w2_hi[:, e].bitcast(F32), ALU.subtract).then_inc(w2_lo_set, 1)

            def h_low(n, p):
                dve.wait_ge(h_full_set[n // FB], of_block(n, p))
                dve.tensor_tensor(h_lo[:, n % H_RING, :], h_full[:, n % FULL_RING, :],
                                  h_hi[:, n % H_RING, :].bitcast(F32), ALU.subtract).then_inc(h_lo_set[n // FB], 1)

            def weigh(e, p, parity):
                dve.wait_ge(w2_mm[e], p + 1)
                if e % COMB_E == 0:
                    dve.wait_ge(comb_in[e // COMB_E], p * 16 + 16)
                if e:
                    m, same = earlier(e - 1, YM_RING, E - 1)
                    if same:
                        dve.wait_ge(y_added[m + 1], p + 1)
                    elif not (isinstance(p, int) and p == 0):
                        dve.wait_ge(y_added[m + 1], p)
                dst = ym[:, (e - 1) % YM_RING, :] if e else acc[parity][:]
                dve.tensor_tensor(dst, yp[e % Y_BANKS][:], combb[parity][:, e, :], ALU.mult).then_inc(y_weighted[e], 1)

            def statistics(i, src, g):
                for q in range(TILES):
                    last = dve.bn_stats(st[i][:, q, :], src[:, q, :])
                last.then_inc(ln_stats[i], 1)
                dve.wait_ge(ln_stats[i], g + 1)
                dve.tensor_tensor(ln[i][0][:], st[i][:, :, 1], st[i][:, :, 4], ALU.add)
                dve.tensor_tensor(ln[i][1][:], st[i][:, :, 1], st[i][:, :, 4], ALU.subtract)
                dve.tensor_tensor(ln[i][2][:], st[i][:, :, 2], st[i][:, :, 5], ALU.add).then_inc(ln_sums[i], 1)
                dve.wait_ge(ln_sums[i], g + 1)
                dve.scalar_tensor_tensor(out=ln[i][3][:], in0=ln[i][1][:], scalar=0.25, in1=ln[i][1][:],
                                         op0=ALU.mult, op1=ALU.mult)
                dve.tensor_scalar(ln[i][4][:], ln[i][2][:], 1.0 / D, LN_EPS, ALU.mult, ALU.add).then_inc(ln_sq[i], 1)
                dve.wait_ge(ln_sq[i], g + 1)
                dve.tensor_tensor(ln[i][5][:], ln[i][4][:], ln[i][3][:], ALU.add).then_inc(ln_var[i], 1)

            def shift(i, g):
                dve.wait_ge(ln_rstd[i], g + 1)
                dve.scalar_tensor_tensor(out=ln[i][7][:], in0=ln[i][0][:], scalar=-0.5, in1=ln[i][6][:],
                                         op0=ALU.mult, op1=ALU.mult).then_inc(ln_bias[i], 1)

            def tile_b(t):
                return t[:].unsqueeze(2).to_broadcast([P, TILES, E])

            def logits(g):
                dve.wait_ge(logit_mm, g + 1)
                dve.tensor_copy(lg[0][:], logit_ps[:, :, E:2 * E]).then_inc(lg_step[0], 1)
                dve.tensor_tensor(lg[2][:], tile_b(ln[1][0]), route_s[:, 0:E].unsqueeze(1).to_broadcast([P, TILES, E]), ALU.mult)
                dve.wait_ge(lg_step[0], g + 1)
                dve.tensor_tensor(lg[1][:], logit_ps[:, :, 0:E], lg[0][:], ALU.add).then_inc(lg_step[1], 1)
                dve.wait_ge(lg_step[1], g + 1)
                dve.scalar_tensor_tensor(out=lg[3][:], in0=lg[2][:], scalar=-0.5, in1=lg[1][:],
                                         op0=ALU.mult, op1=ALU.add).then_inc(lg_step[2], 1)
                dve.wait_ge(lg_step[2], g + 1)
                dve.wait_ge(ln_rstd[1], g + 1)
                dve.tensor_tensor(lg[4][:], lg[3][:], tile_b(ln[1][6]), ALU.mult).then_inc(lg_step[3], 1)
                dve.wait_ge(lg_step[3], g + 1)
                dve.tensor_tensor(lg[5][:], lg[4][:], route_s[:, E:2 * E].unsqueeze(1).to_broadcast([P, TILES, E]),
                                  ALU.add).then_inc(lg_step[4], 1)
                dve.wait_ge(lg_step[4], g + 1)
                dve.tensor_reduce(lmax[:], lg[5][:], AX_X, ALU.max).then_inc(lg_step[5], 1)
                dve.wait_ge(lg_step[5], g + 1)
                dve.tensor_tensor(lg[6][:], lg[5][:], tile_b(lmax), ALU.subtract).then_inc(lg_step[6], 1)

            def ranks(g):
                own = lg[5][:].unsqueeze(3).to_broadcast([P, TILES, E, E])
                other = lg[5][:].unsqueeze(2).to_broadcast([P, TILES, E, E])
                dve.tensor_tensor(ties[:], other, own, ALU.is_equal).then_inc(rank_step[0], 1)
                dve.tensor_tensor(beats[:], other, own, ALU.is_gt)
                dve.wait_ge(rank_step[0], g + 1)
                dve.tensor_tensor(ties[:].rearrange("p q e f -> p q (e f)"), ties[:].rearrange("p q e f -> p q (e f)"),
                                  lower.rearrange("p e f -> p (e f)").unsqueeze(1).to_broadcast([P, TILES, E * E]),
                                  ALU.mult).then_inc(rank_step[1], 1)
                dve.wait_ge(rank_step[1], g + 1)
                dve.tensor_tensor(beats[:], beats[:], ties[:], ALU.add).then_inc(rank_step[2], 1)
                dve.wait_ge(rank_step[2], g + 1)
                dve.tensor_reduce(rank[:], beats[:], AX_X, ALU.add).then_inc(rank_step[3], 1)

            def weights(g):
                dve.wait_ge(exp_set, g + 1)
                dve.tensor_reduce(esum[:], lg[7][:], AX_X, ALU.add).then_inc(lg_step[7], 1)
                dve.wait_ge(rank_step[3], g + 1)
                dve.scalar_tensor_tensor(out=lg[8][:], in0=rank[:], scalar=2.0, in1=lg[7][:], op0=ALU.is_lt, op1=ALU.mult)
                dve.wait_ge(lg_step[7], g + 1)
                dve.reciprocal(einv[:], esum[:]).then_inc(lg_step[8], 1)
                dve.wait_ge(lg_step[8], g + 1)
                dve.tensor_tensor(comb[:].rearrange("p e q -> p q e"), lg[8][:], tile_b(einv), ALU.mult).then_inc(comb_set, 1)

            def residual(p, parity):
                dve.wait_ge(fin_mm, p + 1)
                dve.tensor_tensor(r2[:], cb[:].rearrange("p (q c) -> p q c", q=TILES), x1[parity][:], ALU.add).then_inc(r2_set, 1)
                dve.wait_ge(r2_set, p + 1)
                statistics(2, r2, p)

            def body(p, parity):
                g = p + 1
                if chained(p):
                    dve.wait_ge(out_mm, g + 1)
                    if ffn(p):
                        dve.wait_ge(scale_set, g)
                    else:
                        dve.wait_ge(const_set, 4)
                    for i, bank in enumerate(halves):
                        part = slice(i * HALF, (i + 1) * HALF)
                        last = dve.tensor_tensor(ot[:, part, :], bank[:, 0:HALF * AUG].rearrange("p (b c) -> p b c", c=AUG),
                                                 scale[:, part].unsqueeze(2).to_broadcast([P, HALF, AUG]), ALU.mult)
                    last.then_inc(ot_set, 1)
                    if updated(p):
                        dve.tensor_tensor(ascale[:], group(decay, g), scale[:], ALU.mult).then_inc(ascale_set, 1)
                if ffn(p):
                    h_low(0, p)
                    h_low(1, p)
                if chained(p):
                    dve.wait_ge(th_set, g + 1)
                    dve.scalar_tensor_tensor(out=hid[:], in0=th[:], scalar=1.0, in1=ca[:], op0=ALU.add, op1=ALU.mult).then_inc(hid_set, 1)
                if ffn(p):
                    h_low(2, p)
                    h_low(3, p)
                if chained(p):
                    dve.wait_ge(hid_set, g + 1)
                    if updated(p):
                        dve.tensor_reduce(hsum[:], hid[:].rearrange("p (b c) -> p b c", c=CHUNK), AX_X, ALU.add).then_inc(hsum_set, 1)
                    dve.wait_ge(val_mm, g + 1)
                    dve.wait_ge(ox_set, g + 1)
                    dve.tensor_tensor(rt[:], cb[:], ox[:].rearrange("p b c -> p (b c)"), ALU.add).then_inc(rt_set, 1)
                if ffn(p):
                    weigh(0, p, parity)
                    h_low(4, p)
                    h_low(5, p)
                if chained(p):
                    if updated(p):
                        dve.wait_ge(err_mm, g + 1)
                        dve.scalar_tensor_tensor(out=err[:], in0=err_ps, scalar=1.0 / CHUNK, in1=ot[:, :, CHUNK],
                                                 op0=ALU.mult, op1=ALU.add).then_inc(err_set, 1)
                    dve.wait_ge(r_mm, g + 1)
                    statistics(0, ca[:].rearrange("p (q c) -> p q c", q=TILES), g)
                    if updated(p):
                        dve.wait_ge(errt_mm, g + 1)
                        dve.tensor_copy(errrow[:], errt_ps).then_inc(errrow_set, 1)
                if ffn(p):
                    h_low(6, p)
                    h_low(7, p)
                if chained(p):
                    shift(0, g)
                if ffn(p):
                    weigh(1, p, parity)
                if finished(p):
                    residual(p - 1, 1 - parity)
                if ffn(p):
                    h_low(8, p)
                    h_low(9, p)
                    weigh(2, p, parity)
                if finished(p):
                    shift(2, p - 1)
                if chained(p):
                    dve.wait_ge(x1t_hi_set, g + 1)
                    dve.tensor_tensor(x1t_lo[1 - parity][:], cb[:], x1t_hi[1 - parity][:].bitcast(F32), ALU.subtract).then_inc(x1t_lo_set, 1)
                    dve.wait_ge(x1_set, g + 1)
                    statistics(1, x1[1 - parity], g)
                if ffn(p):
                    weigh(3, p, parity)
                    h_low(10, p)
                    h_low(11, p)
                if chained(p):
                    logits(g)
                    if updated(p):
                        dve.wait_ge(upd_mm, g + 1)
                        dve.wait_ge(am_set, g + 1)
                        for i, bank in enumerate(halves):
                            part = slice(i * HALF, (i + 1) * HALF)
                            last = dve.tensor_tensor(mt[:, part, :], bank[:].rearrange("p (b c) -> p b c", c=D), am[:, part, :], ALU.add)
                        last.then_inc(mt_set, 1)
                    ranks(g)
                if ffn(p):
                    weigh(4, p, parity)
                    h_low(12, p)
                    h_low(13, p)
                if chained(p) and updated(p):
                    dve.wait_ge(msq_set, g + 1)
                    dve.tensor_reduce(mss[:], msq[:], AX_X, ALU.add).then_inc(mss_set, 1)
                if ffn(p):
                    weigh(5, p, parity)
                if chained(p):
                    weights(g)
                    if updated(p):
                        dve.wait_ge(ss_mm, g + 1)
                        dve.tensor_copy(nrm[0][:], ss_ps).then_inc(nrm_in, 1)
                if ffn(p):
                    h_low(14, p)
                    h_low(15, p)
                    weigh(6, p, parity)
                if chained(p):
                    dve.wait_ge(combt_mm, g + 1)
                    if finished(p):
                        dve.wait_ge(comb_out, g * 16)
                    elif ffn(p):
                        dve.wait_ge(comb_out, g * 16)
                    dve.tensor_copy(combt[:], combt_ps).then_inc(combt_set, 1)
                    if updated(p):
                        dve.wait_ge(nrm_root, g + 1)
                        dve.tensor_scalar(nrm[2][:], nrm[1][:], 1e-6, None, ALU.add).then_inc(nrm_add, 1)
                        dve.wait_ge(nrm_add, g + 1)
                        dve.reciprocal(nrm[3][:], nrm[2][:]).then_inc(nrm_inv, 1)
                        dve.wait_ge(nrm_inv, g + 1)
                        dve.wait_ge(ascale_set, g + 1)
                        dve.tensor_scalar(scale[:], nrm[3][:], MAX_NORM, 1.0, ALU.mult, ALU.min).then_inc(scale_set, 1)
                if ffn(p):
                    weigh(7, p, parity)

            groups_before_loop_and_after(dve, body)
            residual(G - 1, (G - 1) % 2)
            shift(2, G - 1)

        @block.tensor
        def _(pe):
            def outputs(g):
                if isinstance(g, int) and g == 0:
                    pe.wait_ge(m_in, 16)
                else:
                    pe.wait_ge(mt_set, g)
                for b in range(B):
                    dst = halves[b // HALF][:, (b % HALF) * AUG:(b % HALF + 1) * AUG]
                    last = pe.matmul(dst, mt[:, b, :], xgroup(g)[:, b, :], start=True, stop=True)
                last.then_inc(out_mm, 1)

            def hidden(g):
                pe.wait_ge(ot_set, g + 1)
                pe.matmul(ca[:], vw1[:], ot[:, :, 0:CHUNK], start=True, stop=True).then_inc(hid_mm, 1)

            def value(g):
                pe.wait_ge(hid_set, g + 1)
                pe.matmul(cb[:], vw2h[:], hid[:], start=True, stop=True).then_inc(val_mm, 1)

            def turn_r(g):
                pe.wait_ge(rt_set, g + 1)
                for q in range(TILES):
                    last = pe.transpose(ca[:, q * P:(q + 1) * P], rt[:, q * P:(q + 1) * P], ident)
                last.then_inc(r_mm, 1)

            def error(g):
                pe.wait_ge(hsum_set, g + 1)
                pe.matmul(err_ps, vw2h[:], hsum[:], start=True, stop=True).then_inc(err_mm, 1)

            def turn_error(g):
                pe.wait_ge(err_set, g + 1)
                pe.transpose(errt_ps, err[:], ident).then_inc(errt_mm, 1)

            def turn_x1(g, parity):
                pe.wait_ge(x1_set, g + 1)
                if finished(g - 1):
                    pe.wait_ge(r2_set, g - 1)
                for q in range(TILES):
                    last = pe.transpose(cb[:, q * P:(q + 1) * P], x1[parity][:, q, :], ident)
                last.then_inc(x1t_mm, 1)

            def route(g, parity):
                pe.wait_ge(x1t_lo_set, g + 1)
                if updated(g - 1):
                    pe.wait_ge(errrow_set, g + 1)
                for q in range(TILES):
                    part = slice(q * P, (q + 1) * P)
                    pe.matmul(logit_ps[:, q, :], x1t_hi[parity][:, part], route_r[:], start=True, stop=False)
                    last = pe.matmul(logit_ps[:, q, 0:E], x1t_lo[parity][:, part], route_r[:, 0:E], start=False, stop=True)
                last.then_inc(logit_mm, 1)

            def update(g):
                pe.wait_ge(errrow_set, g + 1)
                pe.wait_ge(kmask_set, g + 1)
                for b in range(B):
                    dst = halves[b // HALF][:, (b % HALF) * D:(b % HALF + 1) * D]
                    last = pe.matmul(dst, kmask[:, b, :], errrow[:], start=True, stop=True)
                last.then_inc(upd_mm, 1)

            def norm(g):
                pe.wait_ge(mss_set, g + 1)
                pe.matmul(ss_ps, ones, mss[:], start=True, stop=True).then_inc(ss_mm, 1)

            def turn_comb(g):
                pe.wait_ge(comb_set, g + 1)
                if updated(g - 1):
                    pe.wait_ge(nrm_in, g + 1)
                pe.transpose(combt_ps, comb[:].rearrange("p e q -> p (e q)"), ident).then_inc(combt_mm, 1)

            def finish(p, parity):
                pe.wait_ge(y_added[E - 1], p + 1)
                for q in range(TILES):
                    last = pe.transpose(cb[:, q * P:(q + 1) * P], acc[parity][:, q * P:(q + 1) * P], ident)
                last.then_inc(fin_mm, 1)

            def first(e, p, parity):
                if isinstance(p, int) and p == 0:
                    pe.wait_ge(w1_lo_set, e + 1)
                for k in range(FB):
                    n = FB * e + k
                    part = slice(k * P, (k + 1) * P)
                    wait_earlier_block(pe, h_full_set, n, H_BANKS, p)
                    pe.matmul(hp[n % H_BANKS][:], w1_hi[:, e, part], x1t_hi[parity][:], start=True, stop=False)
                    pe.matmul(hp[n % H_BANKS][:], w1_lo[:, e, part], x1t_hi[parity][:], start=False, stop=False)
                    pe.matmul(hp[n % H_BANKS][:], w1_hi[:, e, part], x1t_lo[parity][:], start=False, stop=True).then_inc(w1_mm[n // FB], 1)

            def second(e, p):
                if isinstance(p, int) and p == 0:
                    pe.wait_ge(w2_lo_set, e + 1)
                m, same = earlier(e, Y_BANKS, E)
                if same:
                    pe.wait_ge(y_weighted[m], p + 1)
                elif not (isinstance(p, int) and p == 0):
                    pe.wait_ge(y_weighted[m], p)
                for k in range(FB):
                    n = FB * e + k
                    pe.wait_ge(h_full_set[n // FB], of_block(n, p))
                    pe.matmul(yp[e % Y_BANKS][:], w2_hi[:, e, k, :], h_hi[:, n % H_RING, :], start=(k == 0), stop=False)
                    pe.matmul(yp[e % Y_BANKS][:], w2_lo[:, e, k, :], h_hi[:, n % H_RING, :], start=False, stop=False)
                for k in range(FB):
                    n = FB * e + k
                    pe.wait_ge(h_lo_set[n // FB], of_block(n, p))
                    last = pe.matmul(yp[e % Y_BANKS][:], w2_hi[:, e, k, :], h_lo[:, n % H_RING, :], start=False, stop=(k == FB - 1))
                last.then_inc(w2_mm[e], 1)

            pe.wait_ge(par_set, 7)
            pe.matmul(route_ps, ones, route_w[:], start=True, stop=True).then_inc(route_mm, 1)
            for i in range(STAT_STEPS):
                pe.wait_ge(kdw_set, i + 1)
                if i >= 2:
                    pe.wait_ge(km_set, i - 1)
                for t in range(STAT_TILES):
                    tile = i * STAT_TILES + t
                    last = pe.matmul(kd_ps[i % 2][:, t, :], xtok[:, tile, :], kdw[:, tile, :], start=True, stop=True)
                last.then_inc(kd_mm, 1)
            pe.wait_ge(xt_in, 16)
            pe.wait_ge(vg_in, 32)
            for c in range(G * B):
                t, b = divmod(c, B)
                last = pe.matmul(lr_ps[:, c, :], xt[:, t, b, 0:CHUNK], prm[:, C_ETA_W:C_ETA_W + 2], start=True, stop=True)
            last.then_inc(lr_mm, 1)
            pe.wait_ge(km_set, STAT_STEPS)
            pe.matmul(gate_ps, gate_rep[:], km[:], start=True, stop=True).then_inc(gate_mm, 1)
            pe.wait_ge(lr_tanh, 2)
            pe.matmul(mean_ps, ones[0:CHUNK, :], lr_th[:].rearrange("p w c -> p (w c)"), start=True, stop=True).then_inc(lr_mean, 1)
            pe.wait_ge(coef_set, 1)
            for t in range(G):
                bank = halves[t // (G // 2)]
                last = pe.transpose(bank[0:B, (t % (G // 2)) * P:(t % (G // 2) + 1) * P], kb[:, t * B:(t + 1) * B], ident)
            last.then_inc(kb_mm, 1)
            pe.wait_ge(kb_set, 1)
            outputs(0)

            def body(p, parity):
                g = p + 1
                f, c = ffn(p), chained(p)
                u = c and updated(p)
                if f:
                    first(0, p, parity)
                    first(1, p, parity)
                if c:
                    hidden(g)
                if f:
                    second(0, p)
                    first(2, p, parity)
                if c:
                    value(g)
                if f:
                    second(1, p)
                if c:
                    if u:
                        error(g)
                    turn_r(g)
                if f:
                    first(3, p, parity)
                if u:
                    turn_error(g)
                if f:
                    second(2, p)
                if finished(p):
                    finish(p - 1, 1 - parity)
                if f:
                    first(4, p, parity)
                    second(3, p)
                if c:
                    turn_x1(g, 1 - parity)
                if f:
                    first(5, p, parity)
                if c:
                    route(g, 1 - parity)
                if f:
                    second(4, p)
                if u:
                    update(g)
                if f:
                    first(6, p, parity)
                    second(5, p)
                    first(7, p, parity)
                if u:
                    norm(g)
                if f:
                    second(6, p)
                if u:
                    outputs(g + 1)
                if f:
                    second(7, p)
                if c:
                    turn_comb(g)

            groups_before_loop_and_after(pe, body)
            finish(G - 1, (G - 1) % 2)


def pack(x, m_init, eta_w, eta_b, alpha_w, alpha_b, gate_w, gate_b, vg_w1, vg_w2, gamma, beta, route_w, w1, w2):
    xs = x.reshape(TILES, 2, G, CHUNK, D)
    x_tok = xs.transpose(1, 3, 2, 0, 4).reshape(P, ALL_TILES, D)
    x_chan = np.zeros((P, G, B, AUG), x.dtype)
    x_chan[..., :CHUNK] = x.reshape(B, G, CHUNK, D).transpose(3, 1, 0, 2)
    params = np.zeros((P, C_PARAMS), x.dtype)
    for column, values in ((C_GAMMA, gamma), (C_BETA, beta), (C_ETA_W, eta_w), (C_ALPHA_W, alpha_w), (C_GATE_W, gate_w),
                           (C_ETA_B, eta_b), (C_ALPHA_B, alpha_b), (C_GATE_B, gate_b)):
        params[:, column] = values
    params[:, C_ROUTE:] = route_w.T
    consts = np.zeros((P, K_CONSTS), np.float32)
    consts[:, K_IDENT:K_IDENT + P] = np.eye(P)
    consts[:, K_ONES:K_ONES + P] = 1
    consts[:CHUNK, K_HALVES] = consts[CHUNK:, K_HALVES + 1] = 1 / CHUNK
    consts[:, K_LOWER:] = np.tril(np.ones((E, E)), -1).ravel()
    return {
        "x_tok": x_tok, "x_chan": x_chan, "m_init_t": m_init.T, "vg_w1t": vg_w1.T, "vg_w2t": vg_w2.T,
        "w1t": w1.transpose(2, 0, 1), "w2t": w2.reshape(E, D, FB, P).transpose(3, 0, 2, 1),
        "params": params, "consts": consts,
    }


def kernel(L0_attn_x, L0_attn_M_init, L0_attn_eta_w, L0_attn_eta_b, L0_attn_alpha_w, L0_attn_alpha_b, L0_attn_gate_w,
           L0_attn_gate_b, L0_attn_vg_w1, L0_attn_vg_w2, L0_ffn_ln_gamma, L0_ffn_ln_beta, L0_ffn_gate_w, L0_ffn_w1, L0_ffn_w2):
    from concourse.bacc import Bacc
    from concourse.bass_utils import run_bass_kernel_spmd

    given = [L0_attn_x, L0_attn_M_init, L0_attn_eta_w, L0_attn_eta_b, L0_attn_alpha_w, L0_attn_alpha_b, L0_attn_gate_w,
             L0_attn_gate_b, L0_attn_vg_w1, L0_attn_vg_w2, L0_ffn_ln_gamma, L0_ffn_ln_beta, L0_ffn_gate_w, L0_ffn_w1, L0_ffn_w2]
    arrays = {f"in_{n}": np.ascontiguousarray(a) for n, a in pack(*(np.asarray(a) for a in given)).items()}
    nc = Bacc("TRN2", target_bir_lowering=False, num_devices=1)
    ins = [nc.dram_tensor(n, a.shape, mybir.dt.from_np(a.dtype), kind="ExternalInput").ap() for n, a in arrays.items()]
    out = nc.dram_tensor("out_dev", (G, P, TILES * D), F32, kind="ExternalOutput").ap()
    build(nc, *ins, out)
    got = run_bass_kernel_spmd(nc, [arrays], core_ids=[0]).results[0]["out_dev"]
    return got.reshape(G, 2, CHUNK, TILES, D).transpose(3, 1, 0, 2, 4).reshape(B, S, D)
```

```python
from contextlib import ExitStack

import numpy as np

import concourse.bass as bass
from concourse import mybir

F32 = mybir.dt.float32
F32R = mybir.dt.float32r
ALU = mybir.AluOpType
ACT = mybir.ActivationFunctionType
AX_X = mybir.AxisListType.X

P = 128
B, S, D = 8, 512, 128
CHUNK = 64
G = S // CHUNK
TOK = B * CHUNK
TILES = TOK // P
ALL_TILES = G * TILES
AUG = CHUNK + 1
HALF = B // 2
E = 8
F = 256
FB = F // P
BLOCKS = E * FB
H_BANKS = 3
H_RING = 6
FULL_RING = 6
Y_BANKS = 2
YM_RING = 3
COMB_PARTS = 4
COMB_E = E // COMB_PARTS
STAT_G = 2
STAT_TILES = STAT_G * TILES
STAT_STEPS = G // STAT_G
STAT_C = STAT_G * B
ROWS = 3 * B
MAX_LR, MIN_DECAY, MAX_NORM, NORM_EPS, LN_EPS = 0.2, 0.5, 30.0, 1e-5, 1e-5

NORM_IN, NORM_ROOT, NORM_MULT, NORM_ADD, NORM_INV, NORM_MIN, SCALE = range(7)
NORM_STEPS = 7
L_BETA, L_SUM, L_MEAN, L_RSTD, L_LOGIT, L_MAX, L_CENTRED, L_DOWN, L_INV, L_RATIO, L_EXP, L_ESUM, L_EINV = range(13)
LOGIT_STEPS = 13
R_TIES, R_LOWER, R_BEATS, R_RANK = range(4)
RANK_STEPS = 4

C_GAMMA, C_BETA, C_ETA_W, C_ALPHA_W, C_GATE_W, C_ETA_B, C_ALPHA_B, C_GATE_B, C_ROUTE = range(9)
C_PARAMS = C_ROUTE + E
K_IDENT, K_ONES, K_HALVES, K_LOWER = 0, P, 2 * P, 2 * P + 2
K_BATCH = K_LOWER + E * E
K_CONSTS = K_BATCH + B


def build(nc, x_tok, x_chan, m_init_t, vg_w1t, vg_w2t, w1t, w2t, params, consts, out):
    with ExitStack() as ctx:
        def sb(name, shape, dt=F32):
            return ctx.enter_context(nc.sbuf_tensor(name, shape, dt))

        def sem(name):
            return ctx.enter_context(nc.semaphore(name))

        def sems(name, n):
            return [sem(f"{name}{i}") for i in range(n)]

        def pairs(name, n):
            return sems(name, (n + 1) // 2)

        hp = [ctx.enter_context(nc.psum_tensor(f"hp{i}", [P, TOK], F32)) for i in range(H_BANKS)]
        yp = [ctx.enter_context(nc.psum_tensor(f"yp{i}", [P, TOK], F32)) for i in range(Y_BANKS)]
        ca = ctx.enter_context(nc.psum_tensor("ca", [P, TOK], F32))
        cb = ctx.enter_context(nc.psum_tensor("cb", [P, TOK], F32))
        small = ctx.enter_context(nc.psum_tensor("small", [P, TOK], F32))
        err_ps = small[:, 0:B]
        errt_ps = small[0:ROWS, 8:8 + P]
        ss_ps = small[:, 136:136 + B]
        logit_ps = small[:, 144:144 + TILES * 2 * E].rearrange("p (q e) -> p q e", q=TILES)
        combt_ps = small[0:E * TILES, 208:208 + P]
        kd_ps = yp[0][:, 0:STAT_TILES * 4].rearrange("p (t w) -> p t w", w=4)
        lr_ps = yp[1][0:CHUNK, 0:STAT_C * 2].rearrange("p (c w) -> p c w", w=2)
        mean_ps = hp[0][:, 0:2 * STAT_C].rearrange("p (w c) -> p w c", w=2)
        gate_ps = hp[1][:, 0:STAT_C]
        krow_ps = hp[2][0:ROWS, 0:STAT_G * P]
        route_ps = small[:, 0:2 * E]
        halves = [ca, cb]

        xtok = sb("xtok", [P, ALL_TILES, D])
        xt = sb("xt", [P, G, B, AUG])
        prm = sb("prm", [P, C_PARAMS])
        cst = sb("cst", [P, K_CONSTS])
        vw1 = sb("vw1", [P, D])
        vw2 = sb("vw2", [P, D])
        vw2h = sb("vw2h", [P, D])
        combb = [sb(f"combb{i}", [P, E, TOK]) for i in range(2)]
        raw = combb[1][:].rearrange("p e t -> p (e t)")
        w1 = raw[:, 0:E * F].rearrange("p (e f) -> p e f", e=E)
        w2 = raw[:, E * F:2 * E * F].rearrange("p (e k c) -> p e k c", e=E, k=FB)
        w1_hi, w1_lo = sb("w1_hi", [P, E, F], F32R), sb("w1_lo", [P, E, F], F32R)
        w2_hi, w2_lo = sb("w2_hi", [P, E, FB, D], F32R), sb("w2_lo", [P, E, FB, D], F32R)
        ident = cst[:, K_IDENT:K_IDENT + P]
        ones = cst[:, K_ONES:K_ONES + P]
        half64 = cst[:, K_HALVES:K_HALVES + 2]
        lower = cst[:, K_LOWER:K_LOWER + E * E]
        own_batch = cst[0:ROWS, K_BATCH:K_BATCH + B]

        sq = sb("sq", [P, STAT_TILES, D])
        ssq = sb("ssq", [P, ALL_TILES])
        inv = sb("inv", [P, ALL_TILES])
        kdw = sb("kdw", [P, ALL_TILES, 4])
        km = sb("km", [P, G * B])
        kb = sb("kb", [P, G, 3, B], F32R)
        krow = sb("krow", [ROWS, G, P], F32R)
        lr_th = sb("lr_th", [CHUNK, 2, STAT_C])
        lr_bias = sb("lr_bias", [P, 3])
        eta = sb("eta", [P, G * B])
        alpha = sb("alpha", [P, G * B])
        gate = sb("gate", [P, G * B])
        gate_rep = sb("gate_rep", [P, P])
        decay = sb("decay", [P, G * B])
        lrate = sb("lrate", [P, G * B])
        c_half = sb("c_half", [P, ALL_TILES])
        c_root = sb("c_root", [P, B])
        c_one = sb("c_one", [ROWS, P])

        m0 = sb("m0", [P, D])
        mt = sb("mt", [P, B, D])
        msq = sb("msq", [P, B, D])
        mss = sb("mss", [P, B])
        scale = sb("scale", [P, B])
        scale_d = sb("scale_d", [P, B])
        scale_i = sb("scale_i", [P, B])
        err_scale = sb("err_scale", [P, B])
        nrm = [sb(f"nrm{i}", [P, B]) for i in range(6)]
        ot = sb("ot", [P, B, AUG])
        ox = sb("ox", [P, B, CHUNK])
        th = sb("th", [P, TOK])
        hid = sb("hid", [P, TOK])
        hsum = sb("hsum", [P, B])
        err = sb("err", [P, B])
        err_f = sb("err_f", [P, B])
        err_r = sb("err_r", [P, 3, B], F32R)
        err_row = sb("err_row", [ROWS, B, P], F32R)
        kcur = sb("kcur", [ROWS, P], F32R)
        rt = sb("rt", [P, TOK])

        st = [sb(f"st{i}", [P, TILES, 6]) for i in range(3)]
        ln = [[sb(f"ln{i}_{j}", [P, TILES]) for j in range(9)] for i in range(3)]
        x1 = [sb(f"x1_{i}", [P, TILES, D]) for i in range(2)]
        x1t_hi = [sb(f"x1t_hi{i}", [P, TOK], F32R) for i in range(2)]
        x1t_lo = [sb(f"x1t_lo{i}", [P, TOK], F32R) for i in range(2)]
        route_w = sb("route_w", [P, 2 * E])
        route_r = sb("route_r", [P, 2 * E], F32R)
        route_s = sb("route_s", [P, 2 * E])
        lg = [sb(f"lg{i}", [P, TILES, E]) for i in range(13)]
        lmax = sb("lmax", [P, TILES])
        esum = sb("esum", [P, TILES])
        einv = sb("einv", [P, TILES])
        beats = sb("beats", [P, TILES, E, E])
        ties = sb("ties", [P, TILES, E, E])
        rank = sb("rank", [P, TILES, E])
        x1_junk = sb("x1_junk", [P, TILES, D])
        x1sum, x1sq = sb("x1sum", [P, TILES]), sb("x1sq", [P, TILES])
        comb = sb("comb", [P, E, TILES])
        combt = sb("combt", [E * TILES, P])
        comb_dram = nc.dram_tensor("comb_dram", [2, E * TILES, P], F32).ap()

        h_full = sb("h_full", [P, FULL_RING, TOK])
        h_hi = sb("h_hi", [P, H_RING, TOK], F32R)
        h_lo = sb("h_lo", [P, H_RING, TOK], F32R)
        ym = sb("ym", [P, YM_RING, TOK])
        acc = [sb(f"acc{i}", [P, TOK]) for i in range(2)]
        r2 = sb("r2", [P, TILES, D])

        def result(g):
            return xtok[:, g * TILES:(g + 1) * TILES, :] if isinstance(g, int) else xtok[:, bass.ds(g * TILES, TILES), :]

        x_in, xt_in = sems("x_in", STAT_STEPS), sems("xt_in", STAT_STEPS)
        m_in, par_in, vg_in = sem("m_in"), sem("par_in"), sem("vg_in")
        w1_in, w2_in = sems("w1_in", 2), sems("w2_in", 2)
        const_set, par_set, route_mm = sem("const_set"), sem("par_set"), sem("route_mm")
        sq_set, ssq_sum, ssq_set, inv_set, kd_half, kdw_set, kd_mm, km_copy, km_set, k_hi, kb_set, krow_mm, krow_set = (sem(n) for n in (
            "sq_set", "ssq_sum", "ssq_set", "inv_set", "kd_half", "kdw_set", "kd_mm", "km_copy", "km_set", "k_hi", "kb_set", "krow_mm", "krow_set"))
        lr_mm, lr_tanh, lr_mean, gate_mm, gate_tanh, coef_in, coef_mult, coef_set = (sem(n) for n in (
            "lr_mm", "lr_tanh", "lr_mean", "gate_mm", "gate_tanh", "coef_in", "coef_mult", "coef_set"))
        w1_hi_set, w1_lo_set, w2_hi_set, w2_lo_set = (sem(n) for n in ("w1_hi_set", "w1_lo_set", "w2_hi_set", "w2_lo_set"))
        out_mm, ot_set, ox_set, hid_mm, th_set, hid_set, hsum_set, val_mm, rt_set, r_mm = (sem(n) for n in (
            "out_mm", "ot_set", "ox_set", "hid_mm", "th_set", "hid_set", "hsum_set", "val_mm", "rt_set", "r_mm"))
        err_mm, err_sum, err_hi, err_set, errt_mm, err_row_set, kcur_set, upd_mm, mt_set, msq_set, ss_mm = (sem(n) for n in (
            "err_mm", "err_sum", "err_hi", "err_set", "errt_mm", "err_row_set", "kcur_set", "upd_mm", "mt_set", "msq_set", "ss_mm"))
        norm_step = pairs("norm_step", NORM_STEPS)
        sd_set, si_set, es_set = sem("sd_set"), sem("si_set"), sem("es_set")
        ln_step, ln_sq, ln_var, ln_rstd, ln_bias = (sems(n, 3) for n in ("ln_step", "ln_sq", "ln_var", "ln_rstd", "ln_bias"))
        x1_set, x1sq_set, x1t_mm, x1t_hi_set, x1t_lo_set, logit_mm = (sem(n) for n in (
            "x1_set", "x1sq_set", "x1t_mm", "x1t_hi_set", "x1t_lo_set", "logit_mm"))
        logit_step = pairs("logit_step", LOGIT_STEPS)
        rank_step = pairs("rank_step", RANK_STEPS)
        exp_tanh, comb_set, combt_mm, combt_set, comb_out = (sem(n) for n in ("exp_tanh", "comb_set", "combt_mm", "combt_set", "comb_out"))
        comb_in = sems("comb_in", COMB_PARTS)
        w1_mm = sems("w1_mm", E)
        h_full_set = sems("h_full_set", E)
        h_lo_set = sems("h_lo_set", E)
        w2_mm = pairs("w2_mm", E)
        y_weighted = pairs("y_weighted", E)
        y_added = pairs("y_added", E - 1)
        fin_mm, r2_set, osb_set = sem("fin_mm"), sem("r2_set"), sem("osb_set")
        stored = sem("stored")

        def earlier(n, ring, count):
            if n >= ring:
                return n - ring, True
            return max(m for m in range(count) if m % ring == n % ring), False

        def wait_event(eng, pair_sems, k, n, g):
            eng.wait_ge(pair_sems[k // 2], g * min(2, n - k // 2 * 2) + (k % 2 + 1))

        def of_block(n, p):
            return p * FB + (n % FB + 1)

        def wait_earlier_block(eng, sem_list, n, ring, p):
            m, same = earlier(n, ring, BLOCKS)
            if same:
                eng.wait_ge(sem_list[m // FB], of_block(m, p))
            elif not (isinstance(p, int) and p == 0):
                eng.wait_ge(sem_list[m // FB], of_block(m, p - 1))

        def groups_before_loop_and_after(eng, body):
            body(-1, 1)
            body(0, 0)
            with eng.Fori(0, 2) as pair:
                for j in range(2):
                    body(pair * 2 + (1 + j), 1 - j)
            for p in range(5, G):
                body(p, p % 2)

        def chained(p):
            return not isinstance(p, int) or p + 1 < G

        def updated(p):
            return not isinstance(p, int) or p + 2 < G

        def ffn(p):
            return not isinstance(p, int) or p >= 0

        def finished(p):
            return not isinstance(p, int) or p >= 1

        def group(t, g):
            return t[:, bass.ds(g * B, B)] if not isinstance(g, int) else t[:, g * B:(g + 1) * B]

        def xgroup(g):
            return xt[:, g] if isinstance(g, int) else xt[:, bass.ds(g, 1)].rearrange("p o b c -> p (o b) c")

        def kpart(i):
            return slice(i * STAT_C, (i + 1) * STAT_C)

        block = ctx.enter_context(nc.Block())

        @block.sync
        def _(sp):
            sp.dma_start(prm[:], params).then_inc(par_in, 16)
            for i in range(STAT_STEPS):
                part, groups = slice(i * STAT_TILES, (i + 1) * STAT_TILES), slice(i * STAT_G, (i + 1) * STAT_G)
                sp.dma_start(xtok[:, part, :], x_tok[:, part, :]).then_inc(x_in[i], 16)
                if i == 0:
                    sp.dma_start(cst[:], consts).then_inc(par_in, 16)
                sp.dma_start(xt[:, groups], x_chan[:, groups]).then_inc(xt_in[i], 16)
                if i >= 2:
                    half = slice((i - 2) * E // 2, (i - 1) * E // 2)
                    sp.dma_start(w1[:, half], w1t[:, half]).then_inc(w1_in[i - 2], 16)
            for i in range(2):
                half = slice(i * E // 2, (i + 1) * E // 2)
                sp.dma_start(w2[:, half], w2t[:, half]).then_inc(w2_in[i], 16)

            def body(p, parity):
                if ffn(p):
                    sp.wait_ge(combt_set, p + 1)
                    sp.dma_start(comb_dram[parity], combt[:]).then_inc(comb_out, 16)
                    if not isinstance(p, int) or p >= 2:
                        wait_event(sp, y_weighted, E - 1, E, p - 2)
                    if isinstance(p, int) and p == 1:
                        sp.wait_ge(w1_lo_set, E)
                        sp.wait_ge(w2_lo_set, E)
                    sp.wait_ge(comb_out, p * 16 + 16)
                    for c in range(COMB_PARTS):
                        part = slice(c * COMB_E, (c + 1) * COMB_E)
                        src = comb_dram[parity, c * COMB_E * TILES:(c + 1) * COMB_E * TILES, :].rearrange("(o q) t -> o (q t)", o=1)
                        sp.dma_start(combb[parity][:, part, :].rearrange("p e t -> p (e t)"),
                                     src.to_broadcast([P, COMB_E * TOK])).then_inc(comb_in[c], 16)
                if finished(p):
                    sp.wait_ge(osb_set, p)
                    row = out[p - 1] if isinstance(p, int) else out[bass.ds(p - 1, 1)].rearrange("o p c -> (o p) c")
                    sp.dma_start(row, result(p - 1).rearrange("p q c -> p (q c)")).then_inc(stored, 16)

            groups_before_loop_and_after(sp, body)
            sp.wait_ge(osb_set, G)
            sp.dma_start(out[G - 1], result(G - 1).rearrange("p q c -> p (q c)")).then_inc(stored, 16)
            sp.wait_ge(stored, 16 * G)

        @block.gpsimd
        def _(pool):
            pool.memset(c_half[:], -0.5).then_inc(const_set, 1)
            pool.memset(c_root[:], 0.5).then_inc(const_set, 1)
            pool.memset(c_one[:], 1.0).then_inc(const_set, 1)
            pool.memset(scale[:], 1.0).then_inc(const_set, 1)
            pool.wait_ge(const_set, 4)

            def token_norms(i):
                part = slice(i * STAT_TILES, (i + 1) * STAT_TILES)
                pool.wait_ge(ssq_set, i + 1)
                pool.tensor_tensor(inv[:, part], ssq[:, part], c_half[:, part], ALU.pow).then_inc(inv_set, 1)

            def split_w1(experts):
                for e in experts:
                    pool.wait_ge(w1_hi_set, e + 1)
                    pool.tensor_tensor(w1_lo[:, e, :], w1[:, e, :], w1_hi[:, e, :].bitcast(F32), ALU.subtract).then_inc(w1_lo_set, 1)

            def power(i, g):
                pool.wait_ge(ln_var[i], g + 1)
                pool.tensor_tensor(ln[i][6][:], ln[i][5][:], c_half[:, 0:TILES], ALU.pow).then_inc(ln_rstd[i], 1)

            def y_add(e, p, parity):
                wait_event(pool, y_weighted, e, E, p)
                if e > 1:
                    wait_event(pool, y_added, e - 2, E - 1, p)
                pool.tensor_tensor(acc[parity][:], acc[parity][:], ym[:, (e - 1) % YM_RING, :], ALU.add).then_inc(y_added[(e - 1) // 2], 1)

            def h_low(n, p):
                pool.wait_ge(h_full_set[n // FB], of_block(n, p))
                pool.tensor_tensor(h_lo[:, n % H_RING, :], h_full[:, n % FULL_RING, :],
                                   h_hi[:, n % H_RING, :].bitcast(F32), ALU.subtract).then_inc(h_lo_set[n // FB], 1)

            token_norms(0)

            def add_inputs(g):
                pool.wait_ge(ot_set, g + 1)
                pool.tensor_tensor(ox[:], ot[:, :, 0:CHUNK], xgroup(g)[:, :, 0:CHUNK], ALU.add).then_inc(ox_set, 1)

            def k_rows(g):
                pool.wait_ge(krow_set, g // STAT_G + 1 if isinstance(g, int) else STAT_STEPS)
                src = krow[:, g, :] if isinstance(g, int) else krow[:, bass.ds(g, 1), :].rearrange("p o c -> p (o c)")
                pool.tensor_tensor(kcur[:], src.bitcast(F32), c_one[:], ALU.mult).then_inc(kcur_set, 1)

            def norm_root(g):
                wait_event(pool, norm_step, NORM_IN, NORM_STEPS, g)
                pool.tensor_tensor(nrm[1][:], nrm[0][:], c_root[:], ALU.pow).then_inc(norm_step[NORM_ROOT // 2], 1)

            def lower_ties(g):
                wait_event(pool, rank_step, R_TIES, RANK_STEPS, g)
                pool.tensor_tensor(ties[:].rearrange("p q e f -> p q (e f)"), ties[:].rearrange("p q e f -> p q (e f)"),
                                   lower.unsqueeze(1).to_broadcast([P, TILES, E * E]), ALU.mult).then_inc(rank_step[R_LOWER // 2], 1)

            def ahead(g):
                wait_event(pool, rank_step, R_LOWER, RANK_STEPS, g)
                pool.tensor_tensor(beats[:].rearrange("p q e f -> p (q e f)"), beats[:].rearrange("p q e f -> p (q e f)"),
                                   ties[:].rearrange("p q e f -> p (q e f)"), ALU.add).then_inc(rank_step[R_BEATS // 2], 1)

            def body(p, parity):
                g = p + 1
                f, fin, c, u, start = ffn(p), finished(p), chained(p), chained(p) and updated(p), not ffn(p)
                if f:
                    h_low(2, p)
                if c:
                    add_inputs(g)
                if start:
                    token_norms(1)
                if u:
                    k_rows(g)
                if fin:
                    y_add(7, p - 1, 1 - parity)
                if f:
                    h_low(4, p)
                    h_low(6, p)
                if c:
                    power(0, g)
                if start:
                    token_norms(2)
                if f:
                    y_add(1, p, parity)
                    h_low(8, p)
                    y_add(2, p, parity)
                if start:
                    token_norms(3)
                    split_w1(range(4))
                if f:
                    h_low(10, p)
                    y_add(3, p, parity)
                    h_low(12, p)
                    y_add(4, p, parity)
                if fin:
                    power(2, p - 1)
                if u:
                    norm_root(g)
                if c:
                    power(1, g)
                if f:
                    y_add(5, p, parity)
                if c:
                    lower_ties(g)
                    ahead(g)
                if f:
                    y_add(6, p, parity)
                if start:
                    split_w1(range(4, E))

            groups_before_loop_and_after(pool, body)
            y_add(7, G - 1, (G - 1) % 2)
            power(2, G - 1)

        @block.scalar
        def _(act):
            act.dma_start(m0[:], m_init_t).then_inc(m_in, 16)
            act.dma_start(vw1[:], vg_w1t).then_inc(vg_in, 16)
            act.dma_start(vw2[:], vg_w2t).then_inc(vg_in, 16)

            def squares(i):
                act.wait_ge(x_in[i], 16)
                if i:
                    act.wait_ge(ssq_sum, i)
                act.activation(sq[:], xtok[:, i * STAT_TILES:(i + 1) * STAT_TILES, :], ACT.Square).then_inc(sq_set, 1)

            def rates(i):
                act.wait_ge(lr_mm, i + 1)
                act.wait_ge(par_set, 1)
                if i:
                    act.wait_ge(lr_mean, i)
                for w in range(2):
                    last = act.activation(lr_th[:, w, :], lr_ps[:, :, w], ACT.Tanh, scale=0.5, bias=lr_bias[0:CHUNK, w:w + 1])
                last.then_inc(lr_tanh, 1)
                act.wait_ge(gate_mm, i + 1)
                act.activation(gate[:, kpart(i)], gate_ps, ACT.Tanh, scale=0.5, bias=lr_bias[:, 2:3]).then_inc(gate_tanh, 1)

            def split_w1(experts):
                for e in experts:
                    act.wait_ge(w1_in[e // (E // 2)], 16)
                    act.activation(w1_hi[:, e, :], w1[:, e, :], ACT.Copy).then_inc(w1_hi_set, 1)

            def split_w2(experts):
                for e in experts:
                    act.wait_ge(w2_in[e // (E // 2)], 16)
                    act.activation(w2_hi[:, e], w2[:, e], ACT.Copy).then_inc(w2_hi_set, 1)

            def gelus(n, p):
                act.wait_ge(w1_mm[n // FB], of_block(n, p))
                m, same = earlier(n, H_RING, BLOCKS)
                if same:
                    wait_event(act, w2_mm, m // FB, E, p)
                elif not (isinstance(p, int) and p == 0):
                    wait_event(act, w2_mm, m // FB, E, p - 1)
                act.activation(h_hi[:, n % H_RING, :], hp[n % H_BANKS][:], ACT.Gelu)
                m, same = earlier(n, FULL_RING, BLOCKS)
                if same:
                    act.wait_ge(h_lo_set[m // FB], of_block(FB - 1, p))
                elif not (isinstance(p, int) and p == 0):
                    act.wait_ge(h_lo_set[m // FB], of_block(FB - 1, p - 1))
                act.activation(h_full[:, n % FULL_RING, :], hp[n % H_BANKS][:], ACT.Gelu).then_inc(h_full_set[n // FB], 1)

            def normalise(i, src, dst, done, g, sums=None):
                act.wait_ge(ln_bias[i], g + 1)
                for q in range(TILES):
                    extra = {} if sums is None else {"accum_out": sums[:, q:q + 1]}
                    last = act.activation(dst[:, q, :], src[:, q, :], ACT.Identity,
                                          scale=ln[i][6][:, q:q + 1], bias=ln[i][7][:, q:q + 1], **extra)
                last.then_inc(done, 1)

            def norm_squares(batches, g):
                act.wait_ge(mt_set, g + 1)
                for b in batches:
                    last = act.activation(msq[:, b, :], mt[:, b, :], ACT.Square, accum_out=mss[:, b:b + 1])
                last.then_inc(msq_set, 1)

            squares(0)
            rates(0)

            def half_tanh(g):
                act.wait_ge(hid_mm, g + 1)
                act.activation(th[:], ca[:], ACT.Tanh, scale=0.5).then_inc(th_set, 1)

            def first_norm(g, parity):
                if finished(g - 1):
                    act.wait_ge(r2_set, g - 1)
                normalise(0, ca[:].rearrange("p (q c) -> p q c", q=TILES), x1[parity], x1_set, g, x1sum)

            def x1_square_sums(g, parity):
                act.wait_ge(x1_set, g + 1)
                for q in range(TILES):
                    last = act.activation(x1_junk[:, q, :], x1[parity][:, q, :], ACT.Square, accum_out=x1sq[:, q:q + 1])
                last.then_inc(x1sq_set, 1)

            def x1_high(g, parity):
                act.wait_ge(x1t_mm, g + 1)
                act.activation(x1t_hi[parity][:], cb[:], ACT.Copy).then_inc(x1t_hi_set, 1)

            def exp_tanhs(g):
                wait_event(act, logit_step, L_CENTRED, LOGIT_STEPS, g)
                act.activation(lg[7][:], lg[6][:], ACT.Tanh, scale=0.25).then_inc(exp_tanh, 1)

            def body(p, parity):
                g = p + 1
                f, fin, c, u, start = ffn(p), finished(p), chained(p), chained(p) and updated(p), not ffn(p)
                if f:
                    gelus(0, p)
                    gelus(1, p)
                    gelus(2, p)
                    gelus(3, p)
                    gelus(4, p)
                if start:
                    squares(1)
                if c:
                    half_tanh(g)
                if start:
                    rates(1)
                    squares(2)
                if f:
                    gelus(5, p)
                    gelus(6, p)
                    gelus(7, p)
                    gelus(8, p)
                    gelus(9, p)
                if c:
                    first_norm(g, 1 - parity)
                if start:
                    rates(2)
                    squares(3)
                    split_w1(range(4))
                if f:
                    gelus(10, p)
                    gelus(11, p)
                    gelus(12, p)
                if u:
                    norm_squares(range(HALF), g)
                    norm_squares(range(HALF, B), g)
                if start:
                    rates(3)
                if c:
                    x1_high(g, 1 - parity)
                if f:
                    gelus(13, p)
                if c:
                    x1_square_sums(g, 1 - parity)
                if f:
                    gelus(14, p)
                    gelus(15, p)
                if fin:
                    normalise(2, r2, result(p - 1), osb_set, p - 1)
                if start:
                    split_w1(range(4, E))
                if c:
                    exp_tanhs(g)
                if start:
                    split_w2(range(E))

            groups_before_loop_and_after(act, body)
            normalise(2, r2, result(G - 1), osb_set, G - 1)

        @block.vector
        def _(dve):
            dve.wait_ge(par_in, 32)
            dve.tensor_scalar(lr_bias[:], prm[:, C_ETA_B:C_ETA_B + 3], 0.5, None, ALU.mult).then_inc(par_set, 1)
            dve.tensor_scalar(route_w[:, 0:E], prm[:, C_ROUTE:C_PARAMS], prm[:, C_GAMMA:C_GAMMA + 1], None, ALU.mult).then_inc(par_set, 1)
            dve.tensor_scalar(route_w[:, E:2 * E], prm[:, C_ROUTE:C_PARAMS], prm[:, C_BETA:C_BETA + 1], None, ALU.mult).then_inc(par_set, 1)
            dve.tensor_scalar(gate_rep[:], ones, prm[:, C_GATE_W:C_GATE_W + 1], None, ALU.mult).then_inc(par_set, 1)
            half_b = half64.unsqueeze(1).to_broadcast([P, STAT_TILES, 2])

            def token_squares(i):
                part = slice(i * STAT_TILES, (i + 1) * STAT_TILES)
                dve.wait_ge(sq_set, i + 1)
                dve.tensor_reduce(ssq[:, part], sq[:], AX_X, ALU.add).then_inc(ssq_sum, 1)
                dve.wait_ge(ssq_sum, i + 1)
                dve.tensor_scalar(ssq[:, part], ssq[:, part], NORM_EPS ** 2, None, ALU.max).then_inc(ssq_set, 1)

            def token_weights(i):
                part = slice(i * STAT_TILES, (i + 1) * STAT_TILES)
                dve.wait_ge(inv_set, i + 1)
                dve.tensor_tensor(kdw[:, part, 0:2], inv[:, part].unsqueeze(2).to_broadcast([P, STAT_TILES, 2]), half_b,
                                  ALU.mult).then_inc(kd_half, 1)
                dve.wait_ge(kd_half, i + 1)
                dve.tensor_tensor(kdw[:, part, 2:4], half_b, kdw[:, part, 0:2], ALU.subtract).then_inc(kdw_set, 1)

            def means(i):
                groups = slice(i * STAT_G, (i + 1) * STAT_G)
                dve.wait_ge(kd_mm, i + 1)
                dve.tensor_copy(km[:, kpart(i)].rearrange("p (t h) -> p t h", h=2), kd_ps[:, :, 0:2]).then_inc(km_copy, 1)
                dve.wait_ge(xt_in[i], 16)
                dve.tensor_copy(xt[:, groups, :, CHUNK].rearrange("p t (q h) -> p (t q) h", h=2), kd_ps[:, :, 2:4]).then_inc(km_set, 1)
                k = km[:, kpart(i)].rearrange("p (t b) -> p t b", b=B)
                dve.wait_ge(km_copy, i + 1)
                for j in (0, 2):
                    last = dve.tensor_copy(kb[:, groups, j, :], k)
                last.then_inc(k_hi, 1)
                dve.wait_ge(k_hi, i + 1)
                dve.tensor_tensor(kb[:, groups, 1, :], k, kb[:, groups, 0, :].bitcast(F32), ALU.subtract).then_inc(kb_set, 1)

            def coefficients(i):
                part = kpart(i)
                dve.wait_ge(krow_mm, i + 1)
                dve.tensor_copy(krow[:, i * STAT_G:(i + 1) * STAT_G, :], krow_ps.rearrange("p (t c) -> p t c", c=P)).then_inc(krow_set, 1)
                dve.wait_ge(lr_mean, i + 1)
                dve.tensor_scalar(eta[:, part], mean_ps[:, 0, :], MAX_LR / 2 / CHUNK, MAX_LR / 2, ALU.mult, ALU.add)
                dve.tensor_scalar(alpha[:, part], mean_ps[:, 1, :], (1 - MIN_DECAY) / 2 / CHUNK, (MIN_DECAY - 1) / 2, ALU.mult, ALU.add)
                dve.wait_ge(gate_tanh, i + 1)
                dve.tensor_scalar(gate[:, part], gate[:, part], 0.5, 0.5, ALU.mult, ALU.add).then_inc(coef_in, 1)
                dve.wait_ge(coef_in, i + 1)
                dve.tensor_tensor(decay[:, part], gate[:, part], alpha[:, part], ALU.mult)
                dve.tensor_tensor(lrate[:, part], gate[:, part], eta[:, part], ALU.mult).then_inc(coef_mult, 1)
                dve.wait_ge(coef_mult, i + 1)
                dve.tensor_scalar(decay[:, part], decay[:, part], 1.0, None, ALU.add).then_inc(coef_set, 1)

            def split_w2(experts):
                for e in experts:
                    dve.wait_ge(w2_hi_set, e + 1)
                    dve.tensor_tensor(w2_lo[:, e], w2[:, e], w2_hi[:, e].bitcast(F32), ALU.subtract).then_inc(w2_lo_set, 1)

            def h_low(n, p):
                dve.wait_ge(h_full_set[n // FB], of_block(n, p))
                dve.tensor_tensor(h_lo[:, n % H_RING, :], h_full[:, n % FULL_RING, :],
                                  h_hi[:, n % H_RING, :].bitcast(F32), ALU.subtract).then_inc(h_lo_set[n // FB], 1)

            def weigh(e, p, parity):
                wait_event(dve, w2_mm, e, E, p)
                if e % COMB_E == 0:
                    dve.wait_ge(comb_in[e // COMB_E], p * 16 + 16)
                if e:
                    m, same = earlier(e - 1, YM_RING, E - 1)
                    if same:
                        wait_event(dve, y_added, m, E - 1, p)
                    elif not (isinstance(p, int) and p == 0):
                        wait_event(dve, y_added, m, E - 1, p - 1)
                dst = ym[:, (e - 1) % YM_RING, :] if e else acc[parity][:]
                dve.tensor_tensor(dst, yp[e % Y_BANKS][:], combb[parity][:, e, :], ALU.mult).then_inc(y_weighted[e // 2], 1)

            def row_stats(i, src, g):
                for q in range(TILES):
                    last = dve.bn_stats(st[i][:, q, :], src[:, q, :])
                last.then_inc(ln_step[i], 1)

            def row_sums(i, g):
                wait_event(dve, [ln_step[i]], 0, 2, g)
                dve.tensor_tensor(ln[i][0][:], st[i][:, :, 1], st[i][:, :, 4], ALU.add)
                dve.tensor_tensor(ln[i][1][:], st[i][:, :, 1], st[i][:, :, 4], ALU.subtract)
                dve.tensor_tensor(ln[i][2][:], st[i][:, :, 2], st[i][:, :, 5], ALU.add).then_inc(ln_step[i], 1)

            def row_squares(i, g):
                wait_event(dve, [ln_step[i]], 1, 2, g)
                dve.scalar_tensor_tensor(out=ln[i][3][:], in0=ln[i][1][:], scalar=0.25, in1=ln[i][1][:],
                                         op0=ALU.mult, op1=ALU.mult)
                dve.tensor_scalar(ln[i][4][:], ln[i][2][:], 1.0 / D, LN_EPS, ALU.mult, ALU.add).then_inc(ln_sq[i], 1)

            def row_variance(i, g):
                dve.wait_ge(ln_sq[i], g + 1)
                dve.tensor_tensor(ln[i][5][:], ln[i][4][:], ln[i][3][:], ALU.add).then_inc(ln_var[i], 1)

            def x1_squares(g):
                dve.wait_ge(x1sq_set, g + 1)
                dve.scalar_tensor_tensor(out=ln[1][3][:], in0=x1sum[:], scalar=-1.0 / (D * D), in1=x1sum[:],
                                         op0=ALU.mult, op1=ALU.mult)
                dve.tensor_scalar(ln[1][4][:], x1sq[:], 1.0 / D, LN_EPS, ALU.mult, ALU.add).then_inc(ln_sq[1], 1)

            def shift(i, g):
                dve.wait_ge(ln_rstd[i], g + 1)
                dve.scalar_tensor_tensor(out=ln[i][7][:], in0=ln[i][0][:], scalar=-0.5, in1=ln[i][6][:],
                                         op0=ALU.mult, op1=ALU.mult).then_inc(ln_bias[i], 1)

            def tile_b(t):
                return t[:].unsqueeze(2).to_broadcast([P, TILES, E])

            def expert_b(t):
                return t.unsqueeze(1).to_broadcast([P, TILES, E])

            def logit(step, g):
                after = {L_BETA: None, L_RSTD: L_MEAN, L_ESUM: L_EXP}.get(step, step - 1)
                if step == L_BETA:
                    dve.wait_ge(logit_mm, g + 1)
                elif step == L_RSTD:
                    dve.wait_ge(ln_rstd[1], g + 1)
                elif step == L_DOWN:
                    dve.wait_ge(exp_tanh, g + 1)
                if after is not None and step != L_DOWN:
                    wait_event(dve, logit_step, after, LOGIT_STEPS, g)
                if step == L_BETA:
                    dve.tensor_tensor(lg[2][:], tile_b(x1sum), expert_b(route_s[:, 0:E]), ALU.mult)
                    op = dve.tensor_copy(lg[0][:], logit_ps[:, :, E:2 * E])
                elif step == L_SUM:
                    op = dve.tensor_tensor(lg[1][:], logit_ps[:, :, 0:E], lg[0][:], ALU.add)
                elif step == L_MEAN:
                    op = dve.scalar_tensor_tensor(out=lg[3][:], in0=lg[2][:], scalar=-1.0 / D, in1=lg[1][:], op0=ALU.mult, op1=ALU.add)
                elif step == L_RSTD:
                    op = dve.tensor_tensor(lg[4][:], lg[3][:], tile_b(ln[1][6]), ALU.mult)
                elif step == L_LOGIT:
                    op = dve.tensor_tensor(lg[5][:], lg[4][:], expert_b(route_s[:, E:2 * E]), ALU.add)
                elif step == L_MAX:
                    op = dve.tensor_reduce(lmax[:], lg[5][:], AX_X, ALU.max)
                elif step == L_CENTRED:
                    op = dve.tensor_tensor(lg[6][:], lg[5][:], tile_b(lmax), ALU.subtract)
                elif step == L_DOWN:
                    op = dve.tensor_scalar(lg[8][:], lg[7][:], -1.0, 1.0, ALU.mult, ALU.add)
                elif step == L_INV:
                    op = dve.reciprocal(lg[9][:], lg[8][:])
                elif step == L_RATIO:
                    op = dve.scalar_tensor_tensor(out=lg[10][:], in0=lg[7][:], scalar=1.0, in1=lg[9][:], op0=ALU.add, op1=ALU.mult)
                elif step == L_EXP:
                    op = dve.tensor_tensor(lg[11][:], lg[10][:], lg[10][:], ALU.mult)
                elif step == L_ESUM:
                    op = dve.tensor_reduce(esum[:], lg[11][:], AX_X, ALU.add)
                else:
                    op = dve.reciprocal(einv[:], esum[:])
                op.then_inc(logit_step[step // 2], 1)

            def compare(g):
                own = lg[5][:].unsqueeze(3).to_broadcast([P, TILES, E, E])
                other = lg[5][:].unsqueeze(2).to_broadcast([P, TILES, E, E])
                dve.tensor_tensor(beats[:], other, own, ALU.is_gt)
                dve.tensor_tensor(ties[:], other, own, ALU.is_equal).then_inc(rank_step[R_TIES // 2], 1)

            def rank_sum(g):
                wait_event(dve, rank_step, R_BEATS, RANK_STEPS, g)
                dve.tensor_reduce(rank[:], beats[:], AX_X, ALU.add).then_inc(rank_step[R_RANK // 2], 1)

            def keep_two(g):
                wait_event(dve, rank_step, R_RANK, RANK_STEPS, g)
                dve.scalar_tensor_tensor(out=lg[12][:], in0=rank[:], scalar=2.0, in1=lg[11][:], op0=ALU.is_lt, op1=ALU.mult)

            def routing(g):
                wait_event(dve, logit_step, L_EINV, LOGIT_STEPS, g)
                dve.tensor_tensor(comb[:].rearrange("p e q -> p q e"), lg[12][:], tile_b(einv), ALU.mult).then_inc(comb_set, 1)

            def norm(step, g):
                if step == NORM_IN:
                    dve.wait_ge(ss_mm, g + 1)
                    op = dve.tensor_copy(nrm[0][:], ss_ps)
                else:
                    wait_event(dve, norm_step, step - 1, NORM_STEPS, g)
                if step == NORM_MULT:
                    op = dve.tensor_tensor(nrm[2][:], nrm[1][:], scale_d[:], ALU.mult)
                elif step == NORM_ADD:
                    op = dve.tensor_scalar(nrm[3][:], nrm[2][:], 1e-6, None, ALU.add)
                elif step == NORM_INV:
                    op = dve.reciprocal(nrm[4][:], nrm[3][:])
                elif step == NORM_MIN:
                    op = dve.tensor_scalar(nrm[5][:], nrm[4][:], MAX_NORM, 1.0, ALU.mult, ALU.min)
                elif step == SCALE:
                    op = dve.tensor_tensor(scale[:], nrm[5][:], scale_d[:], ALU.mult)
                op.then_inc(norm_step[step // 2], 1)

            def decayed_scale(g):
                if isinstance(g, int) and g == 0:
                    dve.wait_ge(const_set, 4)
                    dve.wait_ge(coef_set, 1)
                else:
                    wait_event(dve, norm_step, SCALE, NORM_STEPS, g - 1)
                dve.tensor_tensor(scale_d[:], group(decay, g), scale[:], ALU.mult).then_inc(sd_set, 1)

            def inverse_scale(g):
                dve.wait_ge(sd_set, g + 1)
                dve.reciprocal(scale_i[:], scale_d[:]).then_inc(si_set, 1)

            def error_scale(g):
                dve.wait_ge(si_set, g + 1)
                dve.tensor_tensor(err_scale[:], group(lrate, g), scale_i[:], ALU.mult).then_inc(es_set, 1)

            def scaled_outputs(g):
                dve.wait_ge(out_mm, g + 1)
                if isinstance(g, int) and g == 0:
                    dve.wait_ge(const_set, 4)
                else:
                    wait_event(dve, norm_step, SCALE, NORM_STEPS, g - 1)
                for i, bank in enumerate(halves):
                    part = slice(i * HALF, (i + 1) * HALF)
                    last = dve.tensor_tensor(ot[:, part, :], bank[:, 0:HALF * AUG].rearrange("p (b c) -> p b c", c=AUG),
                                             scale[:, part].unsqueeze(2).to_broadcast([P, HALF, AUG]), ALU.mult)
                last.then_inc(ot_set, 1)

            token_squares(0)
            dve.wait_ge(par_set, 4)
            dve.tensor_copy(route_r[:, 0:E], route_w[:, 0:E]).then_inc(par_set, 1)
            token_weights(0)
            dve.wait_ge(par_set, 5)
            dve.tensor_tensor(route_r[:, E:2 * E], route_w[:, 0:E], route_r[:, 0:E].bitcast(F32), ALU.subtract).then_inc(par_set, 1)
            means(0)
            dve.wait_ge(route_mm, 1)
            dve.tensor_copy(route_s[:], route_ps)
            dve.wait_ge(vg_in, 32)
            dve.tensor_scalar(vw2h[:], vw2[:], 0.5, None, ALU.mult).then_inc(par_set, 1)

            def comb_rows(p):
                dve.wait_ge(combt_mm, p + 1)
                if finished(p):
                    dve.wait_ge(comb_out, p * 16)
                dve.tensor_copy(combt[:], combt_ps).then_inc(combt_set, 1)

            def silus(g):
                dve.wait_ge(th_set, g + 1)
                dve.scalar_tensor_tensor(out=hid[:], in0=th[:], scalar=1.0, in1=ca[:], op0=ALU.add, op1=ALU.mult).then_inc(hid_set, 1)

            def silu_sums(g):
                dve.wait_ge(hid_set, g + 1)
                dve.tensor_reduce(hsum[:], hid[:].rearrange("p (b c) -> p b c", c=CHUNK), AX_X, ALU.add).then_inc(hsum_set, 1)

            def memory_residual(g):
                dve.wait_ge(val_mm, g + 1)
                dve.wait_ge(ox_set, g + 1)
                dve.tensor_tensor(rt[:], cb[:], ox[:].rearrange("p b c -> p (b c)"), ALU.add).then_inc(rt_set, 1)

            def errors(g):
                dve.wait_ge(err_mm, g + 1)
                dve.scalar_tensor_tensor(out=err[:], in0=err_ps, scalar=1.0 / CHUNK, in1=ot[:, :, CHUNK],
                                         op0=ALU.mult, op1=ALU.add).then_inc(err_sum, 1)

            def error_high(g):
                dve.wait_ge(err_sum, g + 1)
                dve.wait_ge(es_set, g + 1)
                dve.tensor_tensor(err_f[:], err[:], err_scale[:], ALU.mult)
                dve.tensor_tensor(err_r[:, 0:2, :], err[:].unsqueeze(1).to_broadcast([P, 2, B]),
                                  err_scale[:].unsqueeze(1).to_broadcast([P, 2, B]), ALU.mult).then_inc(err_hi, 1)

            def error_low(g):
                dve.wait_ge(err_hi, g + 1)
                dve.tensor_tensor(err_r[:, 2, :], err_f[:], err_r[:, 0, :].bitcast(F32), ALU.subtract).then_inc(err_set, 1)

            def error_rows(g):
                dve.wait_ge(errt_mm, g + 1)
                dve.tensor_tensor(err_row[:], errt_ps.unsqueeze(1).to_broadcast([ROWS, B, P]),
                                  own_batch.unsqueeze(2).to_broadcast([ROWS, B, P]), ALU.mult).then_inc(err_row_set, 1)

            def expert_residual(p, parity):
                dve.wait_ge(fin_mm, p + 1)
                if not isinstance(p, int) or p >= 1:
                    dve.wait_ge(osb_set, p)
                dve.tensor_tensor(r2[:], cb[:].rearrange("p (q c) -> p q c", q=TILES), x1[parity][:], ALU.add).then_inc(r2_set, 1)

            def r2_stats(p):
                dve.wait_ge(r2_set, p + 1)
                row_stats(2, r2, p)

            def r_stats(g):
                dve.wait_ge(r_mm, g + 1)
                row_stats(0, ca[:].rearrange("p (q c) -> p q c", q=TILES), g)

            def new_memory(g):
                dve.wait_ge(upd_mm, g + 1)
                for i, bank in enumerate(halves):
                    part = slice(i * HALF, (i + 1) * HALF)
                    before = m0[:].unsqueeze(1).to_broadcast([P, HALF, D]) if isinstance(g, int) and g == 0 else mt[:, part, :]
                    last = dve.tensor_tensor(mt[:, part, :], bank[:].rearrange("p (b c) -> p b c", c=D), before, ALU.add)
                last.then_inc(mt_set, 1)

            def x1_low(g, parity):
                dve.wait_ge(x1t_hi_set, g + 1)
                dve.tensor_tensor(x1t_lo[parity][:], cb[:], x1t_hi[parity][:].bitcast(F32), ALU.subtract).then_inc(x1t_lo_set, 1)

            def body(p, parity):
                g = p + 1
                f, fin, c, u, start = ffn(p), finished(p), chained(p), chained(p) and updated(p), not ffn(p)
                if c:
                    scaled_outputs(g)
                if start:
                    token_squares(1)
                    coefficients(0)
                if fin:
                    weigh(7, p - 1, 1 - parity)
                if f:
                    comb_rows(p)
                if u:
                    decayed_scale(g)
                if f:
                    h_low(0, p)
                if u:
                    inverse_scale(g)
                if f:
                    h_low(1, p)
                if start:
                    token_weights(1)
                if c:
                    silus(g)
                if f:
                    h_low(3, p)
                    h_low(5, p)
                if start:
                    means(1)
                if c:
                    memory_residual(g)
                if u:
                    error_scale(g)
                    silu_sums(g)
                if c:
                    r_stats(g)
                if u:
                    errors(g)
                if c:
                    row_sums(0, g)
                if u:
                    error_high(g)
                if c:
                    row_squares(0, g)
                if f:
                    weigh(0, p, parity)
                if c:
                    row_variance(0, g)
                if start:
                    coefficients(1)
                    token_squares(2)
                if f:
                    weigh(1, p, parity)
                if u:
                    error_low(g)
                if fin:
                    expert_residual(p - 1, 1 - parity)
                if c:
                    shift(0, g)
                if f:
                    h_low(7, p)
                    h_low(9, p)
                if u:
                    error_rows(g)
                if start:
                    token_weights(2)
                    means(2)
                    token_squares(3)
                if f:
                    weigh(2, p, parity)
                if u:
                    new_memory(g)
                if start:
                    coefficients(2)
                    token_weights(3)
                    means(3)
                if f:
                    weigh(3, p, parity)
                    h_low(11, p)
                if fin:
                    r2_stats(p - 1)
                    row_sums(2, p - 1)
                if f:
                    weigh(4, p, parity)
                if fin:
                    row_squares(2, p - 1)
                    row_variance(2, p - 1)
                if c:
                    x1_low(g, 1 - parity)
                if start:
                    coefficients(3)
                if u:
                    norm(NORM_IN, g)
                if f:
                    h_low(13, p)
                if fin:
                    shift(2, p - 1)
                if c:
                    x1_squares(g)
                    logit(L_BETA, g)
                    row_variance(1, g)
                if f:
                    weigh(5, p, parity)
                if c:
                    logit(L_SUM, g)
                    logit(L_MEAN, g)
                if u:
                    norm(NORM_MULT, g)
                if f:
                    h_low(14, p)
                if c:
                    logit(L_RSTD, g)
                    logit(L_LOGIT, g)
                if u:
                    norm(NORM_ADD, g)
                if c:
                    logit(L_MAX, g)
                    compare(g)
                    logit(L_CENTRED, g)
                if f:
                    h_low(15, p)
                if c:
                    logit(L_DOWN, g)
                if f:
                    weigh(6, p, parity)
                if c:
                    logit(L_INV, g)
                if u:
                    norm(NORM_INV, g)
                if c:
                    logit(L_RATIO, g)
                    logit(L_EXP, g)
                if u:
                    norm(NORM_MIN, g)
                if c:
                    rank_sum(g)
                    logit(L_ESUM, g)
                if u:
                    norm(SCALE, g)
                if c:
                    keep_two(g)
                    logit(L_EINV, g)
                    routing(g)
                if start:
                    split_w2(range(E))

            groups_before_loop_and_after(dve, body)
            weigh(7, G - 1, (G - 1) % 2)
            expert_residual(G - 1, (G - 1) % 2)
            r2_stats(G - 1)
            row_sums(2, G - 1)
            row_squares(2, G - 1)
            row_variance(2, G - 1)
            shift(2, G - 1)

        @block.tensor
        def _(pe):
            def outputs(g):
                if isinstance(g, int) and g == 0:
                    pe.wait_ge(m_in, 16)
                    for i in range(2):
                        last = pe.matmul(halves[i][:, 0:HALF * AUG], m0[:], xt[:, 0, i * HALF:(i + 1) * HALF, :], start=True, stop=True)
                    last.then_inc(out_mm, 1)
                    return
                pe.wait_ge(mt_set, g)
                for b in range(B):
                    dst = halves[b // HALF][:, (b % HALF) * AUG:(b % HALF + 1) * AUG]
                    last = pe.matmul(dst, mt[:, b, :], xgroup(g)[:, b, :], start=True, stop=True)
                last.then_inc(out_mm, 1)

            def hidden(g):
                pe.wait_ge(ot_set, g + 1)
                pe.matmul(ca[:], vw1[:], ot[:, :, 0:CHUNK], start=True, stop=True).then_inc(hid_mm, 1)

            def value(g):
                pe.wait_ge(hid_set, g + 1)
                pe.matmul(cb[:], vw2h[:], hid[:], start=True, stop=True).then_inc(val_mm, 1)

            def turn_r(g):
                pe.wait_ge(rt_set, g + 1)
                for q in range(TILES):
                    last = pe.transpose(ca[:, q * P:(q + 1) * P], rt[:, q * P:(q + 1) * P], ident)
                last.then_inc(r_mm, 1)

            def error(g):
                pe.wait_ge(hsum_set, g + 1)
                pe.matmul(err_ps, vw2h[:], hsum[:], start=True, stop=True).then_inc(err_mm, 1)

            def turn_error(g):
                pe.wait_ge(err_set, g + 1)
                pe.transpose(errt_ps, err_r[:].rearrange("p j b -> p (j b)").bitcast(F32), ident).then_inc(errt_mm, 1)

            def turn_x1(g, parity):
                if updated(g - 1):
                    pe.wait_ge(mt_set, g + 1)
                else:
                    pe.wait_ge(r2_set, g - 1)
                pe.wait_ge(x1_set, g + 1)
                for q in range(TILES):
                    last = pe.transpose(cb[:, q * P:(q + 1) * P], x1[parity][:, q, :], ident)
                last.then_inc(x1t_mm, 1)

            def route(g, parity):
                pe.wait_ge(x1t_lo_set, g + 1)
                if updated(g - 1):
                    wait_event(pe, norm_step, NORM_IN, NORM_STEPS, g)
                for q in range(TILES):
                    part = slice(q * P, (q + 1) * P)
                    pe.matmul(logit_ps[:, q, :], x1t_hi[parity][:, part], route_r[:], start=True, stop=False)
                    last = pe.matmul(logit_ps[:, q, 0:E], x1t_lo[parity][:, part], route_r[:, 0:E], start=False, stop=True)
                last.then_inc(logit_mm, 1)

            def update(g):
                pe.wait_ge(kcur_set, g + 1)
                if finished(g - 1):
                    pe.wait_ge(r2_set, g - 1)
                pe.wait_ge(x1_set, g + 1)
                pe.wait_ge(err_row_set, g + 1)
                for i, bank in enumerate(halves):
                    src = err_row[:, i * HALF:(i + 1) * HALF, :].rearrange("p b c -> p (b c)")
                    last = pe.matmul(bank[:], kcur[:], src, start=True, stop=True)
                last.then_inc(upd_mm, 1)

            def norm(g):
                wait_event(pe, [msq_set], 1, 2, g)
                pe.wait_ge(err_row_set, g + 1)
                pe.matmul(ss_ps, ones, mss[:], start=True, stop=True).then_inc(ss_mm, 1)

            def turn_comb(g):
                pe.wait_ge(comb_set, g + 1)
                pe.transpose(combt_ps, comb[:].rearrange("p e q -> p (e q)"), ident).then_inc(combt_mm, 1)

            def finish(p, parity):
                wait_event(pe, y_added, E - 2, E - 1, p)
                for q in range(TILES):
                    last = pe.transpose(cb[:, q * P:(q + 1) * P], acc[parity][:, q * P:(q + 1) * P], ident)
                last.then_inc(fin_mm, 1)

            def first(n, p, parity):
                e, k = divmod(n, FB)
                if isinstance(p, int) and p == 0 and k == 0:
                    pe.wait_ge(w1_lo_set, e + 1)
                    if e == 0:
                        pe.wait_ge(coef_in, STAT_STEPS)
                part = slice(k * P, (k + 1) * P)
                wait_earlier_block(pe, h_full_set, n, H_BANKS, p)
                pe.matmul(hp[n % H_BANKS][:], w1_hi[:, e, part], x1t_hi[parity][:], start=True, stop=False)
                pe.matmul(hp[n % H_BANKS][:], w1_lo[:, e, part], x1t_hi[parity][:], start=False, stop=False)
                pe.matmul(hp[n % H_BANKS][:], w1_hi[:, e, part], x1t_lo[parity][:], start=False, stop=True).then_inc(w1_mm[e], 1)

            def second_high(e, p):
                if isinstance(p, int) and p == 0:
                    pe.wait_ge(w2_lo_set, e + 1)
                m, same = earlier(e, Y_BANKS, E)
                if same:
                    wait_event(pe, y_weighted, m, E, p)
                elif not (isinstance(p, int) and p == 0):
                    wait_event(pe, y_weighted, m, E, p - 1)
                for k in range(FB):
                    n = FB * e + k
                    pe.wait_ge(h_full_set[e], of_block(n, p))
                    pe.matmul(yp[e % Y_BANKS][:], w2_hi[:, e, k, :], h_hi[:, n % H_RING, :], start=(k == 0), stop=False)
                    pe.matmul(yp[e % Y_BANKS][:], w2_lo[:, e, k, :], h_hi[:, n % H_RING, :], start=False, stop=False)

            def second_low(e, p):
                pe.wait_ge(h_lo_set[e], of_block(FB - 1, p))
                for k in range(FB):
                    last = pe.matmul(yp[e % Y_BANKS][:], w2_hi[:, e, k, :], h_lo[:, (FB * e + k) % H_RING, :], start=False, stop=(k == FB - 1))
                last.then_inc(w2_mm[e // 2], 1)

            def chunk_sums(i):
                pe.wait_ge(kdw_set, i + 1)
                if i:
                    pe.wait_ge(km_set, i)
                for t in range(STAT_TILES):
                    tile = i * STAT_TILES + t
                    last = pe.matmul(kd_ps[:, t, :], xtok[:, tile, :], kdw[:, tile, :], start=True, stop=True)
                last.then_inc(kd_mm, 1)

            def token_rates(i):
                pe.wait_ge(xt_in[i], 16)
                if i:
                    pe.wait_ge(lr_tanh, i)
                for c in range(STAT_C):
                    t, b = divmod(c, B)
                    last = pe.matmul(lr_ps[:, c, :], xt[:, i * STAT_G + t, b, 0:CHUNK], prm[:, C_ETA_W:C_ETA_W + 2], start=True, stop=True)
                last.then_inc(lr_mm, 1)

            def chunk_rates(i):
                pe.wait_ge(km_copy, i + 1)
                if i:
                    pe.wait_ge(gate_tanh, i)
                pe.matmul(gate_ps, gate_rep[:], km[:, kpart(i)], start=True, stop=True).then_inc(gate_mm, 1)
                pe.wait_ge(kb_set, i + 1)
                if i:
                    pe.wait_ge(krow_set, i)
                for t in range(STAT_G):
                    last = pe.transpose(krow_ps[:, t * P:(t + 1) * P],
                                        kb[:, i * STAT_G + t].rearrange("p j b -> p (j b)").bitcast(F32), ident)
                last.then_inc(krow_mm, 1)
                pe.wait_ge(lr_tanh, i + 1)
                if i:
                    pe.wait_ge(coef_in, i)
                pe.matmul(mean_ps, ones[0:CHUNK, :], lr_th[:].rearrange("p w c -> p (w c)"), start=True, stop=True).then_inc(lr_mean, 1)

            pe.wait_ge(par_set, 4)
            pe.matmul(route_ps, ones, route_w[:], start=True, stop=True).then_inc(route_mm, 1)
            token_rates(0)
            chunk_sums(0)
            pe.wait_ge(km_set, 1)
            outputs(0)
            chunk_rates(0)
            pe.wait_ge(vg_in, 32)

            def body(p, parity):
                g = p + 1
                f, fin, c, u, start = ffn(p), finished(p), chained(p), chained(p) and updated(p), not ffn(p)
                if f:
                    first(0, p, parity)
                if fin:
                    second_high(7, p - 1)
                if f:
                    first(1, p, parity)
                    first(2, p, parity)
                if fin:
                    second_low(7, p - 1)
                if f:
                    first(3, p, parity)
                    first(4, p, parity)
                    turn_comb(p)
                    first(5, p, parity)
                if c:
                    hidden(g)
                if start:
                    token_rates(1)
                    chunk_sums(1)
                if f:
                    second_high(0, p)
                    second_high(1, p)
                if c:
                    value(g)
                if start:
                    chunk_rates(1)
                if f:
                    second_low(0, p)
                    first(6, p, parity)
                if c:
                    turn_r(g)
                if start:
                    token_rates(2)
                if f:
                    first(7, p, parity)
                if u:
                    error(g)
                if f:
                    second_low(1, p)
                    first(8, p, parity)
                if fin:
                    finish(p - 1, 1 - parity)
                if f:
                    first(9, p, parity)
                    first(10, p, parity)
                if u:
                    turn_error(g)
                if f:
                    second_high(2, p)
                    second_high(3, p)
                    second_low(2, p)
                    first(11, p, parity)
                if u:
                    update(g)
                if start:
                    chunk_sums(2)
                    chunk_rates(2)
                    token_rates(3)
                if f:
                    second_low(3, p)
                    first(12, p, parity)
                    second_high(4, p)
                if c:
                    turn_x1(g, 1 - parity)
                if start:
                    chunk_sums(3)
                    chunk_rates(3)
                if f:
                    first(13, p, parity)
                    second_low(4, p)
                    second_high(5, p)
                    first(14, p, parity)
                    second_low(5, p)
                if u:
                    norm(g)
                if f:
                    first(15, p, parity)
                if c:
                    route(g, 1 - parity)
                if f:
                    second_high(6, p)
                if u:
                    outputs(g + 1)
                if f:
                    second_low(6, p)

            groups_before_loop_and_after(pe, body)
            second_high(7, G - 1)
            second_low(7, G - 1)
            finish(G - 1, (G - 1) % 2)


def pack(x, m_init, eta_w, eta_b, alpha_w, alpha_b, gate_w, gate_b, vg_w1, vg_w2, gamma, beta, route_w, w1, w2):
    xs = x.reshape(TILES, 2, G, CHUNK, D)
    x_tok = xs.transpose(1, 3, 2, 0, 4).reshape(P, ALL_TILES, D)
    x_chan = np.zeros((P, G, B, AUG), x.dtype)
    x_chan[..., :CHUNK] = x.reshape(B, G, CHUNK, D).transpose(3, 1, 0, 2)
    params = np.zeros((P, C_PARAMS), x.dtype)
    for column, values in ((C_GAMMA, gamma), (C_BETA, beta), (C_ETA_W, eta_w), (C_ALPHA_W, alpha_w), (C_GATE_W, gate_w),
                           (C_ETA_B, eta_b), (C_ALPHA_B, alpha_b), (C_GATE_B, gate_b)):
        params[:, column] = values
    params[:, C_ROUTE:] = route_w.T
    consts = np.zeros((P, K_CONSTS), np.float32)
    consts[:, K_IDENT:K_IDENT + P] = np.eye(P)
    consts[:, K_ONES:K_ONES + P] = 1
    consts[:CHUNK, K_HALVES] = consts[CHUNK:, K_HALVES + 1] = 1 / CHUNK
    consts[:, K_LOWER:K_BATCH] = np.tril(np.ones((E, E)), -1).ravel()
    consts[:ROWS, K_BATCH:] = np.tile(np.eye(B), (3, 1))
    return {
        "x_tok": x_tok, "x_chan": x_chan, "m_init_t": m_init.T, "vg_w1t": vg_w1.T, "vg_w2t": vg_w2.T,
        "w1t": w1.transpose(2, 0, 1), "w2t": w2.reshape(E, D, FB, P).transpose(3, 0, 2, 1),
        "params": params, "consts": consts,
    }


def kernel(L0_attn_x, L0_attn_M_init, L0_attn_eta_w, L0_attn_eta_b, L0_attn_alpha_w, L0_attn_alpha_b, L0_attn_gate_w,
           L0_attn_gate_b, L0_attn_vg_w1, L0_attn_vg_w2, L0_ffn_ln_gamma, L0_ffn_ln_beta, L0_ffn_gate_w, L0_ffn_w1, L0_ffn_w2):
    from concourse.bacc import Bacc
    from concourse.bass_utils import run_bass_kernel_spmd

    given = [L0_attn_x, L0_attn_M_init, L0_attn_eta_w, L0_attn_eta_b, L0_attn_alpha_w, L0_attn_alpha_b, L0_attn_gate_w,
             L0_attn_gate_b, L0_attn_vg_w1, L0_attn_vg_w2, L0_ffn_ln_gamma, L0_ffn_ln_beta, L0_ffn_gate_w, L0_ffn_w1, L0_ffn_w2]
    arrays = {f"in_{n}": np.ascontiguousarray(a) for n, a in pack(*(np.asarray(a) for a in given)).items()}
    nc = Bacc("TRN2", target_bir_lowering=False, num_devices=1)
    ins = [nc.dram_tensor(n, a.shape, mybir.dt.from_np(a.dtype), kind="ExternalInput").ap() for n, a in arrays.items()]
    out = nc.dram_tensor("out_dev", (G, P, TILES * D), F32, kind="ExternalOutput").ap()
    build(nc, *ins, out)
    got = run_bass_kernel_spmd(nc, [arrays], core_ids=[0]).results[0]["out_dev"]
    return got.reshape(G, 2, CHUNK, TILES, D).transpose(3, 1, 0, 2, 4).reshape(B, S, D)
```

```python
from contextlib import ExitStack

import numpy as np

import concourse.bass as bass
from concourse import mybir

F32 = mybir.dt.float32
F32R = mybir.dt.float32r
ALU = mybir.AluOpType
ACT = mybir.ActivationFunctionType
AX_X = mybir.AxisListType.X

P = 128
B, S, D = 8, 512, 128
CHUNK = 64
G = S // CHUNK
TOK = B * CHUNK
TILES = TOK // P
ALL_TILES = G * TILES
AUG = CHUNK + 1
PAIR = 2 * AUG
HALF = B // 2
E = 8
F = 256
FB = F // P
BLOCKS = E * FB
H_BANKS = 3
H_RING = 6
FULL_RING = 6
Y_BANKS = 2
YM_RING = 3
COMB_PARTS = 4
COMB_E = E // COMB_PARTS
STAT_G = 2
STAT_TILES = STAT_G * TILES
STAT_STEPS = G // STAT_G
STAT_C = STAT_G * B
RATE_G = 4
RATE_STEPS = G // RATE_G
RATE_ROWS = P // RATE_G
KD_ROWS = P // TILES
ROWS = 3 * B
MAX_LR, MIN_DECAY, MAX_NORM, NORM_EPS, LN_EPS = 0.2, 0.5, 30.0, 1e-5, 1e-5

NORM_IN, NORM_ROOT, NORM_MULT, NORM_ADD, NORM_INV, NORM_MIN, SCALE = range(7)
NORM_STEPS = 7
L_BETA, L_SUM, L_MEAN, L_RSTD, L_LOGIT, L_MAX, L_CENTRED, L_DOWN, L_INV, L_RATIO, L_EXP, L_ESUM, L_EINV = range(13)
LOGIT_STEPS = 13
R_TIES, R_LOWER, R_BEATS, R_RANK, R_KEEP = range(5)
RANK_STEPS = 5

C_GAMMA, C_BETA, C_GATE_W, C_RATE_B, C_GATE_B, C_ROUTE = range(6)
C_RATE_W = C_ROUTE + E
C_PARAMS = C_RATE_W + RATE_ROWS
K_IDENT, K_ONES, K_HALVES, K_LOWER = 0, P, 2 * P, 2 * P + 2
K_BATCH = K_LOWER + E * E
K_RATE = K_BATCH + B
K_CONSTS = K_RATE + 2 * RATE_G


def build(nc, x_tok, x_chan, m_init_t, vg_w1t, vg_w2t, w1t, w2t, params, consts, out):
    with ExitStack() as ctx:
        def sb(name, shape, dt=F32):
            return ctx.enter_context(nc.sbuf_tensor(name, shape, dt))

        def sem(name):
            return ctx.enter_context(nc.semaphore(name))

        def sems(name, n):
            return [sem(f"{name}{i}") for i in range(n)]

        def pairs(name, n):
            return sems(name, (n + 1) // 2)

        hp = [ctx.enter_context(nc.psum_tensor(f"hp{i}", [P, TOK], F32)) for i in range(H_BANKS)]
        yp = [ctx.enter_context(nc.psum_tensor(f"yp{i}", [P, TOK], F32)) for i in range(Y_BANKS)]
        ca = ctx.enter_context(nc.psum_tensor("ca", [P, TOK], F32))
        cb = ctx.enter_context(nc.psum_tensor("cb", [P, TOK], F32))
        small = ctx.enter_context(nc.psum_tensor("small", [P, TOK], F32))
        err_ps = small[:, 0:B]
        errt_ps = small[0:ROWS, 8:8 + P]
        ss_ps = small[:, 136:136 + B]
        logit_ps = small[:, 144:144 + TILES * 2 * E].rearrange("p (q e) -> p q e", q=TILES)
        combt_ps = small[0:E * TILES, 208:208 + P]
        kd_row_ps = yp[0][:, 0:STAT_G * P]
        kd_ps = yp[0][:, STAT_G * P:2 * STAT_G * P]
        rate_ps = yp[1]
        mean_ps = hp[0][:, 0:2 * RATE_G * B].rearrange("p (w c) -> p w c", w=2)
        gate_ps = hp[1][:, 0:STAT_C]
        krow_ps = hp[2][0:ROWS, 0:STAT_G * P]
        route_ps = small[:, 0:2 * E]
        halves = [ca, cb]

        xtok = sb("xtok", [P, ALL_TILES, D])
        xt = sb("xt", [P, G, TILES, PAIR])
        prm = sb("prm", [P, C_PARAMS])
        cst = sb("cst", [P, K_CONSTS])
        vw1 = sb("vw1", [P, D])
        vw2 = sb("vw2", [P, D])
        vw2h = sb("vw2h", [P, D])
        combb = [sb(f"combb{i}", [P, E, TOK]) for i in range(2)]
        raw = combb[1][:].rearrange("p e t -> p (e t)")
        w1 = raw[:, 0:E * F].rearrange("p (e f) -> p e f", e=E)
        w2 = raw[:, E * F:2 * E * F].rearrange("p (e k c) -> p e k c", e=E, k=FB)
        w1_hi, w1_lo = sb("w1_hi", [P, E, F], F32R), sb("w1_lo", [P, E, F], F32R)
        w2_hi, w2_lo = sb("w2_hi", [P, E, FB, D], F32R), sb("w2_lo", [P, E, FB, D], F32R)
        ident = cst[:, K_IDENT:K_IDENT + P]
        ones = cst[:, K_ONES:K_ONES + P]
        half64 = cst[:, K_HALVES:K_HALVES + 2]
        lower = cst[:, K_LOWER:K_LOWER + E * E]
        own_rate = cst[:, K_RATE:K_RATE + 2 * RATE_G]
        own_batch = cst[0:ROWS, K_BATCH:K_BATCH + B]

        sq = sb("sq", [P, STAT_TILES, D])
        ssq = sb("ssq", [P, ALL_TILES])
        inv = sb("inv", [P, ALL_TILES])
        kdw = [sb(f"kdw{i}", [P, STAT_TILES, KD_ROWS]) for i in range(2)]
        kd_row = sb("kd_row", [P, STAT_G * P])
        km = sb("km", [P, G * B])
        kb = sb("kb", [P, G, 3, B], F32R)
        krow = sb("krow", [ROWS, G, P], F32R)
        rate_th = sb("rate_th", [P, TOK])
        rate_sum = sb("rate_sum", [P, B])
        rate_mask = sb("rate_mask", [P, 2 * RATE_G, B])
        lr_bias = sb("lr_bias", [P, 2])
        eta = sb("eta", [P, G * B])
        alpha = sb("alpha", [P, G * B])
        gate = sb("gate", [P, G * B])
        gate_rep = sb("gate_rep", [P, P])
        decay = sb("decay", [P, G * B])
        lrate = sb("lrate", [P, G * B])
        c_half = sb("c_half", [P, ALL_TILES])
        c_root = sb("c_root", [P, B])
        c_one = sb("c_one", [ROWS, P])

        m0 = sb("m0", [P, D])
        mt = sb("mt", [P, B, D])
        msq = sb("msq", [P, B, D])
        mss = sb("mss", [P, B])
        scale = sb("scale", [P, B])
        scale_d = sb("scale_d", [P, B])
        scale_i = sb("scale_i", [P, B])
        err_scale = sb("err_scale", [P, B])
        nrm = [sb(f"nrm{i}", [P, B]) for i in range(6)]
        ot = sb("ot", [P, B, AUG])
        ot_pairs = ot[:].rearrange("p (q h) c -> p q (h c)", h=2)
        ox = sb("ox", [P, TILES, P])
        th = sb("th", [P, TOK])
        hid = sb("hid", [P, TOK])
        hsum = sb("hsum", [P, B])
        err = sb("err", [P, B])
        err_f = sb("err_f", [P, B])
        err_r = sb("err_r", [P, 3, B], F32R)
        err_row = sb("err_row", [ROWS, B, P], F32R)
        kcur = sb("kcur", [ROWS, P], F32R)
        rt = sb("rt", [P, TOK])

        st = [sb(f"st{i}", [P, TILES, 6]) for i in range(3)]
        ln = [[sb(f"ln{i}_{j}", [P, TILES]) for j in range(9)] for i in range(3)]
        x1 = [sb(f"x1_{i}", [P, TILES, D]) for i in range(2)]
        x1t_hi = [sb(f"x1t_hi{i}", [P, TOK], F32R) for i in range(2)]
        x1t_lo = [sb(f"x1t_lo{i}", [P, TOK], F32R) for i in range(2)]
        route_w = sb("route_w", [P, 2 * E])
        route_r = sb("route_r", [P, 2 * E], F32R)
        route_s = sb("route_s", [P, 2 * E])
        lg = [sb(f"lg{i}", [P, TILES, E]) for i in range(13)]
        lmax = sb("lmax", [P, TILES])
        esum = sb("esum", [P, TILES])
        einv = sb("einv", [P, TILES])
        beats = sb("beats", [P, TILES, E, E])
        ties = sb("ties", [P, TILES, E, E])
        rank = sb("rank", [P, TILES, E])
        x1_junk = sb("x1_junk", [P, TILES, D])
        x1sum, x1sq = sb("x1sum", [P, TILES]), sb("x1sq", [P, TILES])
        comb = sb("comb", [P, E, TILES])
        combt = sb("combt", [E * TILES, P])
        comb_dram = nc.dram_tensor("comb_dram", [2, E * TILES, P], F32).ap()

        h_full = sb("h_full", [P, FULL_RING, TOK])
        h_hi = sb("h_hi", [P, H_RING, TOK], F32R)
        h_lo = sb("h_lo", [P, H_RING, TOK], F32R)
        ym = sb("ym", [P, YM_RING, TOK])
        acc = [sb(f"acc{i}", [P, TOK]) for i in range(2)]
        r2 = sb("r2", [P, TILES, D])

        def result(g):
            return xtok[:, g * TILES:(g + 1) * TILES, :] if isinstance(g, int) else xtok[:, bass.ds(g * TILES, TILES), :]

        x_in, xt_in = sems("x_in", STAT_STEPS), sems("xt_in", STAT_STEPS)
        m_in, par_in, vg_in = sem("m_in"), sem("par_in"), sem("vg_in")
        w1_in, w2_in = sems("w1_in", 2), sems("w2_in", 2)
        const_set, par_set, d_set = sem("const_set"), sem("par_set"), sem("d_set")
        start_mm = sem("start_mm")
        sq_set, ssq_sum, ssq_set, inv_set, kd_half, kdw_set, kd_mm, kd_row_set, kd_turned, km_copy, km_set, k_hi, kb_set, krow_mm, krow_set = (sem(n) for n in (
            "sq_set", "ssq_sum", "ssq_set", "inv_set", "kd_half", "kdw_set", "kd_mm", "kd_row_set", "kd_turned", "km_copy", "km_set", "k_hi", "kb_set", "krow_mm", "krow_set"))
        lr_mm, lr_tanh, lr_sum, lr_masked, lr_mean, gate_mm, gate_tanh, coef_in, coef_mult, coef_set = (sem(n) for n in (
            "lr_mm", "lr_tanh", "lr_sum", "lr_masked", "lr_mean", "gate_mm", "gate_tanh", "coef_in", "coef_mult", "coef_set"))
        w1_hi_set, w1_lo_set, w2_hi_set, w2_lo_set = (sem(n) for n in ("w1_hi_set", "w1_lo_set", "w2_hi_set", "w2_lo_set"))
        out_mm, ot_set, ox_set, hid_mm, th_set, hid_set, hsum_set, val_mm, rt_set, r_mm = (sem(n) for n in (
            "out_mm", "ot_set", "ox_set", "hid_mm", "th_set", "hid_set", "hsum_set", "val_mm", "rt_set", "r_mm"))
        err_mm, err_sum, err_hi, err_set, errt_mm, err_row_set, kcur_set, upd_mm, mt_set, msq_set, ss_mm = (sem(n) for n in (
            "err_mm", "err_sum", "err_hi", "err_set", "errt_mm", "err_row_set", "kcur_set", "upd_mm", "mt_set", "msq_set", "ss_mm"))
        norm_step = pairs("norm_step", NORM_STEPS)
        sd_set, si_set, es_set = sem("sd_set"), sem("si_set"), sem("es_set")
        ln_step, ln_sq, ln_var, ln_rstd, ln_bias = (sems(n, 3) for n in ("ln_step", "ln_sq", "ln_var", "ln_rstd", "ln_bias"))
        x1_set, x1sq_set, x1t_mm, x1t_hi_set, x1t_lo_set, logit_mm = (sem(n) for n in (
            "x1_set", "x1sq_set", "x1t_mm", "x1t_hi_set", "x1t_lo_set", "logit_mm"))
        logit_step = pairs("logit_step", LOGIT_STEPS)
        rank_step = pairs("rank_step", RANK_STEPS)
        exp_tanh, comb_set, combt_mm, combt_set, comb_out = (sem(n) for n in ("exp_tanh", "comb_set", "combt_mm", "combt_set", "comb_out"))
        comb_in = sems("comb_in", COMB_PARTS)
        w1_mm = sems("w1_mm", E)
        h_full_set = sems("h_full_set", E)
        h_lo_set = sems("h_lo_set", E)
        w2_mm = pairs("w2_mm", E)
        y_weighted = pairs("y_weighted", E)
        y_added = pairs("y_added", E - 1)
        fin_mm, r2_set, osb_set = sem("fin_mm"), sem("r2_set"), sem("osb_set")
        stored = sem("stored")

        def earlier(n, ring, count):
            if n >= ring:
                return n - ring, True
            return max(m for m in range(count) if m % ring == n % ring), False

        def wait_event(eng, pair_sems, k, n, g):
            eng.wait_ge(pair_sems[k // 2], g * min(2, n - k // 2 * 2) + (k % 2 + 1))

        def of_block(n, p):
            return p * FB + (n % FB + 1)

        def wait_earlier_block(eng, sem_list, n, ring, p):
            m, same = earlier(n, ring, BLOCKS)
            if same:
                eng.wait_ge(sem_list[m // FB], of_block(m, p))
            elif not (isinstance(p, int) and p == 0):
                eng.wait_ge(sem_list[m // FB], of_block(m, p - 1))

        def loop_and_after(eng, body):
            with eng.Fori(0, 2) as pair:
                for j in range(2):
                    body(pair * 2 + (1 + j), 1 - j)
            for p in range(5, G):
                body(p, p % 2)

        def chained(p):
            return not isinstance(p, int) or p + 1 < G

        def updated(p):
            return not isinstance(p, int) or p + 2 < G

        def ffn(p):
            return not isinstance(p, int) or p >= 0

        def finished(p):
            return not isinstance(p, int) or p >= 1

        def group(t, g):
            return t[:, bass.ds(g * B, B)] if not isinstance(g, int) else t[:, g * B:(g + 1) * B]

        def xgroup(g):
            return xt[:, g] if isinstance(g, int) else xt[:, bass.ds(g, 1)].rearrange("p o q c -> p (o q) c")

        def kpart(i):
            return slice(i * STAT_C, (i + 1) * STAT_C)

        block = ctx.enter_context(nc.Block())

        @block.sync
        def _(sp):
            sp.dma_start(prm[:], params).then_inc(par_in, 16)
            for i in range(STAT_STEPS):
                part, groups = slice(i * STAT_TILES, (i + 1) * STAT_TILES), slice(i * STAT_G, (i + 1) * STAT_G)
                sp.dma_start(xtok[:, part, :], x_tok[:, part, :]).then_inc(x_in[i], 16)
                if i == 0:
                    sp.dma_start(cst[:], consts).then_inc(par_in, 16)
                sp.dma_start(xt[:, groups], x_chan[:, groups]).then_inc(xt_in[i], 16)
            for i in range(2):
                half = slice(i * E // 2, (i + 1) * E // 2)
                sp.dma_start(w1[:, half], w1t[:, half]).then_inc(w1_in[i], 16)
            for i in range(2):
                half = slice(i * E // 2, (i + 1) * E // 2)
                sp.dma_start(w2[:, half], w2t[:, half]).then_inc(w2_in[i], 16)

            def body(p, parity):
                if ffn(p):
                    sp.wait_ge(combt_set, p + 1)
                    sp.dma_start(comb_dram[parity], combt[:]).then_inc(comb_out, 16)
                    if not isinstance(p, int) or p >= 2:
                        wait_event(sp, y_weighted, E - 1, E, p - 2)
                    if isinstance(p, int) and p == 1:
                        sp.wait_ge(w1_lo_set, E)
                        sp.wait_ge(w2_lo_set, E)
                    sp.wait_ge(comb_out, p * 16 + 16)
                    for c in range(COMB_PARTS):
                        part = slice(c * COMB_E, (c + 1) * COMB_E)
                        src = comb_dram[parity, c * COMB_E * TILES:(c + 1) * COMB_E * TILES, :].rearrange("(o q) t -> o (q t)", o=1)
                        sp.dma_start(combb[parity][:, part, :].rearrange("p e t -> p (e t)"),
                                     src.to_broadcast([P, COMB_E * TOK])).then_inc(comb_in[c], 16)
                if finished(p):
                    sp.wait_ge(osb_set, p)
                    row = out[p - 1] if isinstance(p, int) else out[bass.ds(p - 1, 1)].rearrange("o p c -> (o p) c")
                    sp.dma_start(row, result(p - 1).rearrange("p q c -> p (q c)")).then_inc(stored, 16)

            body(0, 0)
            loop_and_after(sp, body)
            for half in range(2):
                tiles = slice(half * TILES // 2, (half + 1) * TILES // 2)
                sp.wait_ge(osb_set, G - 1 + tiles.stop)
                sp.dma_start(out[G - 1, :, tiles.start * D:tiles.stop * D],
                             result(G - 1)[:, tiles, :].rearrange("p q c -> p (q c)")).then_inc(stored, 16)
            sp.wait_ge(stored, 16 * (G + 1))

        @block.gpsimd
        def _(pool):
            for i in range(2):
                pool.memset(kdw[i][:], 0.0).then_inc(const_set, 1)
            pool.memset(c_half[:], -0.5).then_inc(const_set, 1)
            pool.memset(c_root[:], 0.5).then_inc(const_set, 1)
            pool.memset(c_one[:], 1.0).then_inc(const_set, 1)
            pool.memset(scale[:], 1.0).then_inc(const_set, 1)
            pool.wait_ge(const_set, 6)

            def token_norms(i):
                part = slice(i * STAT_TILES, (i + 1) * STAT_TILES)
                pool.wait_ge(ssq_set, i + 1)
                pool.tensor_tensor(inv[:, part], ssq[:, part], c_half[:, part], ALU.pow).then_inc(inv_set, 1)

            def split_w1(start, stop):
                for e in range(start, stop):
                    pool.wait_ge(w1_hi_set, e + 1)
                    pool.tensor_tensor(w1_lo[:, e, :], w1[:, e, :], w1_hi[:, e, :].bitcast(F32), ALU.subtract).then_inc(w1_lo_set, 1)

            def power(i, g):
                pool.wait_ge(ln_var[i], g + 1)
                pool.tensor_tensor(ln[i][6][:], ln[i][5][:], c_half[:, 0:TILES], ALU.pow).then_inc(ln_rstd[i], 1)

            def y_add(e, p, parity):
                if isinstance(p, int) and p == G - 1 and e == E - 2:
                    return
                wait_event(pool, y_weighted, e, E, p)
                if e > 1:
                    wait_event(pool, y_added, e - 2, E - 1, p)
                pool.tensor_tensor(acc[parity][:], acc[parity][:], ym[:, (e - 1) % YM_RING, :], ALU.add).then_inc(y_added[(e - 1) // 2], 1)

            def h_low(n, p):
                pool.wait_ge(h_full_set[n // FB], of_block(n, p))
                pool.tensor_tensor(h_lo[:, n % H_RING, :], h_full[:, n % FULL_RING, :],
                                   h_hi[:, n % H_RING, :].bitcast(F32), ALU.subtract).then_inc(h_lo_set[n // FB], 1)

            def add_inputs(g):
                pool.wait_ge(ot_set, g + 1)
                pool.tensor_tensor(ox[:], ot_pairs[:, :, 1:1 + P], xgroup(g)[:, :, 1:1 + P], ALU.add).then_inc(ox_set, 1)

            def k_rows(g):
                if not isinstance(g, int) or g >= 1:
                    pool.wait_ge(upd_mm, g)
                pool.wait_ge(krow_set, g // STAT_G + 1 if isinstance(g, int) else STAT_STEPS)
                src = krow[:, g, :] if isinstance(g, int) else krow[:, bass.ds(g, 1), :].rearrange("p o c -> p (o c)")
                pool.tensor_tensor(kcur[:], src.bitcast(F32), c_one[:], ALU.mult).then_inc(kcur_set, 1)

            def norm_root(g):
                wait_event(pool, norm_step, NORM_IN, NORM_STEPS, g)
                pool.tensor_tensor(nrm[1][:], nrm[0][:], c_root[:], ALU.pow).then_inc(norm_step[NORM_ROOT // 2], 1)

            def lower_ties(g):
                wait_event(pool, rank_step, R_TIES, RANK_STEPS, g)
                pool.tensor_tensor(ties[:].rearrange("p q e f -> p q (e f)"), ties[:].rearrange("p q e f -> p q (e f)"),
                                   lower.unsqueeze(1).to_broadcast([P, TILES, E * E]), ALU.mult).then_inc(rank_step[R_LOWER // 2], 1)

            def ahead(g):
                wait_event(pool, rank_step, R_LOWER, RANK_STEPS, g)
                pool.tensor_tensor(beats[:].rearrange("p q e f -> p (q e f)"), beats[:].rearrange("p q e f -> p (q e f)"),
                                   ties[:].rearrange("p q e f -> p (q e f)"), ALU.add).then_inc(rank_step[R_BEATS // 2], 1)

            token_norms(0)
            add_inputs(0)
            token_norms(1)
            token_norms(2)
            power(0, 0)
            token_norms(3)
            k_rows(0)
            split_w1(0, 1)
            power(1, 0)
            norm_root(0)
            split_w1(1, 3)
            lower_ties(0)
            ahead(0)
            add_inputs(1)
            split_w1(3, 4)
            h_low(2, 0)
            split_w1(4, 5)
            k_rows(1)
            split_w1(5, 6)
            power(0, 1)
            h_low(4, 0)
            h_low(6, 0)
            y_add(1, 0, 0)
            h_low(8, 0)
            split_w1(6, 8)
            power(1, 1)
            y_add(2, 0, 0)
            h_low(10, 0)
            norm_root(1)
            lower_ties(1)
            ahead(1)
            h_low(12, 0)
            y_add(3, 0, 0)
            y_add(4, 0, 0)
            y_add(5, 0, 0)
            y_add(6, 0, 0)

            def body(p, parity):
                g = p + 1
                c, u = chained(p), chained(p) and updated(p)
                h_low(2, p)
                if c:
                    add_inputs(g)
                h_low(4, p)
                y_add(7, p - 1, 1 - parity)
                if c:
                    power(0, g)
                if u:
                    k_rows(g)
                h_low(6, p)
                h_low(8, p)
                y_add(1, p, parity)
                h_low(10, p)
                y_add(2, p, parity)
                if c:
                    power(1, g)
                y_add(3, p, parity)
                power(2, p - 1)
                if u:
                    norm_root(g)
                h_low(12, p)
                y_add(4, p, parity)
                if c:
                    lower_ties(g)
                    ahead(g)
                y_add(5, p, parity)
                y_add(6, p, parity)

            loop_and_after(pool, body)
            power(2, G - 1)

        @block.scalar
        def _(act):
            act.dma_start(m0[:], m_init_t).then_inc(m_in, 16)
            act.dma_start(vw1[:], vg_w1t).then_inc(vg_in, 16)
            act.dma_start(vw2[:], vg_w2t).then_inc(vg_in, 16)

            def squares(i):
                act.wait_ge(x_in[i], 16)
                if i:
                    act.wait_ge(ssq_sum, i)
                act.activation(sq[:], xtok[:, i * STAT_TILES:(i + 1) * STAT_TILES, :], ACT.Square).then_inc(sq_set, 1)

            def rates(i):
                act.wait_ge(lr_mm, i + 1)
                act.wait_ge(par_set, 1)
                if i:
                    act.wait_ge(lr_sum, i)
                act.activation(rate_th[:], rate_ps[:], ACT.Tanh, scale=0.5, bias=lr_bias[:, 0:1]).then_inc(lr_tanh, 1)

            def sum_rows(i):
                act.wait_ge(kd_mm, i + 1)
                if i:
                    act.wait_ge(kd_turned, i)
                act.activation(kd_row[:], kd_row_ps, ACT.Copy).then_inc(kd_row_set, 1)

            def gates(i):
                act.wait_ge(gate_mm, i + 1)
                act.activation(gate[:, kpart(i)], gate_ps, ACT.Tanh, scale=0.5, bias=lr_bias[:, 1:2]).then_inc(gate_tanh, 1)

            def split_w1(start, stop):
                for e in range(start, stop):
                    act.wait_ge(w1_in[e // (E // 2)], 16)
                    act.activation(w1_hi[:, e, :], w1[:, e, :], ACT.Copy).then_inc(w1_hi_set, 1)

            def split_w2(start, stop):
                for e in range(start, stop):
                    act.wait_ge(w2_in[e // (E // 2)], 16)
                    act.activation(w2_hi[:, e], w2[:, e], ACT.Copy).then_inc(w2_hi_set, 1)

            def gelus(n, p):
                act.wait_ge(w1_mm[n // FB], of_block(n, p))
                m, same = earlier(n, H_RING, BLOCKS)
                if same:
                    wait_event(act, w2_mm, m // FB, E, p)
                elif not (isinstance(p, int) and p == 0):
                    wait_event(act, w2_mm, m // FB, E, p - 1)
                act.activation(h_hi[:, n % H_RING, :], hp[n % H_BANKS][:], ACT.Gelu)
                m, same = earlier(n, FULL_RING, BLOCKS)
                if same:
                    act.wait_ge(h_lo_set[m // FB], of_block(FB - 1, p))
                elif not (isinstance(p, int) and p == 0):
                    act.wait_ge(h_lo_set[m // FB], of_block(FB - 1, p - 1))
                act.activation(h_full[:, n % FULL_RING, :], hp[n % H_BANKS][:], ACT.Gelu).then_inc(h_full_set[n // FB], 1)

            def normalise(i, src, dst, done, g, sums=None):
                act.wait_ge(ln_bias[i], g + 1)
                for q in range(TILES):
                    extra = {} if sums is None else {"accum_out": sums[:, q:q + 1]}
                    last = act.activation(dst[:, q, :], src[:, q, :], ACT.Identity,
                                          scale=ln[i][6][:, q:q + 1], bias=ln[i][7][:, q:q + 1], **extra)
                last.then_inc(done, 1)

            def norm_squares(batches, g):
                act.wait_ge(mt_set, g + 1)
                for b in batches:
                    last = act.activation(msq[:, b, :], mt[:, b, :], ACT.Square, accum_out=mss[:, b:b + 1])
                last.then_inc(msq_set, 1)

            def half_tanh(g):
                act.wait_ge(hid_mm, g + 1)
                act.activation(th[:], ca[:], ACT.Tanh, scale=0.5).then_inc(th_set, 1)

            def first_norm(g, parity):
                if finished(g - 1):
                    act.wait_ge(r2_set, g - 1)
                normalise(0, ca[:].rearrange("p (q c) -> p q c", q=TILES), x1[parity], x1_set, g, x1sum)

            def x1_square_sums(g, parity):
                act.wait_ge(x1_set, g + 1)
                for q in range(TILES):
                    last = act.activation(x1_junk[:, q, :], x1[parity][:, q, :], ACT.Square, accum_out=x1sq[:, q:q + 1])
                last.then_inc(x1sq_set, 1)

            def x1_high(g, parity):
                act.wait_ge(x1t_mm, g + 1)
                act.activation(x1t_hi[parity][:], cb[:], ACT.Copy).then_inc(x1t_hi_set, 1)

            def exp_tanhs(g):
                wait_event(act, logit_step, L_CENTRED, LOGIT_STEPS, g)
                act.activation(lg[7][:], lg[6][:], ACT.Tanh, scale=0.25).then_inc(exp_tanh, 1)

            squares(0)
            squares(1)
            half_tanh(0)
            squares(2)
            sum_rows(0)
            rates(0)
            squares(3)
            sum_rows(1)
            split_w1(0, 1)
            gates(0)
            split_w1(1, 2)
            gates(1)
            split_w1(2, 4)
            sum_rows(2)
            first_norm(0, 0)
            split_w2(0, 2)
            x1_high(0, 0)
            x1_square_sums(0, 0)
            split_w2(2, 3)
            sum_rows(3)
            rates(1)
            gates(2)
            split_w2(3, 4)
            norm_squares(range(HALF), 0)
            norm_squares(range(HALF, B), 0)
            gates(3)
            split_w2(4, 6)
            split_w1(4, 7)
            gelus(0, 0)
            exp_tanhs(0)
            split_w1(7, 8)
            gelus(1, 0)
            split_w2(6, 7)
            half_tanh(1)
            split_w2(7, 8)
            gelus(2, 0)
            gelus(3, 0)
            gelus(4, 0)
            gelus(5, 0)
            gelus(6, 0)
            gelus(7, 0)
            first_norm(1, 1)
            gelus(8, 0)
            x1_square_sums(1, 1)
            gelus(9, 0)
            norm_squares(range(HALF), 1)
            x1_high(1, 1)
            norm_squares(range(HALF, B), 1)
            gelus(10, 0)
            gelus(11, 0)
            gelus(12, 0)
            gelus(13, 0)
            exp_tanhs(1)
            gelus(14, 0)
            gelus(15, 0)

            def body(p, parity):
                g = p + 1
                c, u = chained(p), chained(p) and updated(p)
                gelus(0, p)
                gelus(1, p)
                gelus(2, p)
                gelus(3, p)
                if c:
                    half_tanh(g)
                gelus(4, p)
                gelus(5, p)
                gelus(6, p)
                gelus(7, p)
                gelus(8, p)
                gelus(9, p)
                if c:
                    first_norm(g, 1 - parity)
                gelus(10, p)
                if c:
                    x1_square_sums(g, 1 - parity)
                gelus(11, p)
                if u:
                    norm_squares(range(HALF), g)
                if c:
                    x1_high(g, 1 - parity)
                if u:
                    norm_squares(range(HALF, B), g)
                gelus(12, p)
                gelus(13, p)
                gelus(14, p)
                gelus(15, p)
                if c:
                    exp_tanhs(g)
                normalise(2, r2, result(p - 1), osb_set, p - 1)

            loop_and_after(act, body)
            act.wait_ge(ln_bias[2], G)
            for q in range(TILES):
                act.activation(result(G - 1)[:, q, :], r2[:, q, :], ACT.Identity,
                               scale=ln[2][6][:, q:q + 1], bias=ln[2][7][:, q:q + 1]).then_inc(osb_set, 1)

        @block.vector
        def _(dve):
            dve.wait_ge(par_in, 32)
            dve.tensor_scalar(lr_bias[:], prm[:, C_RATE_B:C_RATE_B + 2], 0.5, None, ALU.mult).then_inc(par_set, 1)
            dve.tensor_scalar(route_w[:, 0:E], prm[:, C_ROUTE:C_ROUTE + E], prm[:, C_GAMMA:C_GAMMA + 1], None, ALU.mult).then_inc(par_set, 1)
            dve.tensor_scalar(route_w[:, E:2 * E], prm[:, C_ROUTE:C_ROUTE + E], prm[:, C_BETA:C_BETA + 1], None, ALU.mult).then_inc(par_set, 1)
            dve.tensor_scalar(gate_rep[:], ones, prm[:, C_GATE_W:C_GATE_W + 1], None, ALU.mult).then_inc(par_set, 1)
            half_b = half64.unsqueeze(1).to_broadcast([P, STAT_TILES, 2])

            def token_squares(i):
                part = slice(i * STAT_TILES, (i + 1) * STAT_TILES)
                dve.wait_ge(sq_set, i + 1)
                dve.tensor_reduce(ssq[:, part], sq[:], AX_X, ALU.add).then_inc(ssq_sum, 1)
                dve.wait_ge(ssq_sum, i + 1)
                dve.tensor_scalar(ssq[:, part], ssq[:, part], NORM_EPS ** 2, None, ALU.max).then_inc(ssq_set, 1)

            def token_weights(i):
                part = slice(i * STAT_TILES, (i + 1) * STAT_TILES)
                dve.wait_ge(const_set, 6)
                if i >= 2:
                    dve.wait_ge(kd_mm, i - 1)
                dve.wait_ge(inv_set, i + 1)
                dve.tensor_tensor(kdw[i % 2][:, :, 0:2], inv[:, part].unsqueeze(2).to_broadcast([P, STAT_TILES, 2]), half_b,
                                  ALU.mult).then_inc(kd_half, 1)
                dve.wait_ge(kd_half, i + 1)
                dve.tensor_tensor(kdw[i % 2][:, :, 2:4], half_b, kdw[i % 2][:, :, 0:2], ALU.subtract).then_inc(kdw_set, 1)

            def means(i):
                groups = slice(i * STAT_G, (i + 1) * STAT_G)
                sums = kd_ps.rearrange("p (t w) -> p t w", w=KD_ROWS)
                dve.wait_ge(kd_turned, i + 1)
                dve.tensor_copy(km[:, kpart(i)].rearrange("p (t h) -> p t h", h=2), sums[:, :, 0:2]).then_inc(km_copy, 1)
                dve.wait_ge(xt_in[i], 16)
                if i == 0:
                    dve.wait_ge(out_mm, 1)
                dve.tensor_copy(xt[:, groups].rearrange("p t q c -> p (t q) c")[:, :, 0:PAIR:PAIR - 1], sums[:, :, 2:4]).then_inc(km_set, 1)

            def split_k(i):
                groups = slice(i * STAT_G, (i + 1) * STAT_G)
                k = km[:, kpart(i)].rearrange("p (t b) -> p t b", b=B)
                dve.wait_ge(km_copy, i + 1)
                for j in (0, 2):
                    last = dve.tensor_copy(kb[:, groups, j, :], k)
                last.then_inc(k_hi, 1)
                dve.wait_ge(k_hi, i + 1)
                dve.tensor_tensor(kb[:, groups, 1, :], k, kb[:, groups, 0, :].bitcast(F32), ALU.subtract).then_inc(kb_set, 1)

            def sum_rates(i):
                dve.wait_ge(lr_tanh, i + 1)
                dve.tensor_reduce(rate_sum[:], rate_th[:].rearrange("p (b c) -> p b c", c=CHUNK), AX_X, ALU.add).then_inc(lr_sum, 1)

            def mask_rates(i):
                dve.wait_ge(lr_sum, i + 1)
                if i:
                    dve.wait_ge(lr_mean, i)
                dve.tensor_tensor(rate_mask[:], rate_sum[:].unsqueeze(1).to_broadcast([P, 2 * RATE_G, B]),
                                  own_rate.unsqueeze(2).to_broadcast([P, 2 * RATE_G, B]), ALU.mult).then_inc(lr_masked, 1)

            def k_rows(i):
                dve.wait_ge(krow_mm, i + 1)
                dve.tensor_copy(krow[:, i * STAT_G:(i + 1) * STAT_G, :], krow_ps.rearrange("p (t c) -> p t c", c=P)).then_inc(krow_set, 1)

            def coefficients(i):
                part = slice(i * RATE_G * B, (i + 1) * RATE_G * B)
                dve.wait_ge(lr_mean, i + 1)
                dve.tensor_scalar(eta[:, part], mean_ps[:, 0, :], MAX_LR / 2, MAX_LR / 2, ALU.mult, ALU.add)
                dve.tensor_scalar(alpha[:, part], mean_ps[:, 1, :], (1 - MIN_DECAY) / 2, (MIN_DECAY - 1) / 2, ALU.mult, ALU.add)
                dve.wait_ge(gate_tanh, (i + 1) * RATE_G // STAT_G)
                dve.tensor_scalar(gate[:, part], gate[:, part], 0.5, 0.5, ALU.mult, ALU.add).then_inc(coef_in, 1)
                dve.wait_ge(coef_in, i + 1)
                dve.tensor_tensor(decay[:, part], gate[:, part], alpha[:, part], ALU.mult)
                dve.tensor_tensor(lrate[:, part], gate[:, part], eta[:, part], ALU.mult).then_inc(coef_mult, 1)
                dve.wait_ge(coef_mult, i + 1)
                dve.tensor_scalar(decay[:, part], decay[:, part], 1.0, None, ALU.add).then_inc(coef_set, 1)

            def split_w2(start, stop):
                for e in range(start, stop):
                    dve.wait_ge(w2_hi_set, e + 1)
                    dve.tensor_tensor(w2_lo[:, e], w2[:, e], w2_hi[:, e].bitcast(F32), ALU.subtract).then_inc(w2_lo_set, 1)

            def h_low(n, p):
                dve.wait_ge(h_full_set[n // FB], of_block(n, p))
                dve.tensor_tensor(h_lo[:, n % H_RING, :], h_full[:, n % FULL_RING, :],
                                  h_hi[:, n % H_RING, :].bitcast(F32), ALU.subtract).then_inc(h_lo_set[n // FB], 1)

            def weigh(e, p, parity):
                wait_event(dve, w2_mm, e, E, p)
                if e % COMB_E == 0:
                    dve.wait_ge(comb_in[e // COMB_E], p * 16 + 16)
                if e:
                    m, same = earlier(e - 1, YM_RING, E - 1)
                    if same:
                        wait_event(dve, y_added, m, E - 1, p)
                    elif not (isinstance(p, int) and p == 0):
                        wait_event(dve, y_added, m, E - 1, p - 1)
                dst = ym[:, (e - 1) % YM_RING, :] if e else acc[parity][:]
                dve.tensor_tensor(dst, yp[e % Y_BANKS][:], combb[parity][:, e, :], ALU.mult).then_inc(y_weighted[e // 2], 1)

            def row_stats(i, src, g):
                for q in range(TILES):
                    last = dve.bn_stats(st[i][:, q, :], src[:, q, :])
                last.then_inc(ln_step[i], 1)

            def row_sums(i, g):
                wait_event(dve, [ln_step[i]], 0, 2, g)
                dve.tensor_tensor(ln[i][0][:], st[i][:, :, 1], st[i][:, :, 4], ALU.add)
                dve.tensor_tensor(ln[i][1][:], st[i][:, :, 1], st[i][:, :, 4], ALU.subtract)
                dve.tensor_tensor(ln[i][2][:], st[i][:, :, 2], st[i][:, :, 5], ALU.add).then_inc(ln_step[i], 1)

            def row_squares(i, g):
                wait_event(dve, [ln_step[i]], 1, 2, g)
                dve.scalar_tensor_tensor(out=ln[i][3][:], in0=ln[i][1][:], scalar=0.25, in1=ln[i][1][:],
                                         op0=ALU.mult, op1=ALU.mult)
                dve.tensor_scalar(ln[i][4][:], ln[i][2][:], 1.0 / D, LN_EPS, ALU.mult, ALU.add).then_inc(ln_sq[i], 1)

            def row_variance(i, g):
                dve.wait_ge(ln_sq[i], g + 1)
                dve.tensor_tensor(ln[i][5][:], ln[i][4][:], ln[i][3][:], ALU.add).then_inc(ln_var[i], 1)

            def x1_squares(g):
                dve.wait_ge(x1sq_set, g + 1)
                dve.scalar_tensor_tensor(out=ln[1][3][:], in0=x1sum[:], scalar=-1.0 / (D * D), in1=x1sum[:],
                                         op0=ALU.mult, op1=ALU.mult)
                dve.tensor_scalar(ln[1][4][:], x1sq[:], 1.0 / D, LN_EPS, ALU.mult, ALU.add).then_inc(ln_sq[1], 1)

            def shift(i, g):
                dve.wait_ge(ln_rstd[i], g + 1)
                dve.scalar_tensor_tensor(out=ln[i][7][:], in0=ln[i][0][:], scalar=-0.5, in1=ln[i][6][:],
                                         op0=ALU.mult, op1=ALU.mult).then_inc(ln_bias[i], 1)

            def tile_b(t):
                return t[:].unsqueeze(2).to_broadcast([P, TILES, E])

            def expert_b(t):
                return t.unsqueeze(1).to_broadcast([P, TILES, E])

            def logit(step, g):
                after = {L_BETA: None, L_RSTD: L_MEAN, L_ESUM: L_EXP}.get(step, step - 1)
                if step == L_BETA:
                    dve.wait_ge(logit_mm, g + 1)
                elif step == L_RSTD:
                    dve.wait_ge(ln_rstd[1], g + 1)
                elif step == L_DOWN:
                    dve.wait_ge(exp_tanh, g + 1)
                if after is not None and step != L_DOWN:
                    wait_event(dve, logit_step, after, LOGIT_STEPS, g)
                if step == L_BETA:
                    dve.tensor_tensor(lg[2][:], tile_b(x1sum), expert_b(route_s[:, 0:E]), ALU.mult)
                    op = dve.tensor_copy(lg[0][:], logit_ps[:, :, E:2 * E])
                elif step == L_SUM:
                    op = dve.tensor_tensor(lg[1][:], logit_ps[:, :, 0:E], lg[0][:], ALU.add)
                elif step == L_MEAN:
                    op = dve.scalar_tensor_tensor(out=lg[3][:], in0=lg[2][:], scalar=-1.0 / D, in1=lg[1][:], op0=ALU.mult, op1=ALU.add)
                elif step == L_RSTD:
                    op = dve.tensor_tensor(lg[4][:], lg[3][:], tile_b(ln[1][6]), ALU.mult)
                elif step == L_LOGIT:
                    op = dve.tensor_tensor(lg[5][:], lg[4][:], expert_b(route_s[:, E:2 * E]), ALU.add)
                elif step == L_MAX:
                    op = dve.tensor_reduce(lmax[:], lg[5][:], AX_X, ALU.max)
                elif step == L_CENTRED:
                    op = dve.tensor_tensor(lg[6][:], lg[5][:], tile_b(lmax), ALU.subtract)
                elif step == L_DOWN:
                    op = dve.tensor_scalar(lg[8][:], lg[7][:], -1.0, 1.0, ALU.mult, ALU.add)
                elif step == L_INV:
                    op = dve.reciprocal(lg[9][:], lg[8][:])
                elif step == L_RATIO:
                    op = dve.scalar_tensor_tensor(out=lg[10][:], in0=lg[7][:], scalar=1.0, in1=lg[9][:], op0=ALU.add, op1=ALU.mult)
                elif step == L_EXP:
                    op = dve.tensor_tensor(lg[11][:], lg[10][:], lg[10][:], ALU.mult)
                elif step == L_ESUM:
                    op = dve.tensor_reduce(esum[:], lg[11][:], AX_X, ALU.add)
                else:
                    op = dve.reciprocal(einv[:], esum[:])
                op.then_inc(logit_step[step // 2], 1)

            def compare(g):
                own = lg[5][:].unsqueeze(3).to_broadcast([P, TILES, E, E])
                other = lg[5][:].unsqueeze(2).to_broadcast([P, TILES, E, E])
                wait_event(dve, logit_step, L_LOGIT, LOGIT_STEPS, g)
                dve.tensor_tensor(beats[:], other, own, ALU.is_gt)
                dve.tensor_tensor(ties[:], other, own, ALU.is_equal).then_inc(rank_step[R_TIES // 2], 1)

            def rank_sum(g):
                wait_event(dve, rank_step, R_BEATS, RANK_STEPS, g)
                dve.tensor_reduce(rank[:], beats[:], AX_X, ALU.add).then_inc(rank_step[R_RANK // 2], 1)

            def keep_two(g):
                wait_event(dve, logit_step, L_EXP, LOGIT_STEPS, g)
                wait_event(dve, rank_step, R_RANK, RANK_STEPS, g)
                dve.scalar_tensor_tensor(out=lg[12][:], in0=rank[:], scalar=2.0, in1=lg[11][:], op0=ALU.is_lt,
                                         op1=ALU.mult).then_inc(rank_step[R_KEEP // 2], 1)

            def routing(g):
                wait_event(dve, logit_step, L_EINV, LOGIT_STEPS, g)
                wait_event(dve, rank_step, R_KEEP, RANK_STEPS, g)
                dve.tensor_tensor(comb[:].rearrange("p e q -> p q e"), lg[12][:], tile_b(einv), ALU.mult).then_inc(comb_set, 1)

            def norm(step, g):
                if step == NORM_IN:
                    dve.wait_ge(ss_mm, g + 1)
                    op = dve.tensor_copy(nrm[0][:], ss_ps)
                else:
                    wait_event(dve, norm_step, step - 1, NORM_STEPS, g)
                if step == NORM_MULT:
                    op = dve.tensor_tensor(nrm[2][:], nrm[1][:], scale_d[:], ALU.mult)
                elif step == NORM_ADD:
                    op = dve.tensor_scalar(nrm[3][:], nrm[2][:], 1e-6, None, ALU.add)
                elif step == NORM_INV:
                    op = dve.reciprocal(nrm[4][:], nrm[3][:])
                elif step == NORM_MIN:
                    op = dve.tensor_scalar(nrm[5][:], nrm[4][:], MAX_NORM, 1.0, ALU.mult, ALU.min)
                elif step == SCALE:
                    op = dve.tensor_tensor(scale[:], nrm[5][:], scale_d[:], ALU.mult)
                op.then_inc(norm_step[step // 2], 1)

            def decayed_scale(g):
                if isinstance(g, int) and g == 0:
                    dve.wait_ge(const_set, 6)
                    dve.wait_ge(coef_set, 1)
                else:
                    wait_event(dve, norm_step, SCALE, NORM_STEPS, g - 1)
                dve.tensor_tensor(scale_d[:], group(decay, g), scale[:], ALU.mult).then_inc(sd_set, 1)

            def inverse_scale(g):
                dve.wait_ge(sd_set, g + 1)
                dve.reciprocal(scale_i[:], scale_d[:]).then_inc(si_set, 1)

            def error_scale(g):
                dve.wait_ge(si_set, g + 1)
                dve.tensor_tensor(err_scale[:], group(lrate, g), scale_i[:], ALU.mult).then_inc(es_set, 1)

            def scaled_outputs(g):
                dve.wait_ge(out_mm, g + 1)
                if isinstance(g, int) and g == 0:
                    dve.wait_ge(const_set, 6)
                else:
                    wait_event(dve, norm_step, SCALE, NORM_STEPS, g - 1)
                for i, bank in enumerate(halves):
                    part = slice(i * HALF, (i + 1) * HALF)
                    last = dve.tensor_tensor(ot[:, part, :], bank[:, 0:HALF * AUG].rearrange("p (b c) -> p b c", c=AUG),
                                             scale[:, part].unsqueeze(2).to_broadcast([P, HALF, AUG]), ALU.mult)
                last.then_inc(ot_set, 1)

            def split_router():
                dve.wait_ge(par_set, 4)
                dve.tensor_copy(route_r[:, 0:E], route_w[:, 0:E]).then_inc(par_set, 1)
                dve.wait_ge(start_mm, 1)
                dve.tensor_copy(route_s[:], route_ps)
                dve.wait_ge(vg_in, 32)
                dve.tensor_scalar(vw2h[:], vw2[:], 0.5, None, ALU.mult).then_inc(par_set, 1)
                dve.wait_ge(par_set, 5)
                dve.tensor_tensor(route_r[:, E:2 * E], route_w[:, 0:E], route_r[:, 0:E].bitcast(F32), ALU.subtract).then_inc(par_set, 1)

            def comb_rows(p):
                dve.wait_ge(combt_mm, p + 1)
                if finished(p):
                    dve.wait_ge(comb_out, p * 16)
                dve.tensor_copy(combt[:], combt_ps).then_inc(combt_set, 1)

            def silus(g):
                dve.wait_ge(th_set, g + 1)
                dve.scalar_tensor_tensor(out=hid[:], in0=th[:], scalar=1.0, in1=ca[:], op0=ALU.add, op1=ALU.mult).then_inc(hid_set, 1)

            def silu_sums(g):
                dve.wait_ge(hid_set, g + 1)
                dve.tensor_reduce(hsum[:], hid[:].rearrange("p (b c) -> p b c", c=CHUNK), AX_X, ALU.add).then_inc(hsum_set, 1)

            def memory_residual(g):
                dve.wait_ge(val_mm, g + 1)
                dve.wait_ge(ox_set, g + 1)
                dve.tensor_tensor(rt[:], cb[:], ox[:].rearrange("p q c -> p (q c)"), ALU.add).then_inc(rt_set, 1)

            def mean_outputs():
                dve.wait_ge(ot_set, 1)
                dve.wait_ge(start_mm, 2)
                dve.tensor_copy(ot_pairs[:, :, 0:PAIR:PAIR - 1], err_ps.rearrange("p (q h) -> p q h", h=2)).then_inc(d_set, 1)

            def errors(g):
                if isinstance(g, int) and g == 0:
                    dve.wait_ge(d_set, 1)
                dve.wait_ge(err_mm, g + 1)
                dve.scalar_tensor_tensor(out=err[:].rearrange("p (q h) -> p q h", h=2), in0=err_ps.rearrange("p (q h) -> p q h", h=2),
                                         scalar=1.0 / CHUNK, in1=ot_pairs[:, :, 0:PAIR:PAIR - 1],
                                         op0=ALU.mult, op1=ALU.add).then_inc(err_sum, 1)

            def error_high(g):
                dve.wait_ge(err_sum, g + 1)
                dve.wait_ge(es_set, g + 1)
                dve.tensor_tensor(err_f[:], err[:], err_scale[:], ALU.mult)
                dve.tensor_tensor(err_r[:, 0:2, :], err[:].unsqueeze(1).to_broadcast([P, 2, B]),
                                  err_scale[:].unsqueeze(1).to_broadcast([P, 2, B]), ALU.mult).then_inc(err_hi, 1)

            def error_low(g):
                dve.wait_ge(err_hi, g + 1)
                dve.tensor_tensor(err_r[:, 2, :], err_f[:], err_r[:, 0, :].bitcast(F32), ALU.subtract).then_inc(err_set, 1)

            def error_rows(g):
                dve.wait_ge(errt_mm, g + 1)
                dve.tensor_tensor(err_row[:], errt_ps.unsqueeze(1).to_broadcast([ROWS, B, P]),
                                  own_batch.unsqueeze(2).to_broadcast([ROWS, B, P]), ALU.mult).then_inc(err_row_set, 1)

            def expert_residual(p, parity):
                dve.wait_ge(fin_mm, p + 1)
                if not isinstance(p, int) or p >= 1:
                    dve.wait_ge(osb_set, p)
                dve.tensor_tensor(r2[:], cb[:].rearrange("p (q c) -> p q c", q=TILES), x1[parity][:], ALU.add).then_inc(r2_set, 1)

            def r2_stats(p):
                dve.wait_ge(r2_set, p + 1)
                row_stats(2, r2, p)

            def r_stats(g):
                dve.wait_ge(r_mm, g + 1)
                row_stats(0, ca[:].rearrange("p (q c) -> p q c", q=TILES), g)

            def new_memory(g):
                dve.wait_ge(upd_mm, g + 1)
                for i, bank in enumerate(halves):
                    part = slice(i * HALF, (i + 1) * HALF)
                    before = m0[:].unsqueeze(1).to_broadcast([P, HALF, D]) if isinstance(g, int) and g == 0 else mt[:, part, :]
                    last = dve.tensor_tensor(mt[:, part, :], bank[:].rearrange("p (b c) -> p b c", c=D), before, ALU.add)
                last.then_inc(mt_set, 1)

            def x1_low(g, parity):
                dve.wait_ge(x1t_hi_set, g + 1)
                dve.tensor_tensor(x1t_lo[parity][:], cb[:], x1t_hi[parity][:].bitcast(F32), ALU.subtract).then_inc(x1t_lo_set, 1)

            token_squares(0)
            split_router()
            scaled_outputs(0)
            token_weights(0)
            token_squares(1)
            silus(0)
            silu_sums(0)
            token_squares(2)
            memory_residual(0)
            means(0)
            sum_rates(0)
            token_weights(1)
            r_stats(0)
            token_squares(3)
            row_sums(0, 0)
            mask_rates(0)
            means(1)
            row_squares(0, 0)
            token_weights(2)
            row_variance(0, 0)
            mean_outputs()
            split_k(0)
            coefficients(0)
            shift(0, 0)
            decayed_scale(0)
            inverse_scale(0)
            errors(0)
            error_scale(0)
            k_rows(0)
            error_high(0)
            error_low(0)
            means(2)
            split_k(1)
            token_weights(3)
            error_rows(0)
            x1_low(0, 0)
            split_k(2)
            k_rows(1)
            new_memory(0)
            x1_squares(0)
            means(3)
            split_w2(0, 1)
            split_k(3)
            k_rows(2)
            sum_rates(1)
            row_variance(1, 0)
            mask_rates(1)
            split_w2(1, 2)
            norm(NORM_IN, 0)
            coefficients(1)
            k_rows(3)
            split_w2(2, 3)
            logit(L_BETA, 0)
            norm(NORM_MULT, 0)
            logit(L_SUM, 0)
            norm(NORM_ADD, 0)
            logit(L_MEAN, 0)
            logit(L_RSTD, 0)
            norm(NORM_INV, 0)
            logit(L_LOGIT, 0)
            norm(NORM_MIN, 0)
            logit(L_MAX, 0)
            norm(SCALE, 0)
            logit(L_CENTRED, 0)
            scaled_outputs(1)
            logit(L_DOWN, 0)
            compare(0)
            logit(L_INV, 0)
            logit(L_RATIO, 0)
            h_low(0, 0)
            decayed_scale(1)
            logit(L_EXP, 0)
            logit(L_ESUM, 0)
            silus(1)
            rank_sum(0)
            logit(L_EINV, 0)
            keep_two(0)
            h_low(1, 0)
            routing(0)
            memory_residual(1)
            inverse_scale(1)
            comb_rows(0)
            silu_sums(1)
            error_scale(1)
            r_stats(1)
            row_sums(0, 1)
            row_squares(0, 1)
            row_variance(0, 1)
            errors(1)
            h_low(3, 0)
            error_high(1)
            error_low(1)
            shift(0, 1)
            h_low(5, 0)
            error_rows(1)
            split_w2(3, 4)
            weigh(0, 0, 0)
            weigh(1, 0, 0)
            h_low(7, 0)
            new_memory(1)
            split_w2(4, 5)
            x1_squares(1)
            h_low(9, 0)
            weigh(2, 0, 0)
            row_variance(1, 1)
            weigh(3, 0, 0)
            x1_low(1, 1)
            split_w2(5, 6)
            norm(NORM_IN, 1)
            weigh(4, 0, 0)
            split_w2(6, 7)
            logit(L_BETA, 1)
            logit(L_SUM, 1)
            logit(L_MEAN, 1)
            logit(L_RSTD, 1)
            logit(L_LOGIT, 1)
            logit(L_MAX, 1)
            compare(1)
            logit(L_CENTRED, 1)
            h_low(11, 0)
            logit(L_DOWN, 1)
            norm(NORM_MULT, 1)
            logit(L_INV, 1)
            logit(L_RATIO, 1)
            h_low(13, 0)
            logit(L_EXP, 1)
            rank_sum(1)
            logit(L_ESUM, 1)
            logit(L_EINV, 1)
            keep_two(1)
            routing(1)
            split_w2(7, 8)
            weigh(5, 0, 0)
            norm(NORM_ADD, 1)
            norm(NORM_INV, 1)
            norm(NORM_MIN, 1)
            h_low(14, 0)
            norm(SCALE, 1)
            h_low(15, 0)
            weigh(6, 0, 0)

            def body(p, parity):
                g = p + 1
                c, u = chained(p), chained(p) and updated(p)
                if c:
                    scaled_outputs(g)
                if u:
                    decayed_scale(g)
                comb_rows(p)
                h_low(0, p)
                h_low(1, p)
                weigh(7, p - 1, 1 - parity)
                if c:
                    silus(g)
                if u:
                    inverse_scale(g)
                h_low(3, p)
                if u:
                    silu_sums(g)
                if c:
                    memory_residual(g)
                h_low(5, p)
                if c:
                    r_stats(g)
                    row_sums(0, g)
                if u:
                    error_scale(g)
                if c:
                    row_squares(0, g)
                    row_variance(0, g)
                weigh(0, p, parity)
                expert_residual(p - 1, 1 - parity)
                if c:
                    shift(0, g)
                if u:
                    errors(g)
                    error_high(g)
                    error_low(g)
                weigh(1, p, parity)
                if u:
                    error_rows(g)
                h_low(7, p)
                weigh(2, p, parity)
                if u:
                    new_memory(g)
                if c:
                    x1_squares(g)
                r2_stats(p - 1)
                if c:
                    row_variance(1, g)
                weigh(3, p, parity)
                row_sums(2, p - 1)
                h_low(9, p)
                row_squares(2, p - 1)
                h_low(11, p)
                row_variance(2, p - 1)
                if c:
                    x1_low(g, 1 - parity)
                if u:
                    norm(NORM_IN, g)
                weigh(4, p, parity)
                weigh(5, p, parity)
                if c:
                    logit(L_BETA, g)
                h_low(13, p)
                if c:
                    logit(L_SUM, g)
                if u:
                    norm(NORM_MULT, g)
                if c:
                    logit(L_MEAN, g)
                shift(2, p - 1)
                if u:
                    norm(NORM_ADD, g)
                if c:
                    logit(L_RSTD, g)
                    logit(L_LOGIT, g)
                if u:
                    norm(NORM_INV, g)
                if c:
                    logit(L_MAX, g)
                    compare(g)
                    logit(L_CENTRED, g)
                h_low(14, p)
                if c:
                    logit(L_DOWN, g)
                h_low(15, p)
                if c:
                    logit(L_INV, g)
                weigh(6, p, parity)
                if c:
                    logit(L_RATIO, g)
                if u:
                    norm(NORM_MIN, g)
                if c:
                    logit(L_EXP, g)
                    rank_sum(g)
                if u:
                    norm(SCALE, g)
                if c:
                    logit(L_ESUM, g)
                    logit(L_EINV, g)
                    keep_two(g)
                    routing(g)

            loop_and_after(dve, body)
            weigh(7, G - 1, (G - 1) % 2)
            wait_event(dve, y_weighted, E - 1, E, G - 1)
            dve.tensor_tensor(ym[:, (E - 2) % YM_RING, :], ym[:, (E - 2) % YM_RING, :], ym[:, (E - 3) % YM_RING, :],
                              ALU.add).then_inc(y_weighted[-1], 1)
            expert_residual(G - 1, (G - 1) % 2)
            dve.wait_ge(fin_mm, G + 1)
            dve.wait_ge(r2_set, G)
            dve.tensor_tensor(r2[:], ca[:].rearrange("p (q c) -> p q c", q=TILES), r2[:], ALU.add).then_inc(r2_set, 1)
            dve.wait_ge(r2_set, G + 1)
            row_stats(2, r2, G - 1)
            row_sums(2, G - 1)
            row_squares(2, G - 1)
            row_variance(2, G - 1)
            shift(2, G - 1)

        @block.tensor
        def _(pe):
            def router_sums():
                pe.wait_ge(par_set, 4)
                pe.matmul(route_ps, ones, route_w[:], start=True, stop=True).then_inc(start_mm, 1)

            def outputs(g):
                if isinstance(g, int) and g == 0:
                    pe.wait_ge(m_in, 16)
                    pe.wait_ge(xt_in[0], 16)
                    for i in range(2):
                        last = pe.matmul(halves[i][:, 0:HALF * AUG], m0[:], xt[:, 0, i * TILES // 2:(i + 1) * TILES // 2, :], start=True, stop=True)
                    last.then_inc(out_mm, 1)
                    return
                pe.wait_ge(x1t_lo_set, g)
                pe.wait_ge(mt_set, g)
                for b in range(B):
                    dst = halves[b // HALF][:, (b % HALF) * AUG:(b % HALF + 1) * AUG]
                    last = pe.matmul(dst, mt[:, b, :], xgroup(g)[:, b // 2, b % 2 * AUG:(b % 2 + 1) * AUG], start=True, stop=True)
                last.then_inc(out_mm, 1)

            def mean_outputs():
                pe.wait_ge(m_in, 16)
                pe.wait_ge(km_set, 1)
                pe.wait_ge(par_set, 6)
                pe.matmul(err_ps, m0[:], xt[:, 0, :, 0:PAIR:PAIR - 1], start=True, stop=True).then_inc(start_mm, 1)

            def hidden(g):
                if isinstance(g, int) and g == 0:
                    pe.wait_ge(vg_in, 32)
                pe.wait_ge(ot_set, g + 1)
                pe.matmul(ca[:], vw1[:], ot_pairs[:, :, 1:1 + P], start=True, stop=True).then_inc(hid_mm, 1)

            def value(g):
                if isinstance(g, int) and g == 0:
                    pe.wait_ge(par_set, 6)
                pe.wait_ge(hid_set, g + 1)
                pe.matmul(cb[:], vw2h[:], hid[:], start=True, stop=True).then_inc(val_mm, 1)

            def turn_r(g):
                pe.wait_ge(rt_set, g + 1)
                for q in range(TILES):
                    last = pe.transpose(ca[:, q * P:(q + 1) * P], rt[:, q * P:(q + 1) * P], ident)
                last.then_inc(r_mm, 1)

            def error(g):
                if isinstance(g, int) and g <= 1:
                    pe.wait_ge(combt_set if g == 1 else d_set, 1)
                pe.wait_ge(hsum_set, g + 1)
                pe.matmul(err_ps, vw2h[:], hsum[:], start=True, stop=True).then_inc(err_mm, 1)

            def turn_error(g):
                pe.wait_ge(err_set, g + 1)
                pe.transpose(errt_ps, err_r[:].rearrange("p j b -> p (j b)").bitcast(F32), ident).then_inc(errt_mm, 1)

            def turn_x1(g, parity):
                if isinstance(g, int) and g == 0:
                    pe.wait_ge(rt_set, 1)
                elif updated(g - 1):
                    pe.wait_ge(mt_set, g + 1)
                else:
                    pe.wait_ge(r2_set, g - 1)
                pe.wait_ge(x1_set, g + 1)
                for q in range(TILES):
                    last = pe.transpose(cb[:, q * P:(q + 1) * P], x1[parity][:, q, :], ident)
                last.then_inc(x1t_mm, 1)

            def route(g, parity):
                if isinstance(g, int) and g == 0:
                    pe.wait_ge(par_set, 7)
                pe.wait_ge(x1t_lo_set, g + 1)
                if updated(g - 1):
                    wait_event(pe, norm_step, NORM_IN, NORM_STEPS, g)
                for q in range(TILES):
                    part = slice(q * P, (q + 1) * P)
                    pe.matmul(logit_ps[:, q, :], x1t_hi[parity][:, part], route_r[:], start=True, stop=False)
                    last = pe.matmul(logit_ps[:, q, 0:E], x1t_lo[parity][:, part], route_r[:, 0:E], start=False, stop=True)
                last.then_inc(logit_mm, 1)

            def update(g):
                pe.wait_ge(kcur_set, g + 1)
                if finished(g - 1):
                    pe.wait_ge(r2_set, g - 1)
                pe.wait_ge(x1_set, g + 1)
                if isinstance(g, int) and g == 0:
                    pe.wait_ge(x1t_lo_set, 1)
                pe.wait_ge(err_row_set, g + 1)
                for i, bank in enumerate(halves):
                    src = err_row[:, i * HALF:(i + 1) * HALF, :].rearrange("p b c -> p (b c)")
                    last = pe.matmul(bank[:], kcur[:], src, start=True, stop=True)
                last.then_inc(upd_mm, 1)

            def norm(g):
                wait_event(pe, [msq_set], 1, 2, g)
                pe.wait_ge(err_row_set, g + 1)
                pe.matmul(ss_ps, ones, mss[:], start=True, stop=True).then_inc(ss_mm, 1)

            def turn_comb(g):
                pe.wait_ge(comb_set, g + 1)
                pe.transpose(combt_ps, comb[:].rearrange("p e q -> p (e q)"), ident).then_inc(combt_mm, 1)

            def finish(p, parity):
                wait_event(pe, y_added, E - 2, E - 1, p)
                for q in range(TILES):
                    last = pe.transpose(cb[:, q * P:(q + 1) * P], acc[parity][:, q * P:(q + 1) * P], ident)
                last.then_inc(fin_mm, 1)

            def first(n, p, parity):
                e, k = divmod(n, FB)
                if isinstance(p, int) and p == 0 and k == 0:
                    pe.wait_ge(w1_lo_set, e + 1)
                    if e == 0:
                        pe.wait_ge(x1t_lo_set, 1)
                if isinstance(p, int) and p == 0 and n < H_BANKS:
                    done, count = ((coef_in, RATE_STEPS), (gate_tanh, STAT_STEPS), (krow_set, STAT_STEPS))[n]
                    pe.wait_ge(done, count)
                part = slice(k * P, (k + 1) * P)
                wait_earlier_block(pe, h_full_set, n, H_BANKS, p)
                pe.matmul(hp[n % H_BANKS][:], w1_hi[:, e, part], x1t_hi[parity][:], start=True, stop=False)
                pe.matmul(hp[n % H_BANKS][:], w1_lo[:, e, part], x1t_hi[parity][:], start=False, stop=False)
                pe.matmul(hp[n % H_BANKS][:], w1_hi[:, e, part], x1t_lo[parity][:], start=False, stop=True).then_inc(w1_mm[e], 1)

            def second_high(e, p):
                if isinstance(p, int) and p == 0:
                    pe.wait_ge(w2_lo_set, e + 1)
                    if e < Y_BANKS:
                        done, count = ((km_set, STAT_STEPS), (lr_tanh, RATE_STEPS))[e]
                        pe.wait_ge(done, count)
                m, same = earlier(e, Y_BANKS, E)
                if same:
                    wait_event(pe, y_weighted, m, E, p)
                elif not (isinstance(p, int) and p == 0):
                    wait_event(pe, y_weighted, m, E, p - 1)
                for k in range(FB):
                    n = FB * e + k
                    pe.wait_ge(h_full_set[e], of_block(n, p))
                    pe.matmul(yp[e % Y_BANKS][:], w2_hi[:, e, k, :], h_hi[:, n % H_RING, :], start=(k == 0), stop=False)
                    pe.matmul(yp[e % Y_BANKS][:], w2_lo[:, e, k, :], h_hi[:, n % H_RING, :], start=False, stop=False)

            def second_low(e, p):
                pe.wait_ge(h_lo_set[e], of_block(FB - 1, p))
                for k in range(FB):
                    last = pe.matmul(yp[e % Y_BANKS][:], w2_hi[:, e, k, :], h_lo[:, (FB * e + k) % H_RING, :], start=False, stop=(k == FB - 1))
                last.then_inc(w2_mm[e // 2], 1)

            def chunk_sums(i):
                pe.wait_ge(kdw_set, i + 1)
                if i:
                    pe.wait_ge(km_set, i)
                for t in range(STAT_G):
                    for q in range(TILES):
                        tile = (i * STAT_G + t) * TILES + q
                        last = pe.matmul(kd_row_ps[q * KD_ROWS:(q + 1) * KD_ROWS, t * P:(t + 1) * P], kdw[i % 2][:, t * TILES + q, :], xtok[:, tile, :],
                                         start=True, stop=True)
                last.then_inc(kd_mm, 1)

            def turn_sums(i):
                pe.wait_ge(kd_row_set, i + 1)
                for t in range(STAT_G):
                    last = pe.transpose(kd_ps[:, t * P:(t + 1) * P], kd_row[:, t * P:(t + 1) * P], ident)
                last.then_inc(kd_turned, 1)

            def token_rates(i):
                for t in range(i * RATE_G // STAT_G, (i + 1) * RATE_G // STAT_G):
                    pe.wait_ge(xt_in[t], 16)
                pe.wait_ge(par_set, 1)
                if i:
                    pe.wait_ge(lr_tanh, i)
                for t in range(RATE_G):
                    last = pe.matmul(rate_ps[t * RATE_ROWS:(t + 1) * RATE_ROWS, :], prm[:, C_RATE_W:C_PARAMS],
                                     xt[:, i * RATE_G + t, :, 1:1 + P], start=True, stop=True)
                last.then_inc(lr_mm, 1)

            def gate_sums(i):
                pe.wait_ge(km_copy, i + 1)
                if i:
                    pe.wait_ge(gate_tanh, i)
                pe.matmul(gate_ps, gate_rep[:], km[:, kpart(i)], start=True, stop=True).then_inc(gate_mm, 1)

            def turn_k(i):
                pe.wait_ge(kb_set, i + 1)
                if i:
                    pe.wait_ge(krow_set, i)
                for t in range(STAT_G):
                    last = pe.transpose(krow_ps[:, t * P:(t + 1) * P],
                                        kb[:, i * STAT_G + t].rearrange("p j b -> p (j b)").bitcast(F32), ident)
                last.then_inc(krow_mm, 1)

            def mean_rates(i):
                pe.wait_ge(lr_masked, i + 1)
                if i:
                    pe.wait_ge(coef_in, i)
                pe.matmul(mean_ps, ones, rate_mask[:].rearrange("p r b -> p (r b)"), start=True, stop=True).then_inc(lr_mean, 1)

            router_sums()
            outputs(0)
            hidden(0)
            token_rates(0)
            chunk_sums(0)
            value(0)
            turn_sums(0)
            turn_r(0)
            chunk_sums(1)
            gate_sums(0)
            turn_sums(1)
            mean_outputs()
            gate_sums(1)
            mean_rates(0)
            chunk_sums(2)
            error(0)
            turn_k(0)
            turn_sums(2)
            token_rates(1)
            turn_error(0)
            turn_x1(0, 0)
            turn_k(1)
            chunk_sums(3)
            update(0)
            gate_sums(2)
            turn_k(2)
            turn_sums(3)
            outputs(1)
            gate_sums(3)
            norm(0)
            mean_rates(1)
            turn_k(3)
            route(0, 0)
            first(0, 0, 0)
            first(1, 0, 0)
            first(2, 0, 0)
            hidden(1)
            second_high(0, 0)
            first(3, 0, 0)
            value(1)
            first(4, 0, 0)
            turn_comb(0)
            turn_r(1)
            first(5, 0, 0)
            second_low(0, 0)
            first(6, 0, 0)
            error(1)
            first(7, 0, 0)
            second_high(1, 0)
            turn_error(1)
            first(8, 0, 0)
            second_low(1, 0)
            first(9, 0, 0)
            first(10, 0, 0)
            update(1)
            second_high(2, 0)
            second_high(3, 0)
            second_low(2, 0)
            second_low(3, 0)
            turn_x1(1, 1)
            first(11, 0, 0)
            first(12, 0, 0)
            second_high(4, 0)
            norm(1)
            second_low(4, 0)
            route(1, 1)
            first(13, 0, 0)
            outputs(2)
            first(14, 0, 0)
            first(15, 0, 0)
            second_high(5, 0)
            second_high(6, 0)
            second_low(5, 0)
            second_low(6, 0)
            pe.wait_ge(w2_lo_set, E)

            def body(p, parity):
                g = p + 1
                c, u = chained(p), chained(p) and updated(p)
                first(0, p, parity)
                second_high(7, p - 1)
                first(1, p, parity)
                first(2, p, parity)
                second_low(7, p - 1)
                first(3, p, parity)
                turn_comb(p)
                first(4, p, parity)
                if c:
                    hidden(g)
                first(5, p, parity)
                second_high(0, p)
                first(6, p, parity)
                if c:
                    value(g)
                second_low(0, p)
                first(7, p, parity)
                if c:
                    turn_r(g)
                second_high(1, p)
                first(8, p, parity)
                second_low(1, p)
                first(9, p, parity)
                finish(p - 1, 1 - parity)
                if u:
                    error(g)
                second_high(2, p)
                first(10, p, parity)
                if u:
                    turn_error(g)
                second_low(2, p)
                second_high(3, p)
                first(11, p, parity)
                if u:
                    update(g)
                first(12, p, parity)
                second_low(3, p)
                first(13, p, parity)
                if c:
                    turn_x1(g, 1 - parity)
                second_high(4, p)
                first(14, p, parity)
                second_high(5, p)
                second_low(4, p)
                if u:
                    norm(g)
                second_low(5, p)
                if c:
                    route(g, 1 - parity)
                first(15, p, parity)
                second_high(6, p)
                if u:
                    outputs(g + 1)
                second_low(6, p)

            loop_and_after(pe, body)
            second_high(7, G - 1)
            second_low(7, G - 1)
            wait_event(pe, y_added, E - 4, E - 1, G - 1)
            pe.wait_ge(x1t_lo_set, G)
            for q in range(TILES):
                last = pe.transpose(cb[:, q * P:(q + 1) * P], acc[(G - 1) % 2][:, q * P:(q + 1) * P], ident)
            last.then_inc(fin_mm, 1)
            pe.wait_ge(y_weighted[-1], 2 * G + 1)
            pe.wait_ge(x1_set, G)
            for q in range(TILES):
                last = pe.transpose(ca[:, q * P:(q + 1) * P], ym[:, (E - 2) % YM_RING, q * P:(q + 1) * P], ident)
            last.then_inc(fin_mm, 1)


def pack(x, m_init, eta_w, eta_b, alpha_w, alpha_b, gate_w, gate_b, vg_w1, vg_w2, gamma, beta, route_w, w1, w2):
    xs = x.reshape(TILES, 2, G, CHUNK, D)
    x_tok = xs.transpose(1, 3, 2, 0, 4).reshape(P, ALL_TILES, D)
    x_chan = np.zeros((P, G, TILES, PAIR), x.dtype)
    x_chan[..., 1:1 + P] = xs.transpose(4, 2, 0, 1, 3).reshape(P, G, TILES, P)
    params = np.zeros((P, C_PARAMS), x.dtype)
    for column, values in ((C_GAMMA, gamma), (C_BETA, beta), (C_GATE_W, gate_w), (C_GATE_B, gate_b),
                           (C_RATE_W, eta_w), (C_RATE_W + 1, alpha_w)):
        params[:, column] = values
    params[0::RATE_ROWS, C_RATE_B] = eta_b
    params[1::RATE_ROWS, C_RATE_B] = alpha_b
    params[:, C_ROUTE:C_ROUTE + E] = route_w.T
    consts = np.zeros((P, K_CONSTS), np.float32)
    consts[:, K_IDENT:K_IDENT + P] = np.eye(P)
    consts[:, K_ONES:K_ONES + P] = 1
    consts[:CHUNK, K_HALVES] = consts[CHUNK:, K_HALVES + 1] = 1 / CHUNK
    consts[:, K_LOWER:K_BATCH] = np.tril(np.ones((E, E)), -1).ravel()
    consts[:ROWS, K_BATCH:K_RATE] = np.tile(np.eye(B), (3, 1))
    for w in range(2):
        for t in range(RATE_G):
            consts[t * RATE_ROWS + w, K_RATE + w * RATE_G + t] = 1 / CHUNK
    return {
        "x_tok": x_tok, "x_chan": x_chan, "m_init_t": m_init.T, "vg_w1t": vg_w1.T, "vg_w2t": vg_w2.T,
        "w1t": w1.transpose(2, 0, 1), "w2t": w2.reshape(E, D, FB, P).transpose(3, 0, 2, 1),
        "params": params, "consts": consts,
    }


def kernel(L0_attn_x, L0_attn_M_init, L0_attn_eta_w, L0_attn_eta_b, L0_attn_alpha_w, L0_attn_alpha_b, L0_attn_gate_w,
           L0_attn_gate_b, L0_attn_vg_w1, L0_attn_vg_w2, L0_ffn_ln_gamma, L0_ffn_ln_beta, L0_ffn_gate_w, L0_ffn_w1, L0_ffn_w2):
    from concourse.bacc import Bacc
    from concourse.bass_utils import run_bass_kernel_spmd

    given = [L0_attn_x, L0_attn_M_init, L0_attn_eta_w, L0_attn_eta_b, L0_attn_alpha_w, L0_attn_alpha_b, L0_attn_gate_w,
             L0_attn_gate_b, L0_attn_vg_w1, L0_attn_vg_w2, L0_ffn_ln_gamma, L0_ffn_ln_beta, L0_ffn_gate_w, L0_ffn_w1, L0_ffn_w2]
    arrays = {f"in_{n}": np.ascontiguousarray(a) for n, a in pack(*(np.asarray(a) for a in given)).items()}
    nc = Bacc("TRN2", target_bir_lowering=False, num_devices=1)
    ins = [nc.dram_tensor(n, a.shape, mybir.dt.from_np(a.dtype), kind="ExternalInput").ap() for n, a in arrays.items()]
    out = nc.dram_tensor("out_dev", (G, P, TILES * D), F32, kind="ExternalOutput").ap()
    build(nc, *ins, out)
    got = run_bass_kernel_spmd(nc, [arrays], core_ids=[0]).results[0]["out_dev"]
    return got.reshape(G, 2, CHUNK, TILES, D).transpose(3, 1, 0, 2, 4).reshape(B, S, D)
```
